# Optimizing a Trainium2 kernel written in Bass

```python
import numpy as np
import jax
import jax.numpy as jnp

def _softmax(x, axis=-1):
    return jax.nn.softmax(x, axis=axis)

def _gelu(x):
    return jax.nn.gelu(x, approximate=True)

def _silu(x):
    return jax.nn.silu(x)

def _sigmoid(x):
    return jax.nn.sigmoid(x)

def _layernorm(x, axis=-1, eps=1e-05):
    m = jnp.mean(x, axis=axis, keepdims=True)
    v = jnp.var(x, axis=axis, keepdims=True)
    return (x - m) / jnp.sqrt(v + eps)

def _scatter_add(tgt, idx, src, axis=0):
    return tgt.at[idx].add(src)

def _segment_sum(src, seg, n):
    return jax.ops.segment_sum(src, seg, n)
kernel_name = 'mk_vit_tower_cls_d4_tok_img256_r4_1f2343'

def setup_inputs(seed: int=0):
    np.random.seed(seed)
    _w = jnp.asarray

    def _rec_inputs():
        import jax
        import jax.numpy as jnp
        _rk = jax.random.key(seed)
        x = -7.10856e-05 + 0.999911 * jax.random.normal(jax.random.fold_in(_rk, 1), (2, 64, 128, 64), jnp.float32)
        cls_tok = 0.02 * jax.random.normal(jax.random.fold_in(_rk, 5), (1, 1, 64), jnp.float32)
        return (x, cls_tok)
    x, cls_tok = _rec_inputs()

    def _L0_tok_setup():
        import jax, jax.numpy as jnp
        import numpy as np
        PATCH_LEN = 16
        STRIDE = 8
        PAD = 8
        key = jax.random.key(seed)
        k1, k2 = jax.random.split(key)
        x = jax.random.normal(k1, (32, 64, 128, 64), dtype=jnp.float32)
        in_feat = 64 * (PATCH_LEN // 2 + 1) * 2
        W = jax.random.normal(k2, (64, in_feat), dtype=jnp.float32) * 0.02
        return {'x': x, 'W': W}
    _L0_tok_all = _L0_tok_setup()
    _L0_tok_in = {k: v for k, v in _L0_tok_all.items() if k in ('W',)}
    del _L0_tok_all

    def _L0_attn_setup():
        import jax, jax.numpy as jnp
        import numpy as np
        B, N, C, H = (8, 4096, 64, 8)
        D = C // H
        GH = C // 4
        key = jax.random.key(seed)
        ks = jax.random.split(key, 6)
        s = 0.02
        return {'x': jax.random.normal(ks[0], (B, N, C), dtype=jnp.float32), 'Wqkv': jax.random.normal(ks[1], (C, 3 * C), dtype=jnp.float32) * s, 'Wproj': jax.random.normal(ks[2], (C, C), dtype=jnp.float32) * s, 'bproj': jnp.zeros((C,), dtype=jnp.float32), 'ln_g': jnp.ones((C,), dtype=jnp.float32), 'ln_b': jnp.zeros((C,), dtype=jnp.float32), 'Wg1': jax.random.normal(ks[3], (C, GH), dtype=jnp.float32) * s, 'bg1': jnp.zeros((GH,), dtype=jnp.float32), 'Wg2': jax.random.normal(ks[4], (GH, C), dtype=jnp.float32) * s, 'bg2': jnp.zeros((C,), dtype=jnp.float32)}
    _L0_attn_all = _L0_attn_setup()
    _L0_attn_in = {k: v for k, v in _L0_attn_all.items() if k in ('Wqkv', 'Wproj', 'bproj', 'ln_g', 'ln_b', 'Wg1', 'bg1', 'Wg2', 'bg2')}
    del _L0_attn_all

    def _L0_ffn_setup():
        import math
        import jax, jax.numpy as jnp
        import numpy as np
        CAPACITY_FACTOR = 1.25
        key = jax.random.key(seed)
        ks = jax.random.split(key, 5)
        B, L, D, F, E = (8, 2048, 64, 256, 8)
        h = jax.random.normal(ks[0], (B, L, D), dtype=jnp.float32)
        gate_w = jax.random.normal(ks[1], (D, E), dtype=jnp.float32) * 0.02
        gate_b = jnp.zeros((E,), dtype=jnp.float32)
        w1 = jax.random.normal(ks[2], (E, D, F), dtype=jnp.float32) * (1.0 / math.sqrt(D))
        b1 = jnp.zeros((E, F), dtype=jnp.float32)
        w2 = jax.random.normal(ks[3], (E, F, D), dtype=jnp.float32) * (1.0 / math.sqrt(F))
        b2 = jnp.zeros((E, D), dtype=jnp.float32)
        return {'h': h, 'gate_w': gate_w, 'gate_b': gate_b, 'w1': w1, 'b1': b1, 'w2': w2, 'b2': b2}
    _L0_ffn_all = _L0_ffn_setup()
    _L0_ffn_in = {k: v for k, v in _L0_ffn_all.items() if k in ('gate_w', 'gate_b', 'w1', 'b1', 'w2', 'b2')}
    del _L0_ffn_all

    def _L1_attn_setup():
        import jax, jax.numpy as jnp
        import numpy as np
        import math
        N_SEQ, L_RES, D_MODEL = (128, 96, 64)
        N_HEAD, C_HEAD = (8, 32)
        EPS = 1e-05
        key = jax.random.key(seed)
        ks = jax.random.split(key, 8)
        s = 1.0 / math.sqrt(D_MODEL)
        return {'m': jax.random.normal(ks[0], (N_SEQ, L_RES, D_MODEL), jnp.float32), 'gamma': jnp.ones((D_MODEL,), jnp.float32), 'beta': jnp.zeros((D_MODEL,), jnp.float32), 'Wq': jax.random.normal(ks[1], (D_MODEL, N_HEAD * C_HEAD), jnp.float32) * s, 'Wk': jax.random.normal(ks[2], (D_MODEL, N_HEAD * C_HEAD), jnp.float32) * s, 'Wv': jax.random.normal(ks[3], (D_MODEL, N_HEAD * C_HEAD), jnp.float32) * s, 'Wg': jax.random.normal(ks[4], (D_MODEL, N_HEAD * C_HEAD), jnp.float32) * s, 'bg': jnp.zeros((N_HEAD * C_HEAD,), jnp.float32), 'Wo': jax.random.normal(ks[5], (N_HEAD * C_HEAD, D_MODEL), jnp.float32) * s, 'bo': jnp.zeros((D_MODEL,), jnp.float32)}
    _L1_attn_all = _L1_attn_setup()
    _L1_attn_in = {k: v for k, v in _L1_attn_all.items() if k in ('gamma', 'beta', 'Wq', 'Wk', 'Wv', 'Wg', 'bg', 'Wo', 'bo')}
    del _L1_attn_all

    def _L1_ffn_setup():
        import jax, jax.numpy as jnp
        import numpy as np
        B, S, D, E, H, K = (4, 1024, 64, 8, 128, 2)
        key = jax.random.key(seed)
        ks = jax.random.split(key, 6)
        x = jax.random.normal(ks[0], (B, S, D), jnp.float32)
        Wg = jax.random.normal(ks[1], (D, E), jnp.float32) * 0.02
        bg = jnp.zeros((E,), jnp.float32)
        W1 = jax.random.normal(ks[2], (E, D, H), jnp.float32) * 0.02
        b1 = jnp.zeros((E, H), jnp.float32)
        W2 = jax.random.normal(ks[3], (E, H, D), jnp.float32) * 0.02
        b2 = jnp.zeros((E, D), jnp.float32)
        return {'x': x, 'Wg': Wg, 'bg': bg, 'W1': W1, 'b1': b1, 'W2': W2, 'b2': b2}
    _L1_ffn_all = _L1_ffn_setup()
    _L1_ffn_in = {k: v for k, v in _L1_ffn_all.items() if k in ('Wg', 'bg', 'W1', 'b1', 'W2', 'b2')}
    del _L1_ffn_all

    def _L2_attn_setup():
        import jax, jax.numpy as jnp
        import numpy as np
        BSZ, L, D, S, K = (8, 1024, 64, 16, 4)
        key = jax.random.key(seed)
        ks = jax.random.split(key, 8)
        sc = 0.02
        return {'x': jax.random.normal(ks[0], (BSZ, L, D), jnp.float32), 'dt': jax.random.normal(ks[1], (D, S), jnp.float32) * 0.01, 'B_w': jax.random.normal(ks[2], (S, D), jnp.float32) * sc, 'C_w': jax.random.normal(ks[3], (D, S), jnp.float32) * sc, 'conv_w': jax.random.normal(ks[4], (D, 1, K), jnp.float32) * sc, 'conv_b': jnp.zeros((D,), jnp.float32), 'in_w': jax.random.normal(ks[5], (2 * D, D), jnp.float32) * sc, 'in_b': jnp.zeros((2 * D,), jnp.float32), 'out_w': jax.random.normal(ks[6], (D, D), jnp.float32) * sc, 'out_b': jnp.zeros((D,), jnp.float32), 'gamma': jnp.ones((D,), jnp.float32), 'beta': jnp.zeros((D,), jnp.float32)}
    _L2_attn_all = _L2_attn_setup()
    _L2_attn_in = {k: v for k, v in _L2_attn_all.items() if k in ('dt', 'B_w', 'C_w', 'conv_w', 'conv_b', 'in_w', 'in_b', 'out_w', 'out_b', 'gamma', 'beta')}
    del _L2_attn_all

    def _L2_ffn_setup():
        import jax, jax.numpy as jnp
        import numpy as np
        E, D, H, TOP_K = (6, 64, 64, 2)
        ROUTER_H = D // 2
        key = jax.random.key(seed)
        ks = jax.random.split(key, 12)
        s = 1.0 / np.sqrt(D)
        sh = 1.0 / np.sqrt(H)
        sr = 1.0 / np.sqrt(ROUTER_H)
        return {'features': jax.random.normal(ks[0], (8, 1024, D), dtype=jnp.float32), 'router_w1': jax.random.uniform(ks[1], (D, ROUTER_H), jnp.float32, -s, s), 'router_b1': jnp.zeros((ROUTER_H,), jnp.float32), 'router_w2': jax.random.uniform(ks[2], (ROUTER_H, E), jnp.float32, -sr, sr), 'router_b2': jnp.zeros((E,), jnp.float32), 'expert_w1': jax.random.uniform(ks[3], (E, D, H), jnp.float32, -s, s), 'expert_b1': jnp.zeros((E, H), jnp.float32), 'expert_w2': jax.random.uniform(ks[4], (E, H, H), jnp.float32, -sh, sh), 'expert_b2': jnp.zeros((E, H), jnp.float32), 'expert_w3': jax.random.uniform(ks[5], (E, H, D), jnp.float32, -sh, sh), 'expert_b3': jnp.zeros((E, D), jnp.float32)}
    _L2_ffn_all = _L2_ffn_setup()
    _L2_ffn_in = {k: v for k, v in _L2_ffn_all.items() if k in ('router_w1', 'router_b1', 'router_w2', 'router_b2', 'expert_w1', 'expert_b1', 'expert_w2', 'expert_b2', 'expert_w3', 'expert_b3')}
    del _L2_ffn_all

    def _L3_attn_setup():
        import jax, jax.numpy as jnp
        import numpy as np
        D_MODEL = 64
        D_INNER = 128
        D_STATE = 16
        D_CONV = 4
        DT_RANK = 16
        EPS = 1e-05

        def _ln(x, g, b):
            m = x.mean(-1, keepdims=True)
            v = jnp.mean((x - m) ** 2, -1, keepdims=True)
            return (x - m) * jax.lax.rsqrt(v + EPS) * g + b

        def _mamba(x, W_in, conv_w, conv_b, W_x, W_dt, b_dt, A_log, Dp, W_out):
            B, N, _ = x.shape
            xz = x @ W_in.T
            xs, z = jnp.split(xz, 2, axis=-1)
            xp = jnp.pad(xs, ((0, 0), (D_CONV - 1, 0), (0, 0)))
            xc = sum((xp[:, k:k + N, :] * conv_w[:, k] for k in range(D_CONV))) + conv_b
            xc = jax.nn.silu(xc)
            dbl = xc @ W_x.T
            dt, Bm, Cm = jnp.split(dbl, [DT_RANK, DT_RANK + D_STATE], axis=-1)
            dt = jax.nn.softplus(dt @ W_dt.T + b_dt)
            A = -jnp.exp(A_log)
            dA = jnp.exp(dt[..., None] * A)
            dBx = dt[..., None] * Bm[:, :, None, :] * xc[..., None]

            def step(h, inp):
                dA_t, dBx_t, c_t = inp
                h = dA_t * h + dBx_t
                y = jnp.einsum('bds,bs->bd', h, c_t)
                return (h, y)
            h0 = jnp.zeros((B, D_INNER, D_STATE), xs.dtype)
            _, ys = jax.lax.scan(step, h0, (dA.swapaxes(0, 1), dBx.swapaxes(0, 1), Cm.swapaxes(0, 1)))
            y = ys.swapaxes(0, 1) + Dp * xc
            y = y * jax.nn.silu(z)
            return y @ W_out.T

        def _reference_tuple_inner(input_states, position_states, W_in, conv_w, conv_b, W_x, W_dt, b_dt, A_log, Dp, W_out, W_lin, b_lin, ln1_g, ln1_b, W_exp, b_exp, W_sq, b_sq, ln2_g, ln2_b):
            h = _mamba(input_states, W_in, conv_w, conv_b, W_x, W_dt, b_dt, A_log, Dp, W_out)
            h = h @ W_lin.T + b_lin
            h = _ln(h + input_states, ln1_g, ln1_b)
            ff = jax.nn.relu(h @ W_exp.T + b_exp) @ W_sq.T + b_sq
            out = _ln(h + ff, ln2_g, ln2_b)
            return (out, input_states)
        key = jax.random.key(seed)
        ks = jax.random.split(key, 24)
        g = lambda k, s, sc=0.02: jax.random.normal(k, s, jnp.float32) * sc
        inp = {}
        inp['input_states'] = jax.random.normal(ks[0], (1, 2048, D_MODEL), jnp.float32)
        inp['position_states'] = jax.random.normal(ks[1], (1, 2048, D_MODEL), jnp.float32)
        inp['W_in'] = g(ks[2], (2 * D_INNER, D_MODEL))
        inp['conv_w'] = g(ks[3], (D_INNER, D_CONV), 0.2)
        inp['conv_b'] = jnp.zeros((D_INNER,), jnp.float32)
        inp['W_x'] = g(ks[4], (DT_RANK + 2 * D_STATE, D_INNER))
        inp['W_dt'] = g(ks[5], (D_INNER, DT_RANK), 0.1)
        inp['b_dt'] = g(ks[6], (D_INNER,), 0.1)
        inp['A_log'] = jnp.log(jnp.broadcast_to(jnp.arange(1, D_STATE + 1, dtype=jnp.float32), (D_INNER, D_STATE)))
        inp['Dp'] = jnp.ones((D_INNER,), jnp.float32)
        inp['W_out'] = g(ks[7], (D_MODEL, D_INNER))
        inp['W_lin'] = g(ks[8], (D_MODEL, D_MODEL))
        inp['b_lin'] = jnp.zeros((D_MODEL,), jnp.float32)
        inp['ln1_g'] = jnp.ones((D_MODEL,), jnp.float32)
        inp['ln1_b'] = jnp.zeros((D_MODEL,), jnp.float32)
        inp['W_exp'] = g(ks[9], (2 * D_MODEL, D_MODEL))
        inp['b_exp'] = jnp.zeros((2 * D_MODEL,), jnp.float32)
        inp['W_sq'] = g(ks[10], (D_MODEL, 2 * D_MODEL))
        inp['b_sq'] = jnp.zeros((D_MODEL,), jnp.float32)
        inp['ln2_g'] = jnp.ones((D_MODEL,), jnp.float32)
        inp['ln2_b'] = jnp.zeros((D_MODEL,), jnp.float32)
        return inp
    _L3_attn_all = _L3_attn_setup()
    _L3_attn_in = {k: v for k, v in _L3_attn_all.items() if k in ('position_states', 'W_in', 'conv_w', 'conv_b', 'W_x', 'W_dt', 'b_dt', 'A_log', 'Dp', 'W_out', 'W_lin', 'b_lin', 'ln1_g', 'ln1_b', 'W_exp', 'b_exp', 'W_sq', 'b_sq', 'ln2_g', 'ln2_b')}
    del _L3_attn_all

    def _L3_ffn_setup():
        import jax, jax.numpy as jnp
        import numpy as np
        D_MODEL = 64
        EXPERT_DIM = 128
        NUM_EXPERTS = 8
        TOP_K = 2
        SEQ_LEN = 512
        BATCH = 2
        key = jax.random.key(seed)
        ks = jax.random.split(key, 8)
        s = 0.02
        x = jax.random.normal(ks[0], (SEQ_LEN, BATCH, D_MODEL), dtype=jnp.float32)
        Wg = jax.random.normal(ks[1], (D_MODEL, NUM_EXPERTS), dtype=jnp.float32) * s
        bg = jax.random.normal(ks[2], (NUM_EXPERTS,), dtype=jnp.float32) * s
        bias = jnp.zeros((NUM_EXPERTS,), dtype=jnp.float32)
        W1 = jax.random.normal(ks[3], (NUM_EXPERTS, D_MODEL, EXPERT_DIM), dtype=jnp.float32) * s
        b1 = jax.random.normal(ks[4], (NUM_EXPERTS, EXPERT_DIM), dtype=jnp.float32) * s
        W2 = jax.random.normal(ks[5], (NUM_EXPERTS, EXPERT_DIM, D_MODEL), dtype=jnp.float32) * s
        b2 = jax.random.normal(ks[6], (NUM_EXPERTS, D_MODEL), dtype=jnp.float32) * s
        return {'x': x, 'Wg': Wg, 'bg': bg, 'bias': bias, 'W1': W1, 'b1': b1, 'W2': W2, 'b2': b2}
    _L3_ffn_all = _L3_ffn_setup()
    _L3_ffn_in = {k: v for k, v in _L3_ffn_all.items() if k in ('Wg', 'bg', 'bias', 'W1', 'b1', 'W2', 'b2')}
    del _L3_ffn_all
    return {'x': x, 'cls_tok': cls_tok, 'L0_tok_W': _L0_tok_in['W'], 'L0_attn_Wqkv': _L0_attn_in['Wqkv'], 'L0_attn_Wproj': _L0_attn_in['Wproj'], 'L0_attn_bproj': _L0_attn_in['bproj'], 'L0_attn_ln_g': _L0_attn_in['ln_g'], 'L0_attn_ln_b': _L0_attn_in['ln_b'], 'L0_attn_Wg1': _L0_attn_in['Wg1'], 'L0_attn_bg1': _L0_attn_in['bg1'], 'L0_attn_Wg2': _L0_attn_in['Wg2'], 'L0_attn_bg2': _L0_attn_in['bg2'], 'L0_ffn_gate_w': _L0_ffn_in['gate_w'], 'L0_ffn_gate_b': _L0_ffn_in['gate_b'], 'L0_ffn_w1': _L0_ffn_in['w1'], 'L0_ffn_b1': _L0_ffn_in['b1'], 'L0_ffn_w2': _L0_ffn_in['w2'], 'L0_ffn_b2': _L0_ffn_in['b2'], 'L1_attn_gamma': _L1_attn_in['gamma'], 'L1_attn_beta': _L1_attn_in['beta'], 'L1_attn_Wq': _L1_attn_in['Wq'], 'L1_attn_Wk': _L1_attn_in['Wk'], 'L1_attn_Wv': _L1_attn_in['Wv'], 'L1_attn_Wg': _L1_attn_in['Wg'], 'L1_attn_bg': _L1_attn_in['bg'], 'L1_attn_Wo': _L1_attn_in['Wo'], 'L1_attn_bo': _L1_attn_in['bo'], 'L1_ffn_Wg': _L1_ffn_in['Wg'], 'L1_ffn_bg': _L1_ffn_in['bg'], 'L1_ffn_W1': _L1_ffn_in['W1'], 'L1_ffn_b1': _L1_ffn_in['b1'], 'L1_ffn_W2': _L1_ffn_in['W2'], 'L1_ffn_b2': _L1_ffn_in['b2'], 'L2_attn_dt': _L2_attn_in['dt'], 'L2_attn_B_w': _L2_attn_in['B_w'], 'L2_attn_C_w': _L2_attn_in['C_w'], 'L2_attn_conv_w': _L2_attn_in['conv_w'], 'L2_attn_conv_b': _L2_attn_in['conv_b'], 'L2_attn_in_w': _L2_attn_in['in_w'], 'L2_attn_in_b': _L2_attn_in['in_b'], 'L2_attn_out_w': _L2_attn_in['out_w'], 'L2_attn_out_b': _L2_attn_in['out_b'], 'L2_attn_gamma': _L2_attn_in['gamma'], 'L2_attn_beta': _L2_attn_in['beta'], 'L2_ffn_router_w1': _L2_ffn_in['router_w1'], 'L2_ffn_router_b1': _L2_ffn_in['router_b1'], 'L2_ffn_router_w2': _L2_ffn_in['router_w2'], 'L2_ffn_router_b2': _L2_ffn_in['router_b2'], 'L2_ffn_expert_w1': _L2_ffn_in['expert_w1'], 'L2_ffn_expert_b1': _L2_ffn_in['expert_b1'], 'L2_ffn_expert_w2': _L2_ffn_in['expert_w2'], 'L2_ffn_expert_b2': _L2_ffn_in['expert_b2'], 'L2_ffn_expert_w3': _L2_ffn_in['expert_w3'], 'L2_ffn_expert_b3': _L2_ffn_in['expert_b3'], 'L3_attn_position_states': _L3_attn_in['position_states'], 'L3_attn_W_in': _L3_attn_in['W_in'], 'L3_attn_conv_w': _L3_attn_in['conv_w'], 'L3_attn_conv_b': _L3_attn_in['conv_b'], 'L3_attn_W_x': _L3_attn_in['W_x'], 'L3_attn_W_dt': _L3_attn_in['W_dt'], 'L3_attn_b_dt': _L3_attn_in['b_dt'], 'L3_attn_A_log': _L3_attn_in['A_log'], 'L3_attn_Dp': _L3_attn_in['Dp'], 'L3_attn_W_out': _L3_attn_in['W_out'], 'L3_attn_W_lin': _L3_attn_in['W_lin'], 'L3_attn_b_lin': _L3_attn_in['b_lin'], 'L3_attn_ln1_g': _L3_attn_in['ln1_g'], 'L3_attn_ln1_b': _L3_attn_in['ln1_b'], 'L3_attn_W_exp': _L3_attn_in['W_exp'], 'L3_attn_b_exp': _L3_attn_in['b_exp'], 'L3_attn_W_sq': _L3_attn_in['W_sq'], 'L3_attn_b_sq': _L3_attn_in['b_sq'], 'L3_attn_ln2_g': _L3_attn_in['ln2_g'], 'L3_attn_ln2_b': _L3_attn_in['ln2_b'], 'L3_ffn_Wg': _L3_ffn_in['Wg'], 'L3_ffn_bg': _L3_ffn_in['bg'], 'L3_ffn_bias': _L3_ffn_in['bias'], 'L3_ffn_W1': _L3_ffn_in['W1'], 'L3_ffn_b1': _L3_ffn_in['b1'], 'L3_ffn_W2': _L3_ffn_in['W2'], 'L3_ffn_b2': _L3_ffn_in['b2']}

def reference(x, cls_tok, L0_tok_W, L0_attn_Wqkv, L0_attn_Wproj, L0_attn_bproj, L0_attn_ln_g, L0_attn_ln_b, L0_attn_Wg1, L0_attn_bg1, L0_attn_Wg2, L0_attn_bg2, L0_ffn_gate_w, L0_ffn_gate_b, L0_ffn_w1, L0_ffn_b1, L0_ffn_w2, L0_ffn_b2, L1_attn_gamma, L1_attn_beta, L1_attn_Wq, L1_attn_Wk, L1_attn_Wv, L1_attn_Wg, L1_attn_bg, L1_attn_Wo, L1_attn_bo, L1_ffn_Wg, L1_ffn_bg, L1_ffn_W1, L1_ffn_b1, L1_ffn_W2, L1_ffn_b2, L2_attn_dt, L2_attn_B_w, L2_attn_C_w, L2_attn_conv_w, L2_attn_conv_b, L2_attn_in_w, L2_attn_in_b, L2_attn_out_w, L2_attn_out_b, L2_attn_gamma, L2_attn_beta, L2_ffn_router_w1, L2_ffn_router_b1, L2_ffn_router_w2, L2_ffn_router_b2, L2_ffn_expert_w1, L2_ffn_expert_b1, L2_ffn_expert_w2, L2_ffn_expert_b2, L2_ffn_expert_w3, L2_ffn_expert_b3, L3_attn_position_states, L3_attn_W_in, L3_attn_conv_w, L3_attn_conv_b, L3_attn_W_x, L3_attn_W_dt, L3_attn_b_dt, L3_attn_A_log, L3_attn_Dp, L3_attn_W_out, L3_attn_W_lin, L3_attn_b_lin, L3_attn_ln1_g, L3_attn_ln1_b, L3_attn_W_exp, L3_attn_b_exp, L3_attn_W_sq, L3_attn_b_sq, L3_attn_ln2_g, L3_attn_ln2_b, L3_ffn_Wg, L3_ffn_bg, L3_ffn_bias, L3_ffn_W1, L3_ffn_b1, L3_ffn_W2, L3_ffn_b2):
    import jax
    import jax.numpy as jnp

    def _L0_tok_ref(x, W):
        import jax, jax.numpy as jnp
        import numpy as np
        PATCH_LEN = 16
        STRIDE = 8
        PAD = 8
        B, C, T, V = x.shape
        xp = jnp.pad(x, ((0, 0), (0, 0), (0, PAD), (0, 0)), mode='edge')
        Tp = T + PAD
        N = (Tp - PATCH_LEN) // STRIDE + 1
        idx = jnp.arange(N)[:, None] * STRIDE + jnp.arange(PATCH_LEN)[None, :]
        patches = xp[:, :, idx, :]
        patches = jnp.transpose(patches, (0, 4, 2, 3, 1))
        xf = jnp.fft.rfft(patches, axis=-2, norm='ortho')
        F = xf.shape[-2]
        x_real = xf.real.reshape(B, V, N, F * C)
        x_imag = xf.imag.reshape(B, V, N, F * C)
        x_emb = jnp.concatenate([x_real, x_imag], axis=-1)
        x_emb = x_emb @ W.T
        return x_emb.reshape(B, V * N, -1)

    def _L0_attn_ref(x, Wqkv, Wproj, bproj, ln_g, ln_b, Wg1, bg1, Wg2, bg2):
        import jax, jax.numpy as jnp
        import numpy as np
        B, N, C, H = (8, 4096, 64, 8)
        D = C // H
        GH = C // 4
        b, n, c = x.shape
        h, d = (H, D)
        qkv = (x @ Wqkv).reshape(b, n, 3, h, d)
        q, k, v = (qkv[:, :, 0], qkv[:, :, 1], qkv[:, :, 2])
        k = jax.nn.softmax(k, axis=1)
        context = jnp.einsum('bnhd,bnhv->bhdv', k, v)
        out = jnp.einsum('bnhd,bhdv->bnhv', q, context).reshape(b, n, c)
        mu = jnp.mean(x, axis=-1, keepdims=True)
        var = jnp.var(x, axis=-1, keepdims=True)
        xn = (x - mu) * jax.lax.rsqrt(var + 1e-05) * ln_g + ln_b
        hgate = jax.nn.gelu(xn @ Wg1 + bg1, approximate=False)
        gate = jax.nn.sigmoid(hgate @ Wg2 + bg2)
        return out * gate @ Wproj + bproj

    def _L0_ffn_ref(h, gate_w, gate_b, w1, b1, w2, b2):
        import math
        import jax, jax.numpy as jnp
        import numpy as np
        CAPACITY_FACTOR = 1.25
        B, L, D = h.shape
        E = gate_w.shape[1]
        T = B * L
        C = max(1, math.ceil(CAPACITY_FACTOR * T / E))
        x = h.reshape(T, D)
        logits = x @ gate_w + gate_b
        probs = jax.nn.softmax(logits, axis=-1)
        idx = jnp.argmax(probs, axis=-1)
        prb = jnp.take_along_axis(probs, idx[:, None], axis=1)[:, 0]
        one_hot = jax.nn.one_hot(idx, E, dtype=jnp.float32)
        pos = (jnp.cumsum(one_hot, axis=0) * one_hot).sum(-1).astype(jnp.int32) - 1
        kept = pos < C
        pos_safe = jnp.where(kept, pos, C)
        buf = jnp.zeros((E, C, D), dtype=h.dtype).at[idx, pos_safe].set(x, mode='drop')
        hmid = jax.nn.relu(jnp.einsum('ecd,edf->ecf', buf, w1) + b1[:, None, :])
        ybuf = jnp.einsum('ecf,efd->ecd', hmid, w2) + b2[:, None, :]
        pos_g = jnp.minimum(pos, C - 1)
        y_tok = ybuf[idx, pos_g] * (prb * kept)[:, None]
        y = y_tok.reshape(B, L, D)
        y = jnp.nan_to_num(y, nan=0.0, posinf=10000.0, neginf=-10000.0)
        return y

    def _L1_attn_ref(m, gamma, beta, Wq, Wk, Wv, Wg, bg, Wo, bo):
        import jax, jax.numpy as jnp
        import numpy as np
        import math
        N_SEQ, L_RES, D_MODEL = (128, 96, 64)
        N_HEAD, C_HEAD = (8, 32)
        EPS = 1e-05
        N, L, D = m.shape
        H, C = (N_HEAD, C_HEAD)
        mu = jnp.mean(m, axis=-1, keepdims=True)
        var = jnp.mean(jnp.square(m - mu), axis=-1, keepdims=True)
        mn = (m - mu) * jax.lax.rsqrt(var + EPS) * gamma + beta
        q = (mn @ Wq).reshape(N, L, H, C)
        k = (mn @ Wk).reshape(N, L, H, C)
        v = (mn @ Wv).reshape(N, L, H, C)
        g = jax.nn.sigmoid(mn @ Wg + bg).reshape(N, L, H, C)
        scale = 1.0 / math.sqrt(C) / math.sqrt(L)
        att = jnp.einsum('slhc,tlhc->sth', q, k) * scale
        att = jax.nn.softmax(att, axis=1)
        o = jnp.einsum('sth,tlhc->slhc', att, v) * g
        return o.reshape(N, L, H * C) @ Wo + bo

    def _L1_ffn_ref(x, Wg, bg, W1, b1, W2, b2):
        import jax, jax.numpy as jnp
        import numpy as np
        B, S, D, E, H, K = (4, 1024, 64, 8, 128, 2)
        Bv, Sv, Dv = x.shape
        gate_scores = x @ Wg + bg
        _, idx = jax.lax.top_k(gate_scores, K)
        mask = jax.nn.one_hot(idx, E, dtype=x.dtype).sum(axis=-2)
        xf = x.reshape(-1, Dv)
        mf = mask.reshape(-1, E)
        h = jax.nn.gelu(jnp.einsum('td,edh->teh', xf, W1) + b1[None], approximate=False)
        y = jnp.einsum('teh,ehd->ted', h, W2) + b2[None]
        out = jnp.einsum('ted,te->td', y, mf)
        return out.reshape(Bv, Sv, Dv)

    def _L2_attn_ref(x, dt, B_w, C_w, conv_w, conv_b, in_w, in_b, out_w, out_b, gamma, beta):
        import jax, jax.numpy as jnp
        import numpy as np
        BSZ, L, D, S, K = (8, 1024, 64, 16, 4)
        d_model = x.shape[-1]
        k = conv_w.shape[-1]
        xr = x @ in_w.T + in_b
        xp, res = jnp.split(xr, 2, axis=-1)
        xc = jnp.transpose(xp, (0, 2, 1))
        xc = jax.lax.conv_general_dilated(xc, conv_w, window_strides=(1,), padding=[(k - 1, 0)], feature_group_count=d_model, dimension_numbers=('NCH', 'OIH', 'NCH'))
        xc = xc + conv_b[None, :, None]
        xconv = jnp.transpose(xc, (0, 2, 1))
        dA = jnp.exp(jnp.einsum('bld,ds->bls', xconv, dt))
        dB = xconv @ B_w.T
        dA_cp = jnp.cumprod(dA, axis=1)
        yc = jnp.cumsum(dA_cp * dB, axis=1)
        y = jnp.concatenate([dB[:, :1], yc[:, 1:] - yc[:, :-1] * dA[:, 1:]], axis=1)
        y = y @ C_w.T
        out = y * jax.nn.silu(res) @ out_w.T + out_b
        out = out + xconv
        mean = out.mean(axis=(0, 1))
        var = jnp.mean((out - mean) ** 2, axis=(0, 1))
        out = (out - mean) * jax.lax.rsqrt(var + 1e-05) * gamma + beta
        return out

    def _L2_ffn_ref(features, router_w1, router_b1, router_w2, router_b2, expert_w1, expert_b1, expert_w2, expert_b2, expert_w3, expert_b3):
        import jax, jax.numpy as jnp
        import numpy as np
        E, D, H, TOP_K = (6, 64, 64, 2)
        ROUTER_H = D // 2
        rh = jax.nn.relu(features @ router_w1 + router_b1)
        expert_logits = jax.nn.softmax(rh @ router_w2 + router_b2, axis=-1)
        top_w, top_i = jax.lax.top_k(expert_logits, TOP_K)
        routing_weights = jax.nn.softmax(top_w, axis=-1)
        h1 = jax.nn.relu(jnp.einsum('bsd,edh->bseh', features, expert_w1) + expert_b1)
        h2 = jax.nn.relu(jnp.einsum('bseh,ehf->bsef', h1, expert_w2) + expert_b2)
        expert_out = jnp.einsum('bsef,efo->bseo', h2, expert_w3) + expert_b3
        sel = jnp.take_along_axis(expert_out, top_i[:, :, :, None], axis=2)
        combined = jnp.sum(sel * routing_weights[..., None], axis=2)
        return combined

    def _L3_attn_ref(input_states, position_states, W_in, conv_w, conv_b, W_x, W_dt, b_dt, A_log, Dp, W_out, W_lin, b_lin, ln1_g, ln1_b, W_exp, b_exp, W_sq, b_sq, ln2_g, ln2_b):
        import jax, jax.numpy as jnp
        import numpy as np
        D_MODEL = 64
        D_INNER = 128
        D_STATE = 16
        D_CONV = 4
        DT_RANK = 16
        EPS = 1e-05

        def _ln(x, g, b):
            m = x.mean(-1, keepdims=True)
            v = jnp.mean((x - m) ** 2, -1, keepdims=True)
            return (x - m) * jax.lax.rsqrt(v + EPS) * g + b

        def _mamba(x, W_in, conv_w, conv_b, W_x, W_dt, b_dt, A_log, Dp, W_out):
            B, N, _ = x.shape
            xz = x @ W_in.T
            xs, z = jnp.split(xz, 2, axis=-1)
            xp = jnp.pad(xs, ((0, 0), (D_CONV - 1, 0), (0, 0)))
            xc = sum((xp[:, k:k + N, :] * conv_w[:, k] for k in range(D_CONV))) + conv_b
            xc = jax.nn.silu(xc)
            dbl = xc @ W_x.T
            dt, Bm, Cm = jnp.split(dbl, [DT_RANK, DT_RANK + D_STATE], axis=-1)
            dt = jax.nn.softplus(dt @ W_dt.T + b_dt)
            A = -jnp.exp(A_log)
            dA = jnp.exp(dt[..., None] * A)
            dBx = dt[..., None] * Bm[:, :, None, :] * xc[..., None]

            def step(h, inp):
                dA_t, dBx_t, c_t = inp
                h = dA_t * h + dBx_t
                y = jnp.einsum('bds,bs->bd', h, c_t)
                return (h, y)
            h0 = jnp.zeros((B, D_INNER, D_STATE), xs.dtype)
            _, ys = jax.lax.scan(step, h0, (dA.swapaxes(0, 1), dBx.swapaxes(0, 1), Cm.swapaxes(0, 1)))
            y = ys.swapaxes(0, 1) + Dp * xc
            y = y * jax.nn.silu(z)
            return y @ W_out.T

        def _reference_tuple_inner(input_states, position_states, W_in, conv_w, conv_b, W_x, W_dt, b_dt, A_log, Dp, W_out, W_lin, b_lin, ln1_g, ln1_b, W_exp, b_exp, W_sq, b_sq, ln2_g, ln2_b):
            h = _mamba(input_states, W_in, conv_w, conv_b, W_x, W_dt, b_dt, A_log, Dp, W_out)
            h = h @ W_lin.T + b_lin
            h = _ln(h + input_states, ln1_g, ln1_b)
            ff = jax.nn.relu(h @ W_exp.T + b_exp) @ W_sq.T + b_sq
            out = _ln(h + ff, ln2_g, ln2_b)
            return (out, input_states)
        return _reference_tuple_inner(input_states, position_states, W_in, conv_w, conv_b, W_x, W_dt, b_dt, A_log, Dp, W_out, W_lin, b_lin, ln1_g, ln1_b, W_exp, b_exp, W_sq, b_sq, ln2_g, ln2_b)[0]

    def _L3_ffn_ref(x, Wg, bg, bias, W1, b1, W2, b2):
        import jax, jax.numpy as jnp
        import numpy as np
        D_MODEL = 64
        EXPERT_DIM = 128
        NUM_EXPERTS = 8
        TOP_K = 2
        SEQ_LEN = 512
        BATCH = 2
        x_flat = x.reshape(-1, D_MODEL)
        gate_logits = x_flat @ Wg + bg + bias
        topk_vals, topk_idx = jax.lax.top_k(gate_logits, TOP_K)
        topk_w = jax.nn.softmax(topk_vals, axis=-1)
        combine = (jax.nn.one_hot(topk_idx, NUM_EXPERTS, dtype=x.dtype) * topk_w[..., None]).sum(axis=1)
        h = jax.nn.relu(jnp.einsum('td,edh->teh', x_flat, W1) + b1)
        y = jnp.einsum('teh,ehd->ted', h, W2) + b2
        out = jnp.einsum('ted,te->td', y, combine)
        return out.reshape(x.shape)
    h = _L0_tok_ref(x, L0_tok_W)
    h = jnp.concatenate([jnp.broadcast_to(cls_tok, (h.shape[0], 1, h.shape[2])), h], axis=1)
    h = h + _L0_attn_ref(_layernorm(h, axis=-1), L0_attn_Wqkv, L0_attn_Wproj, L0_attn_bproj, L0_attn_ln_g, L0_attn_ln_b, L0_attn_Wg1, L0_attn_bg1, L0_attn_Wg2, L0_attn_bg2)
    h = h + _L0_ffn_ref(_layernorm(h, axis=-1), L0_ffn_gate_w, L0_ffn_gate_b, L0_ffn_w1, L0_ffn_b1, L0_ffn_w2, L0_ffn_b2)
    h = h + _L1_attn_ref(_layernorm(h, axis=-1), L1_attn_gamma, L1_attn_beta, L1_attn_Wq, L1_attn_Wk, L1_attn_Wv, L1_attn_Wg, L1_attn_bg, L1_attn_Wo, L1_attn_bo)
    h = h + _L1_ffn_ref(_layernorm(h, axis=-1), L1_ffn_Wg, L1_ffn_bg, L1_ffn_W1, L1_ffn_b1, L1_ffn_W2, L1_ffn_b2)
    h = h + _L2_attn_ref(_layernorm(h, axis=-1), L2_attn_dt, L2_attn_B_w, L2_attn_C_w, L2_attn_conv_w, L2_attn_conv_b, L2_attn_in_w, L2_attn_in_b, L2_attn_out_w, L2_attn_out_b, L2_attn_gamma, L2_attn_beta)
    h = h + _L2_ffn_ref(_layernorm(h, axis=-1), L2_ffn_router_w1, L2_ffn_router_b1, L2_ffn_router_w2, L2_ffn_router_b2, L2_ffn_expert_w1, L2_ffn_expert_b1, L2_ffn_expert_w2, L2_ffn_expert_b2, L2_ffn_expert_w3, L2_ffn_expert_b3)
    h = h + _L3_attn_ref(_layernorm(h, axis=-1), L3_attn_position_states, L3_attn_W_in, L3_attn_conv_w, L3_attn_conv_b, L3_attn_W_x, L3_attn_W_dt, L3_attn_b_dt, L3_attn_A_log, L3_attn_Dp, L3_attn_W_out, L3_attn_W_lin, L3_attn_b_lin, L3_attn_ln1_g, L3_attn_ln1_b, L3_attn_W_exp, L3_attn_b_exp, L3_attn_W_sq, L3_attn_b_sq, L3_attn_ln2_g, L3_attn_ln2_b)
    h = h + _L3_ffn_ref(_layernorm(h, axis=-1), L3_ffn_Wg, L3_ffn_bg, L3_ffn_bias, L3_ffn_W1, L3_ffn_b1, L3_ffn_W2, L3_ffn_b2)
    return h

_drawn_inputs = setup_inputs


def setup_inputs(seed=0):
    import zlib

    import numpy as np

    out = dict(_drawn_inputs(seed))
    spreads = {'L0_attn_bproj': (0.0, 0.1),
     'L0_attn_ln_g': (1.0, 0.6),
     'L0_attn_ln_b': (0.0, 0.8),
     'L0_attn_bg1': (0.0, 0.8),
     'L0_attn_bg2': (0.0, 0.8),
     'L0_ffn_gate_b': (0.0, 0.1),
     'L0_ffn_b1': (0.0, 0.1),
     'L0_ffn_b2': (0.0, 0.1),
     'L1_attn_gamma': (1.0, 0.2),
     'L1_attn_beta': (0.0, 0.1),
     'L1_attn_bg': (0.0, 0.1),
     'L1_attn_bo': (0.0, 0.1),
     'L1_ffn_bg': (0.0, 0.1),
     'L1_ffn_b1': (0.0, 0.545),
     'L1_ffn_b2': (0.0, 0.1),
     'L2_attn_conv_b': (0.0, 0.1),
     'L2_attn_in_b': (0.0, 0.404),
     'L2_attn_out_b': (0.0, 0.8),
     'L2_attn_gamma': (1.0, 0.2),
     'L2_attn_beta': (0.0, 0.1),
     'L2_ffn_router_b1': (0.0, 0.273),
     'L2_ffn_router_b2': (0.0, 0.1),
     'L2_ffn_expert_b1': (0.0, 0.8),
     'L2_ffn_expert_b2': (0.0, 0.436),
     'L2_ffn_expert_b3': (0.0, 0.1),
     'L3_attn_conv_b': (0.0, 0.8),
     'L3_attn_Dp': (1.0, 0.6),
     'L3_attn_b_lin': (0.0, 0.1),
     'L3_attn_ln1_g': (1.0, 0.2),
     'L3_attn_ln1_b': (0.0, 0.1),
     'L3_attn_b_exp': (0.0, 0.8),
     'L3_attn_b_sq': (0.0, 0.1),
     'L3_attn_ln2_g': (1.0, 0.2),
     'L3_attn_ln2_b': (0.0, 0.1),
     'L3_ffn_bias': (0.0, 0.8)}
    factors = {'cls_tok': 8.0,
     'L0_attn_Wqkv': 8.0,
     'L0_attn_Wproj': 4.585,
     'L0_attn_Wg1': 8.0,
     'L0_attn_Wg2': 8.0,
     'L3_attn_W_in': 8.0,
     'L3_attn_conv_w': 8.0,
     'L3_attn_W_x': 8.0,
     'L3_attn_W_dt': 8.0,
     'L3_attn_b_dt': 8.0,
     'L3_attn_A_log': 8.0,
     'L3_attn_W_out': 8.0,
     'L3_attn_W_lin': 8.0,
     'L3_attn_W_exp': 5.805,
     'L3_attn_W_sq': 4.406,
     'L3_ffn_Wg': 7.512,
     'L3_ffn_bg': 8.0,
     'L3_ffn_W1': 8.0,
     'L3_ffn_b1': 8.0,
     'L3_ffn_W2': 7.738,
     'L3_ffn_b2': 8.0}
    for name, (base, spread) in spreads.items():
        noise = np.random.default_rng([zlib.crc32(name.encode()), seed]).standard_normal(out[name].shape)
        drawn = base * np.exp(spread * noise) if base else spread * noise
        out[name] = jnp.asarray(drawn.astype(out[name].dtype))
    for name, factor in factors.items():
        out[name] = (out[name] * factor).astype(out[name].dtype)
    return out
```

```python
import concourse.bass as bass
from concourse import mybir
from contextlib import ExitStack

F32 = mybir.dt.float32
BF16 = mybir.dt.bfloat16
ALU = mybir.AluOpType
ACT = mybir.ActivationFunctionType
AX = mybir.AxisListType

NB = 2
D = 64
P = NB * D
NTOK = 1025
NCH, CH = 3, 342
TP = NCH * CH
NT, TT = 9, 114
NV, NN = 64, 16
CAPACITY = 321
EPS = 1e-5
LAST = NTOK - (NCH - 1) * CH
SERIES_BELOW = 2.0 ** -6
FLT_MAX = 3.4028234663852886e38

GROUPS = [
    [("dft", 16), ("mean", 128), ("eps", 3), ("ident", 128)],
    [("a0_wk", 128), ("a0_wq", 128), ("a0_wv", 128), ("a0_wproj", 128), ("a0_wg1", 32), ("a0_wg2", 128),
     ("a0_mask", 128), ("a0_g", 1), ("a0_b", 1), ("a0_bproj", 1), ("a0_bg1", 1), ("a0_bg2", 1),
     ("f0_gate", 16), ("f0_gbias", 16), ("f0_b2", 128), ("seqsel", 128), ("rev8", 16), ("rev6", 12), ("shift", 16)],
    [("a1_g", 1), ("a1_b", 1), ("a1_wq", 256), ("a1_wk", 256), ("a1_wv", 256), ("a1_wg", 512), ("a1_bg", 2),
     ("a1_wo", 128), ("a1_bo", 1), ("tdiff", 128), ("f1_gate", 16), ("f1_gbias", 16), ("f1_b2", 128)],
    [("a2_wxp", 128), ("a2_wres", 128), ("a2_bxp", 1), ("a2_bres", 1), ("a2_convw", 4), ("a2_convb", 1),
     ("a2_dt", 32), ("a2_bw", 32), ("a2_cw", 128), ("a2_ow", 128), ("a2_ob", 1), ("a2_g", 1), ("a2_b", 1),
     ("chmean", 128), ("f2_rw1", 64), ("f2_rb1", 1), ("f2_gate", 12), ("f2_gbias", 12), ("f2_b2", 128)],
    [("a3_win", 512), ("a3_convw", 4), ("a3_convb", 1), ("a3_wx", 48), ("a3_wdt", 128), ("a3_bdt", 1),
     ("a3_alog", 16), ("a3_dp", 1), ("a3_wout", 64), ("a3_wlin", 128), ("a3_blin", 1), ("a3_g1", 1),
     ("a3_b1", 1), ("a3_wexp", 256), ("a3_bexp", 1), ("a3_wsq", 64), ("a3_bsq", 1), ("a3_g2", 1),
     ("a3_b2", 1), ("f3_gate", 16), ("f3_gbias", 16), ("f3_gbias2", 16), ("f3_b2", 128)],
]
COL, GROUP_SPAN = {}, []
_at = 0
for _g in GROUPS:
    _from = _at
    for _name, _n in _g:
        COL[_name] = (_at, _n)
        _at += _n
    GROUP_SPAN.append((_from, _at))
NSMALL = _at

SLAB2 = {1: 2 * 128 + 64 + 1 + 128, 2: 2 * 256 + 2 * 64 + 2 + 128}
SLAB3 = 3 * 128 + 2 + 64


class Steps:

    def __init__(self, sem):
        self.sem = sem
        self.n = 0

    def mark(self, instruction):
        self.n += 1
        instruction.then_inc(self.sem, 1)
        return self.n

    def settle(self, engine, instruction):
        engine.wait_ge(self.sem, self.mark(instruction))


class Chip:

    def __init__(self, nc, ctx):
        self.nc, self.ctx = nc, ctx

        def sb(name, shape, dt=F32):
            return ctx.enter_context(nc.sbuf_tensor(name, shape, dt))

        self.small = sb("small", [128, NSMALL])
        self.h = sb("h", [P, TP])
        self.xl = sb("xl", [P, TP])
        self.xc = sb("xc", [P, TP])
        self.sq = sb("sq", [P, TP])
        self.rs = sb("rs", [P, TP])
        self.psum = ctx.enter_context(nc.psum_tensor("psum", [128, 8, 512], F32))
        self.pa, self.pb, self.pc = self.psum[:, 0:3], self.psum[:, 3:6], self.psum[:, 6:8]
        self.small_loaded = [self.sem(f"small_loaded{g}") for g in range(len(GROUPS))]
        self.ln_mean, self.ln_centred = self.sem("ln_mean"), self.sem("ln_centred")
        self.ln_square, self.ln_var = self.sem("ln_square"), self.sem("ln_var")
        self.ln_log, self.ln_rstd, self.ln_out = self.sem("ln_log"), self.sem("ln_rstd"), self.sem("ln_out")
        self.norms = 0
        self.stage_sems, self.cleared = [], []

    def sem(self, name):
        return self.nc.alloc_semaphore(name)

    def stage_sem(self, name):
        s = self.nc.alloc_semaphore(name)
        self.stage_sems.append(s)
        return s

    def end_stage(self):
        for s in self.cleared:
            self.nc.release_semaphore(s)
        for s in self.stage_sems:
            self.nc.gpsimd.sem_clear(s)
        self.cleared, self.stage_sems = self.stage_sems, []

    def next_norm(self):
        self.norms += 1
        return self.norms - 1

    def w(self, name, rows=128, first=0, cols=None, row0=0):
        at, n = COL[name]
        return self.small[row0:row0 + rows, at + first:at + first + (n - first if cols is None else cols)]

    def need(self, engine, group):
        engine.wait_ge(self.small_loaded[group], 16)


def chunk(t, c):
    return t[:, c * CH:(c + 1) * CH]


def chunks(t):
    return t.rearrange("p (c n) -> p c n", n=CH)



def norm_tensor(chip, k, src, ready=None):
    nc, pe = chip.nc, chip.nc.tensor
    for c in range(NCH):
        if ready is not None:
            pe.wait_ge(ready, c + 1)
        nc.tensor.matmul(chip.pa[:, c, 0:CH], chip.w("mean"), chunk(src, c),
                         start=True, stop=True).then_inc(chip.ln_mean, 1)
    for c in range(NCH):
        pe.wait_ge(chip.ln_square, NCH * k + c + 1)
        nc.tensor.matmul(chip.pb[:, c, 0:CH], chip.w("mean"), chunk(chip.sq, c),
                         start=True, stop=True).then_inc(chip.ln_var, 1)


def norm_vector(chip, k, src, out):
    nc, v = chip.nc, chip.nc.vector
    for c in range(NCH):
        v.wait_ge(chip.ln_mean, NCH * k + c + 1)
        nc.vector.tensor_tensor(chunk(chip.xc, c), chunk(src, c), chip.pa[:, c, 0:CH],
                                ALU.subtract).then_inc(chip.ln_centred, 1)
    for c in range(NCH):
        v.wait_ge(chip.ln_rstd, NCH * k + c + 1)
        nc.vector.tensor_tensor(chunk(out, c), chunk(chip.xc, c), chunk(chip.rs, c),
                                ALU.mult).then_inc(chip.ln_out, 1)


def norm_scalar(chip, k, twice=False):
    nc, a = chip.nc, chip.nc.scalar
    eps = chip.w("eps", first=1 if twice else 0, cols=1)
    for c in range(NCH):
        a.wait_ge(chip.ln_centred, NCH * k + c + 1)
        nc.scalar.activation(chunk(chip.sq, c), chunk(chip.xc, c), ACT.Square).then_inc(chip.ln_square, 1)
    for c in range(NCH):
        a.wait_ge(chip.ln_var, NCH * k + c + 1)
        nc.scalar.activation(chunk(chip.sq, c), chip.pb[:, c, 0:CH], ACT.Ln, bias=eps,
                             scale=1.0 + EPS if twice else 1.0).then_inc(chip.ln_log, 1)
        a.wait_ge(chip.ln_log, NCH * k + c + 1)
        nc.scalar.activation(chunk(chip.rs, c), chunk(chip.sq, c), ACT.Exp,
                             scale=-0.5).then_inc(chip.ln_rstd, 1)



def tokenise(chip, x, xedge, tokw, cls2, small):
    nc = chip.nc
    with ExitStack() as ctx:
        def sb(name, shape):
            return ctx.enter_context(nc.sbuf_tensor(name, shape, F32))
        xt = sb("xt", [128, NB, NN, 4, NV])
        xe = sb("xe", [128, NB, NV])
        tw = sb("tw", [18, D, 64])
        wl = sb("wl", [128, 4, 2, D])
        s_x = [[chip.stage_sem(f"x_loaded{b}{j}") for j in range(2)] for b in range(NB)]
        s_e, s_w, s_cls = chip.stage_sem("edge_loaded"), chip.stage_sem("tokw_loaded"), chip.stage_sem("cls_loaded")
        s_wp, s_wl = chip.stage_sem("patch_matrix"), chip.stage_sem("patch_matrix_sb")
        s_conv, s_edge, s_lo, s_hi = (chip.stage_sem("tok_conv"), chip.stage_sem("tok_edge"), chip.stage_sem("tok_low"),
                                      chip.stage_sem("tok_high"))
        pw = chip.psum[:, 7, :]
        pe_edge = chip.psum[:, 6, 0:NB * NV]
        block = ctx.enter_context(nc.Block())

        @block.sync
        def _(sp):
            sp.dma_start(tw[:, :, :], tokw).then_inc(s_w, 16)
            a, z = GROUP_SPAN[0]
            sp.dma_start(chip.small[:, a:z], small[:, a:z]).then_inc(chip.small_loaded[0], 16)
            for b in range(NB):
                for j in range(2):
                    sp.dma_start(xt[:, b, 8 * j:8 * j + 8], x[:, b, 8 * j:8 * j + 8]).then_inc(s_x[b][j], 16)
            for g in range(1, len(GROUPS)):
                a, z = GROUP_SPAN[g]
                sp.dma_start(chip.small[:, a:z], small[:, a:z]).then_inc(chip.small_loaded[g], 16)

        @block.scalar
        def _(act):
            act.dma_start(xe[:, :, :], xedge).then_inc(s_e, 16)
            act.dma_start(chip.h[:, 0:1], cls2).then_inc(s_cls, 16)
            for b in range(NB):
                hv = chip.h[64 * b:64 * b + 64, 1:NTOK].rearrange("p (v n) -> p n v", n=NN)
                for j in range(2):
                    act.wait_ge(s_conv, 2 * b + j + 1)
                    nc.scalar.activation(hv[:, 8 * j:8 * j + 8, :],
                                         chip.psum[0:64, 2 * b + j, :].rearrange("p (m v) -> p m v", v=NV),
                                         ACT.Copy).then_inc(s_lo, 1)

        @block.tensor
        def _(pe):
            pe.wait_ge(s_w, 16)
            chip.need(pe, 0)
            dft = chip.w("dft", rows=18)
            for d in range(D):
                for half in range(2):
                    last = nc.tensor.matmul(pw[64 * half:64 * half + 64, 8 * d:8 * d + 8], tw[:, d, :],
                                            dft[:, 8 * half:8 * half + 8], start=True, stop=True)
            last.then_inc(s_wp, 1)
            pe.wait_ge(s_wl, 1)
            pe.wait_ge(s_e, 16)
            for r in range(4):
                last = nc.tensor.matmul(pe_edge, wl[:, r].rearrange("p t d -> p (t d)"),
                                        xe[:, :, :].rearrange("p b v -> p (b v)"), start=(r == 0), stop=(r == 3))
            last.then_inc(s_edge, 1)
            for b in range(NB):
                for j in range(2):
                    pe.wait_ge(s_x[b][j], 16)
                    for r in range(4):
                        last = nc.tensor.matmul(chip.psum[:, 2 * b + j, :], wl[:, r].rearrange("p t d -> p (t d)"),
                                                xt[:, b, 8 * j:8 * j + 8, r, :], start=(r == 0), stop=(r == 3))
                    last.then_inc(s_conv, 1)

        @block.vector
        def _(v):
            nc.vector.memset(chip.h[:, NTOK:TP], 0.0).then_inc(s_hi, 1)
            v.wait_ge(s_wp, 1)
            nc.vector.tensor_copy(wl[:, :, :, :], pw.rearrange("p (d t r) -> p r t d", t=2, r=4)).then_inc(s_wl, 1)
            for b in range(NB):
                hv = chip.h[64 * b:64 * b + 64, 1:NTOK].rearrange("p (v n) -> p n v", n=NN)
                v.wait_ge(s_lo, 2 * b + 2)
                for n0, n1, src in ((0, 7, chip.psum[64:128, 2 * b, NV:8 * NV]),
                                    (7, 15, chip.psum[64:128, 2 * b + 1, :])):
                    nc.vector.tensor_tensor(hv[:, n0:n1, :], src.rearrange("p (m v) -> p m v", v=NV),
                                            hv[:, n0:n1, :], ALU.add).then_inc(s_hi, 1)
                v.wait_ge(s_edge, 1)
                nc.vector.tensor_tensor(hv[:, 15, :], pe_edge[64:128, NV * b:NV * b + NV], hv[:, 15, :],
                                        ALU.add).then_inc(s_hi, 1)
            v.wait_ge(s_cls, 16)



def linear_attention(chip):
    nc = chip.nc
    k_ln = chip.next_norm()
    with ExitStack() as ctx:
        def sb(name, shape):
            return ctx.enter_context(nc.sbuf_tensor(name, shape, F32))
        xn, ke, q, g = sb("xn", [P, TP]), sb("ke", [P, TP]), sb("q", [P, TP]), sb("g", [P, TP])
        vt, kt = sb("vt", [TT, NT, 128]), sb("kt", [TT, NT, 128])
        hg = sb("hg", [32, TP])
        kmax, nmax, ksum, kinv = sb("kmax", [P, NCH]), sb("nmax", [P, 1]), sb("ksum", [P, NCH]), sb("kinv", [P, 2])
        rs2, sq2 = sb("rs2", [P, TP]), sb("sq2", [P, TP])
        cx = sb("cx", [P, 128])
        (s_r2, s_k, s_xn, s_g1, s_hg, s_g2, s_v, s_vt, s_nmax, s_ke, s_q, s_qs, s_kt, s_kts, s_cx, s_cxs, s_o,
         s_og, s_p) = (chip.stage_sem("a0_" + n) for n in (
             "rstd2", "k", "xn", "gate1", "gate1_act", "gate2", "v", "v_sb", "neg_max", "kexp", "q", "q_sb",
             "kt", "kt_sb", "context", "context_sb", "out", "gated", "proj"))
        s_step = chip.stage_sem("a0_dve_step")
        s_gate = chip.stage_sem("a0_gate")
        s_log2 = chip.stage_sem("a0_log2")
        block = ctx.enter_context(nc.Block())
        pa, pb, pc = chip.pa, chip.pb, chip.pc

        @block.tensor
        def _(pe):
            norm_tensor(chip, k_ln, chip.h)
            chip.need(pe, 1)
            for c in range(NCH):
                pe.wait_ge(chip.ln_out, NCH * k_ln + c + 1)
                nc.tensor.matmul(pa[:, c, 0:CH], chip.w("a0_wk"), chunk(chip.xl, c), start=True, stop=True).then_inc(s_k, 1)
            pe.wait_ge(s_r2, NCH)
            for j in range(NT):
                last = nc.tensor.matmul(pb[0:TT, j // 3, 128 * (j % 3):128 * (j % 3) + 128],
                                        chip.xl[:, TT * j:TT * j + TT], chip.w("a0_wv"), start=True, stop=True)
            last.then_inc(s_v, 1)
            for c in range(NCH):
                pe.wait_ge(s_xn, c + 1)
                if c == 2:
                    pe.wait_ge(s_hg, 1)
                nc.tensor.matmul(pc[0:32, c % 2, 0:CH], chip.w("a0_wg1"), chunk(xn, c), start=True,
                                 stop=True).then_inc(s_g1, 1)
            pe.wait_ge(s_ke, NCH)
            for c in range(NCH):
                nc.tensor.matmul(pa[:, c, 0:CH], chip.w("a0_wq"), chunk(chip.xl, c), start=True,
                                 stop=True).then_inc(s_q, 1)
            pe.wait_ge(s_vt, 1)
            for j in range(NT):
                last = nc.tensor.transpose(pb[0:TT, j // 3, 128 * (j % 3):128 * (j % 3) + 128],
                                           ke[:, TT * j:TT * j + TT], chip.w("ident"))
            last.then_inc(s_kt, 1)
            for c in range(NCH):
                pe.wait_ge(s_hg, NCH)
                if c == 2:
                    pe.wait_ge(s_gate, 1)
                nc.tensor.matmul(pc[:, c % 2, 0:CH], chip.w("a0_wg2", rows=32), hg[:, c * CH:(c + 1) * CH],
                                 start=True, stop=True).then_inc(s_g2, 1)
            pe.wait_ge(s_kts, 1)
            pe.wait_ge(s_gate, NCH)
            for j in range(NT):
                last = nc.tensor.matmul(pc[:, 0, 0:128], kt[:, j, :], vt[:, j, :], start=(j == 0), stop=(j == NT - 1))
            last.then_inc(s_cx, 1)
            pe.wait_ge(s_cxs, 1)
            pe.wait_ge(s_qs, NCH)
            for c in range(NCH):
                nc.tensor.matmul(pa[:, c, 0:CH], cx[:, :], chunk(q, c), start=True, stop=True).then_inc(s_o, 1)
            for c in range(NCH):
                pe.wait_ge(s_og, c + 1)
                nc.tensor.matmul(pb[:, c, 0:CH], chip.w("a0_wproj"), chunk(ke, c), start=True, stop=True).then_inc(s_p, 1)

        @block.scalar
        def _(act):
            norm_scalar(chip, k_ln)
            for c in range(NCH):
                nc.scalar.activation(chunk(sq2, c), pb[:, c, 0:CH], ACT.Ln, bias=chip.w("eps", first=1, cols=1),
                                     scale=1.0 + EPS).then_inc(s_log2, 1)
                act.wait_ge(s_log2, c + 1)
                nc.scalar.activation(chunk(rs2, c), chunk(sq2, c), ACT.Exp, scale=-0.5).then_inc(s_r2, 1)
            act.wait_ge(s_nmax, 1)
            for c in range(NCH):
                n = LAST if c == NCH - 1 else CH
                nc.scalar.activation(ke[:, c * CH:c * CH + n], pa[:, c, 0:n], ACT.Exp, bias=nmax[:, :],
                                     accum_out=ksum[:, c:c + 1]).then_inc(s_ke, 1)
            for c in range(NCH):
                act.wait_ge(s_g1, c + 1)
                nc.scalar.activation(hg[:, c * CH:(c + 1) * CH], pc[0:32, c % 2, 0:CH], ACT.Gelu,
                                     bias=chip.w("a0_bg1", rows=32)).then_inc(s_hg, 1)
            act.wait_ge(s_kt, 1)
            nc.scalar.activation(kt[:, :, :].rearrange("p (c j) n -> p c j n", c=3), pb[0:TT, :, 0:384].rearrange("p c (j n) -> p c j n", n=128),
                                 ACT.Copy).then_inc(s_kts, 1)
            for c in range(NCH):
                act.wait_ge(s_g2, c + 1)
                nc.scalar.activation(chunk(g, c), pc[:, c % 2, 0:CH], ACT.Sigmoid,
                                     bias=chip.w("a0_bg2")).then_inc(s_gate, 1)

        @block.vector
        def _(v):
            steps = Steps(s_step)
            norm_vector(chip, k_ln, chip.h, chip.xl)
            chip.need(v, 1)
            for c in range(NCH):
                v.wait_ge(s_k, c + 1)
                n = LAST if c == NCH - 1 else CH
                last = steps.mark(nc.vector.reduce_max(kmax[:, c:c + 1], pa[:, c, 0:n], AX.X))
            v.wait_ge(s_step, last)
            nc.vector.tensor_reduce(nmax[:, :], kmax[:, :], AX.X, ALU.max, negate=True).then_inc(s_nmax, 1)
            for c in range(NCH):
                v.wait_ge(s_r2, c + 1)
                steps.settle(v, nc.vector.tensor_tensor(chunk(xn, c), chunk(chip.xc, c), chunk(rs2, c), ALU.mult))
                nc.vector.tensor_scalar(chunk(xn, c), chunk(xn, c), chip.w("a0_g"), chip.w("a0_b"),
                                        ALU.mult, ALU.add).then_inc(s_xn, 1)
            nc.vector.memset(ke[:, NTOK:TP], 0.0).then_inc(s_ke, 1)
            v.wait_ge(s_v, 1)
            nc.vector.tensor_copy(vt[:, :, :].rearrange("p (c j) n -> p c j n", c=3), pb[0:TT, :, 0:384].rearrange("p c (j n) -> p c j n", n=128)
                                  ).then_inc(s_vt, 1)
            v.wait_ge(s_ke, NCH + 1)
            steps.settle(v, nc.vector.reduce_sum(kinv[:, 0:1], ksum[:, :], AX.X))
            steps.settle(v, nc.vector.reciprocal(kinv[:, 1:2], kinv[:, 0:1]))
            for c in range(NCH):
                v.wait_ge(s_q, c + 1)
                nc.vector.tensor_copy(chunk(q, c), pa[:, c, 0:CH]).then_inc(s_qs, 1)
            v.wait_ge(s_cx, 1)
            nc.vector.scalar_tensor_tensor(cx[:, :], pc[:, 0, 0:128], kinv[:, 1:2], chip.w("a0_mask"),
                                           ALU.mult, ALU.mult).then_inc(s_cxs, 1)
            for c in range(NCH):
                v.wait_ge(s_o, c + 1)
                v.wait_ge(s_gate, NCH)
                nc.vector.tensor_tensor(chunk(ke, c), pa[:, c, 0:CH], chunk(g, c), ALU.mult).then_inc(s_og, 1)
            for c in range(NCH):
                v.wait_ge(s_p, c + 1)
                nc.vector.scalar_tensor_tensor(chunk(chip.h, c), pb[:, c, 0:CH], chip.w("a0_bproj"),
                                               chunk(chip.h, c), ALU.add, ALU.add).then_inc(s_step, 1)



def route_vector(chip, steps, r, kind, n_e, group_bias2, s):
    nc, v = chip.nc, chip.nc.vector
    e2 = 2 * n_e
    lg, eq, cand, o1, o2 = r["lg"], r["eq"], r["cand"], r["o1"], r["o2"]
    m1, m2, mm, ssum, w1, w2, dd = (r[x] for x in ("m1", "m2", "mm", "ssum", "w1", "w2", "dd"))

    def by_tile(t):
        return t[:, :, :].rearrange("p (j b) e -> p j (b e)", b=2)

    def over_tiles(row):
        return row[0:TT].unsqueeze(1).to_broadcast([TT, NT, e2])

    def over_experts(m):
        return m[:, :].unsqueeze(2).to_broadcast([TT, 2 * NT, n_e])

    def first_best(src, best, one_hot):
        steps.settle(v, nc.vector.tensor_reduce(best[:, :], src[:, :, :], AX.X, ALU.max))
        steps.settle(v, nc.vector.tensor_tensor(eq[:, :, :], src[:, :, :], over_experts(best), ALU.is_equal))
        steps.settle(v, nc.vector.tensor_tensor(by_tile(cand), by_tile(eq), over_tiles(chip.w(f"rev{n_e}")), ALU.mult))
        steps.settle(v, nc.vector.tensor_reduce(mm[:, :], cand[:, :, :], AX.X, ALU.max))
        steps.settle(v, nc.vector.tensor_tensor(one_hot[:, :, :], cand[:, :, :], over_experts(mm), ALU.is_equal))

    v.wait_ge(s["logits"], 1)
    steps.settle(v, nc.vector.tensor_tensor(
        by_tile(lg), chip.pc[0:TT, 1, 0:NT * e2].rearrange("p (j n) -> p j n", n=e2),
        over_tiles(chip.w(r["name"] + "_gbias")), ALU.add))
    if group_bias2:
        steps.settle(v, nc.vector.tensor_tensor(by_tile(lg), by_tile(lg), over_tiles(chip.w(r["name"] + "_gbias2")), ALU.add))
    first_best(lg, m1, o1)
    tg = r["tg"]

    def spread():
        nc.vector.tensor_tensor(r["d"][:, :, :], lg[:, :, :], over_experts(m1), ALU.subtract).then_inc(s["d"], 1)

    if kind == "switch":
        spread()
        nc.vector.memset(tg[:, :, e2:32], 0.0).then_inc(s["gates"], 1)
        nc.vector.tensor_copy(tg[:, :, 0:e2], by_tile(o1)).then_inc(s["gates"], 1)
        v.wait_ge(s["exp"], 1)
        steps.settle(v, nc.vector.tensor_reduce(ssum[:, :], r["ex"][:, :, :], AX.X, ALU.add))
        steps.settle(v, nc.vector.reciprocal(w1[:, :], ssum[:, :]))
        nc.vector.tensor_copy(tg[:, :, 32:34], w1[:, :].rearrange("p (j b) -> p j b", b=2)).then_inc(s["gates"], 1)
        return 3
    steps.settle(v, nc.vector.scalar_tensor_tensor(r["lg2"][:, :, :], o1[:, :, :], -1e30, lg[:, :, :], ALU.mult, ALU.add))
    first_best(r["lg2"], m2, o2)
    if kind == "mask":
        nc.vector.tensor_tensor(tg[:, :, 0:e2], by_tile(o1), by_tile(o2), ALU.add).then_inc(s["gates"], 1)
        return 1
    steps.settle(v, nc.vector.tensor_tensor(dd[:, 0:2 * NT], m2[:, :], m1[:, :], ALU.subtract))
    if kind == "probs":
        spread()
        nc.vector.tensor_copy(dd[:, 2 * NT:4 * NT], dd[:, 0:2 * NT]).then_inc(s["d"], 1)
        v.wait_ge(s["exp"], 2)
        steps.settle(v, nc.vector.tensor_reduce(ssum[:, :], r["ex"][:, :, :], AX.X, ALU.add))
        steps.settle(v, nc.vector.reciprocal(w1[:, :], ssum[:, :]))
        steps.settle(v, nc.vector.tensor_scalar(dd[:, 0:2 * NT], dd[:, 2 * NT:4 * NT], 1.0, None, ALU.subtract))
        nc.vector.tensor_tensor(r["gap"][:, :], dd[:, 0:2 * NT], w1[:, :], ALU.mult).then_inc(s["gap"], 1)
    else:
        nc.vector.tensor_copy(r["gap"][:, :], dd[:, 0:2 * NT]).then_inc(s["gap"], 1)
    v.wait_ge(s["weights"], 2)
    steps.settle(v, nc.vector.tensor_tensor(o1[:, :, :], o1[:, :, :], over_experts(r["s1"]), ALU.mult))
    steps.settle(v, nc.vector.tensor_tensor(o2[:, :, :], o2[:, :, :], over_experts(r["s2"]), ALU.mult))
    steps.settle(v, nc.vector.tensor_tensor(o1[:, :, :], o1[:, :, :], o2[:, :, :], ALU.add))
    for part in range(3):
        at = tg[:, :, part * e2:part * e2 + e2]
        steps.settle(v, nc.vector.tensor_copy(r["low"][:, :, :], by_tile(o1)))
        steps.settle(v, nc.vector.tensor_copy(at, r["low"][:, :, :]))
        if part < 2:
            steps.settle(v, nc.vector.tensor_tensor(by_tile(o1), by_tile(o1), at, ALU.subtract))
    nc.vector.memset(r["scrap"][:, :], 0.0).then_inc(s["gates"], 1)
    return 1


def route_scalar(chip, r, kind, s):
    nc, act = chip.nc, chip.nc.scalar
    if kind in ("switch", "probs"):
        act.wait_ge(s["d"], 1)
        nc.scalar.activation(r["ex"][:, :, :], r["d"][:, :, :], ACT.Exp).then_inc(s["exp"], 1)
    if kind == "probs":
        act.wait_ge(s["d"], 2)
        nc.scalar.activation(r["dd"][:, 2 * NT:4 * NT], r["dd"][:, 2 * NT:4 * NT], ACT.Exp).then_inc(s["exp"], 1)
    if kind in ("probs", "logits"):
        act.wait_ge(s["gap"], 1)
        nc.scalar.activation(r["s1"][:, :], r["gap"][:, :], ACT.Sigmoid, scale=-1.0).then_inc(s["weights"], 1)
        nc.scalar.activation(r["s2"][:, :], r["gap"][:, :], ACT.Sigmoid).then_inc(s["weights"], 1)


def route_tiles(chip, sb, name, n_e, n_rows):
    r = {x: sb(name + x, [TT, 2 * NT, n_e]) for x in ("lg", "lg2", "eq", "cand", "o1", "o2", "d", "ex")}
    r.update({x: sb(name + x, [TT, 2 * NT]) for x in ("m1", "m2", "mm", "ssum", "w1", "w2", "s1", "s2", "gap")})
    r["dd"] = sb(name + "dd", [TT, 4 * NT])
    r["scrap"] = sb(name + "scrap", [TT, 1])
    r["low"] = sb(name + "low", [TT, NT, 2 * n_e], BF16)
    r["tg"] = sb(name + "tg", [TT, NT, n_rows])
    r["rows"] = sb(name + "rows", [n_rows, TP])
    r["rows16"] = sb(name + "rows16", [128, TP], BF16)
    r["name"] = name
    return r


RING = 3
LEAD = 2


def experts2(chip, name, slab, group, n_e, hc, func, kind):
    nc = chip.nc
    k_ln = chip.next_norm()
    hid = 128 * hc
    nu = 6 * hc
    pairs = n_e // 2
    e2 = 2 * n_e
    n_parts = 3 if kind == "logits" else 1
    k_rows = n_parts * e2
    n_rows = 34 if kind == "switch" else k_rows
    with ExitStack() as ctx:
        def sb(nm, shape, dt=F32):
            return ctx.enter_context(nc.sbuf_tensor(nm, shape, dt))
        ws = sb(name + "slab", [128, 2, SLAB2[hc]])
        hs = sb(name + "hs", [128, RING, CH])
        hm = sb(name + "hm", [128, RING, CH])
        r = route_tiles(chip, sb, name, n_e, n_rows)
        s = {x: chip.stage_sem(name + "_" + x) for x in
             ("logits", "d", "exp", "gap", "weights", "gates", "rows", "rows_sb", "total", "first", "act",
              "gated", "second", "done", "step", "prob", "prob_sb")}
        s_slab = [chip.stage_sem(f"{name}_slab{k}") for k in range(2)]
        if kind == "switch":
            cnt, zero, thr = sb("cnt", [e2, TP]), sb("zero", [e2, TP]), sb("thr", [e2, 1])
            tot = sb("tot", [e2, 1])
            big = sb("big", [128, 2])
            yp, yn = sb("yp", [P, TP]), sb("yn", [P, TP])
            probs = sb("probs", [P, TP])
            mk = sb("mk", [P, TP], mybir.dt.uint32)
        block = ctx.enter_context(nc.Block())
        pa, pb, pc = chip.pa, chip.pb, chip.pc
        n_gates = 3 if kind == "switch" else 1

        def w1(k, b, h):
            return ws[:, k, hid * b + 128 * h:hid * b + 128 * h + 128]

        def w2(k, h):
            return ws[:, k, 2 * hid + 64 * h:2 * hid + 64 * h + 64]

        def b1(k, h):
            return ws[:, k, 2 * hid + 64 * hc + h:2 * hid + 64 * hc + h + 1]

        def sel(k, b):
            n = 2 * hid + 65 * hc + 64 * b
            return ws[0:k_rows, k, n:n + 64].bitcast(BF16)

        def unit(n):
            k, m = divmod(n, nu)
            bc, h = divmod(m, hc)
            b, c = divmod(bc, NCH)
            return k, b, c, h

        @block.sync
        def _(sp):
            for k in range(2):
                sp.dma_start(ws[:, k, :], slab[k]).then_inc(s_slab[k], 16)
            with sp.Fori(1, pairs) as i:
                for k in range(2):
                    sp.wait_ge(s["second"], 2 * nu * i + (RING - 2 * nu + (k + 1) * nu))
                    sp.dma_start(ws[:, k, :], slab[bass.ds(2 * i + k, 1)].rearrange("a p n -> p (a n)")
                                 ).then_inc(s_slab[k], 16)

        @block.tensor
        def _(pe):
            norm_tensor(chip, k_ln, chip.h)
            chip.need(pe, group)
            for j in range(NT):
                if j % 3 == 0:
                    pe.wait_ge(chip.ln_out, NCH * k_ln + j // 3 + 1)
                last = nc.tensor.matmul(pc[0:TT, 1, e2 * j:e2 * j + e2], chip.xl[:, TT * j:TT * j + TT],
                                        chip.w(name + "_gate"), start=True, stop=True)
            last.then_inc(s["logits"], 1)
            pe.wait_ge(s["gates"], n_gates)
            for j in range(NT):
                last = nc.tensor.transpose(pb[0:n_rows, j // 3, TT * (j % 3):TT * (j % 3) + TT], r["tg"][:, j, :],
                                           chip.w("ident", rows=TT, cols=TT))
            last.then_inc(s["rows"], 1)
            if kind == "switch":
                pe.wait_ge(s["total"], 1)
                nc.tensor.matmul(pc[0:e2, 0, 0:1], chip.w("shift", rows=e2), cnt[:, NTOK - 1:NTOK],
                                 start=True, stop=True).then_inc(s["total"], 1)
            pe.wait_ge(s["rows_sb"], 2)
            for c in range(NCH):
                nc.tensor.matmul(pa[:, c, 0:CH], chip.w(name + "_b2", rows=k_rows), chunk(r["rows"][0:k_rows], c),
                                 start=True, stop=False, skip_group_check=True)

            def first(i, n):
                k, b, c, h = unit(n % (2 * nu))
                i = i + n // (2 * nu)
                if (n % nu) == 0:
                    pe.wait_ge(s_slab[k], 16 * i + 16)
                if h == 0:
                    q = (n // hc) % 2
                    pe.wait_ge(s["gated"], 2 * nu * i + (n % (2 * nu)) - hc + RING)
                    nc.tensor.matmul(pc[:, q, 0:CH], sel(k, b), chunk(r["rows16"][0:k_rows], c), start=True, stop=True)
                pe.wait_ge(s["act"], 2 * nu * i + (n % (2 * nu)) + 1)
                nc.tensor.matmul(pb[:, n % RING, 0:CH], w1(k, b, h), chunk(chip.xl, c), start=True,
                                 stop=True).then_inc(s["first"], 1)

            def pair(i, last_pair):
                for n in range(2 * nu):
                    k, b, c, h = unit(n)
                    pe.wait_ge(s["gated"], 2 * nu * i + n + 1 + RING)
                    nc.tensor.matmul(pa[64 * b:64 * b + 64, c, 0:CH], w2(k, h), hm[:, n % RING, :], start=False,
                                     stop=False, skip_group_check=True).then_inc(s["second"], 1)
                    if not (last_pair and n + LEAD >= 2 * nu):
                        first(i, n + LEAD)

            for n in range(LEAD):
                first(0, n)
            with pe.Fori(0, pairs - 1) as i:
                pair(i, False)
            pair(pairs - 1, True)
            if kind == "switch":
                for c in range(NCH):
                    nc.tensor.matmul(pb[:, c, 0:CH], chip.w("seqsel", rows=2, row0=32), r["rows"][32:34, c * CH:(c + 1) * CH],
                                     start=True, stop=True).then_inc(s["prob"], 1)

        @block.scalar
        def _(act):
            norm_scalar(chip, k_ln)
            route_scalar(chip, r, kind, s)
            act.sem_inc(s["act"], RING)
            with act.Fori(0, pairs) as i:
                for n in range(2 * nu):
                    k, b, c, h = unit(n)
                    act.wait_ge(s["first"], 2 * nu * i + n + 1)
                    act.wait_ge(s["gated"], 2 * nu * i + n + 1)
                    nc.scalar.activation(hs[:, n % RING, :], pb[:, n % RING, 0:CH], func,
                                         bias=b1(k, h)).then_inc(s["act"], 1)
            if kind == "switch":
                for c in range(NCH):
                    act.wait_ge(s["prob"], c + 1)
                    nc.scalar.activation(chunk(probs, c), pb[:, c, 0:CH], ACT.Copy).then_inc(s["prob_sb"], 1)

        @block.vector
        def _(v):
            steps = Steps(s["step"])
            norm_vector(chip, k_ln, chip.h, chip.xl)
            chip.need(v, group)
            assert route_vector(chip, steps, r, kind, n_e, name == "f3", s) == n_gates
            v.sem_inc(s["gated"], RING)
            v.wait_ge(s["rows"], 1)
            if kind == "switch":
                steps.settle(v, nc.vector.memset(zero[:, :], 0.0))
                steps.settle(v, nc.vector.tensor_copy(chunks(r["rows"][0:34]), pb[0:34, :, 0:CH]))
                steps.settle(v, nc.vector.tensor_tensor_scan(cnt[:, :], r["rows"][0:e2, :], zero[:, :], 0.0, ALU.add, ALU.add))
                v.sem_inc(s["total"], 1)
                v.wait_ge(s["total"], 2)
                steps.settle(v, nc.vector.tensor_scalar(thr[:, :], pc[0:e2, 0, 0:1], -1.0, float(CAPACITY), ALU.mult, ALU.add))
                steps.settle(v, nc.vector.scalar_tensor_tensor(cnt[:, :], cnt[:, :], thr[:, :], r["rows"][0:e2, :],
                                                               ALU.is_le, ALU.mult))
                nc.vector.tensor_copy(r["rows"][0:e2, :], cnt[:, :]).then_inc(s["rows_sb"], 1)
                nc.vector.tensor_copy(r["rows16"][0:e2, :], cnt[:, :]).then_inc(s["rows_sb"], 1)
            else:
                nc.vector.tensor_copy(chunks(r["rows"][0:k_rows]), pb[0:k_rows, :, 0:CH]).then_inc(s["rows_sb"], 1)
                nc.vector.tensor_copy(chunks(r["rows16"][0:k_rows]), pb[0:k_rows, :, 0:CH]).then_inc(s["rows_sb"], 1)
            v.sem_inc(s["second"], RING)
            with v.Fori(0, pairs) as i:
                for n in range(2 * nu):
                    v.wait_ge(s["act"], 2 * nu * i + n + 1 + RING)
                    v.wait_ge(s["second"], 2 * nu * i + n + 1)
                    nc.vector.tensor_tensor(hm[:, n % RING, :], hs[:, n % RING, :], pc[:, (n // hc) % 2, 0:CH],
                                            ALU.mult).then_inc(s["gated"], 1)
            v.wait_ge(s["second"], n_e * nu + RING)
            if kind != "switch":
                nc.vector.tensor_tensor(chunks(chip.h[:, :]), chunks(chip.h[:, :]), pa[:, :, 0:CH], ALU.add
                                        ).then_inc(s["done"], 1)
                return
            v.wait_ge(s["prob_sb"], NCH)
            nc.vector.memset(big[:, 0:1], 1e4).then_inc(s["done"], 1)
            nc.vector.memset(big[:, 1:2], -1e4).then_inc(s["done"], 1)
            steps.settle(v, nc.vector.tensor_tensor(chunks(probs[:, :]), pa[:, :, 0:CH], chunks(probs[:, :]), ALU.mult))
            steps.settle(v, nc.vector.tensor_scalar(yp[:, :], probs[:, :], 0.0, None, ALU.max))
            steps.settle(v, nc.vector.tensor_scalar(yn[:, :], probs[:, :], 0.0, None, ALU.min))
            steps.settle(v, nc.vector.tensor_scalar(mk[:, :], yp[:, :], FLT_MAX, None, ALU.is_gt))
            steps.settle(v, nc.vector.copy_predicated(yp[:, :], mk[:, :], big[:, 0:1].to_broadcast([P, TP])))
            steps.settle(v, nc.vector.tensor_scalar(mk[:, :], yn[:, :], -FLT_MAX, None, ALU.is_lt))
            steps.settle(v, nc.vector.copy_predicated(yn[:, :], mk[:, :], big[:, 1:2].to_broadcast([P, TP])))
            steps.settle(v, nc.vector.tensor_tensor(yp[:, :], yp[:, :], yn[:, :], ALU.add))
            nc.vector.tensor_tensor(chip.h[:, :], chip.h[:, :], yp[:, :], ALU.add).then_inc(s["done"], 1)


def row_attention(chip):
    nc = chip.nc
    k_ln = chip.next_norm()
    n_heads, c_head = 8, 32
    hc = n_heads * c_head
    scale = 1.0 / (c_head * NTOK) ** 0.5
    with ExitStack() as ctx:
        def sb(name, shape):
            return ctx.enter_context(nc.sbuf_tensor(name, shape, F32))
        mn = sb("a1mn", [P, TP])
        mt = sb("a1mt", [TT, NT, 128])
        gram = sb("a1gram", [P, P])
        prod = sb("a1prod", [P, NB, hc])
        red = sb("a1red", [P, NB, n_heads])
        att = sb("a1att", [P, NB, n_heads])
        wa = sb("a1wa", [P, NB, hc])
        g = sb("a1g", [128, NB, 2, TP])
        s_mn, s_t, s_ts, s_g, s_gs, s_a, s_red, s_d, s_att, s_wa, s_gp, s_gate, s_o, s_og, s_y, s_h, s_step = (
            chip.stage_sem("a1_" + n) for n in ("mn", "mt", "mt_sb", "gram", "gram_sb", "scores", "summed", "diff",
                                                "att", "wv", "gate_in", "gate", "out", "gated", "proj", "h", "step"))
        block = ctx.enter_context(nc.Block())
        pa, pb, pc = chip.pa, chip.pb, chip.pc
        units = [(s, k, c) for s in range(NB) for k in range(2) for c in range(NCH)]

        @block.tensor
        def _(pe):
            norm_tensor(chip, k_ln, chip.h)
            chip.need(pe, 2)
            for j in range(NT):
                pe.wait_ge(s_mn, 4)
                last = nc.tensor.transpose(pa[0:TT, j // 3, 128 * (j % 3):128 * (j % 3) + 128],
                                           mn[:, TT * j:TT * j + TT], chip.w("ident"))
            last.then_inc(s_t, 1)

            def gate(u):
                s, k, c = units[u]
                if u >= 3:
                    pe.wait_ge(s_gate, u - 2)
                nc.tensor.matmul(pb[:, u % 3, 0:CH], chip.w("a1_wg", first=hc * s + 128 * k, cols=128), chunk(mn, c),
                                 start=True, stop=True).then_inc(s_gp, 1)

            for u in range(3):
                gate(u)
            pe.wait_ge(s_ts, 1)
            for j in range(NT):
                last = nc.tensor.matmul(pc[:, 0, 0:128], mt[:, j, :], mt[:, j, :], start=(j == 0), stop=(j == NT - 1))
            last.then_inc(s_g, 1)
            for u in range(3, 6):
                gate(u)
            pe.wait_ge(s_gs, 1)
            for s in range(NB):
                nc.tensor.matmul(pa[:, s, 0:hc], gram[64 * s:64 * s + 64, :], chip.w("a1_wq", rows=64, row0=64 * s),
                                 start=True, stop=True).then_inc(s_a, 1)
            for u in range(6, 9):
                gate(u)
            pe.wait_ge(s_red, 1)
            nc.tensor.matmul(pc[:, 1, 0:NB * n_heads], chip.w("tdiff"), red[:, :, :].rearrange("p s h -> p (s h)"),
                             start=True, stop=True).then_inc(s_d, 1)
            for u in range(9, 12):
                gate(u)
            pe.wait_ge(s_wa, 1)
            out_banks = [pc[:, 0], pc[:, 1]]
            for u, (s, k, c) in enumerate(units):
                if u >= 2:
                    pe.wait_ge(s_og, u - 1)
                nc.tensor.matmul(out_banks[u % 2][:, 0:CH], wa[:, s, 128 * k:128 * k + 128], chunk(mn, c),
                                 start=True, stop=True).then_inc(s_o, 1)
            for s in range(NB):
                for c in range(NCH):
                    for k in range(2):
                        pe.wait_ge(s_og, 6 * s + 3 * k + c + 1)
                        last = nc.tensor.matmul(pa[64 * s:64 * s + 64, c, 0:CH], chip.w("a1_wo", first=64 * k, cols=64),
                                                g[:, s, k, c * CH:(c + 1) * CH], start=(k == 0), stop=(k == 1))
                    last.then_inc(s_y, 1)

        @block.scalar
        def _(act):
            norm_scalar(chip, k_ln, twice=True)
            chip.need(act, 2)
            for u, (s, k, c) in enumerate(units):
                if u == 3:
                    act.wait_ge(s_g, 1)
                    nc.scalar.activation(gram[:, :], pc[:, 0, 0:128], ACT.Copy).then_inc(s_gs, 1)
                if u == 9:
                    act.wait_ge(s_d, 1)
                    nc.scalar.activation(att[:, :, :], pc[:, 1, 0:NB * n_heads].rearrange("p (s h) -> p s h", s=NB),
                                         ACT.Sigmoid, scale=scale).then_inc(s_att, 1)
                act.wait_ge(s_gp, u + 1)
                nc.scalar.activation(g[:, s, k, c * CH:(c + 1) * CH], pb[:, u % 3, 0:CH], ACT.Sigmoid,
                                     bias=chip.w("a1_bg", first=k, cols=1)).then_inc(s_gate, 1)

        @block.vector
        def _(v):
            steps = Steps(s_step)
            norm_vector(chip, k_ln, chip.h, chip.xl)
            chip.need(v, 2)
            for c in range(NCH):
                v.wait_ge(chip.ln_out, NCH * k_ln + c + 1)
                nc.vector.tensor_scalar(chunk(mn, c), chunk(chip.xl, c), chip.w("a1_g"), chip.w("a1_b"),
                                        ALU.mult, ALU.add).then_inc(s_mn, 1)
            v.wait_ge(s_mn, 3)
            nc.vector.memset(mn[:, NTOK:TP], 0.0).then_inc(s_mn, 1)
            v.wait_ge(s_t, 1)
            nc.vector.tensor_copy(mt[:, :, :].rearrange("p (c j) n -> p c j n", c=3),
                                  pa[0:TT, :, 0:384].rearrange("p c (j n) -> p c j n", n=128)).then_inc(s_ts, 1)
            for s in range(NB):
                v.wait_ge(s_a, s + 1)
                steps.settle(v, nc.vector.tensor_tensor(prod[:, s, :], pa[:, s, 0:hc], chip.w("a1_wk"), ALU.mult))
            nc.vector.tensor_reduce(red[:, :, :], prod[:, :, :].rearrange("p s (h c) -> p s h c", c=c_head), AX.X,
                                    ALU.add).then_inc(s_red, 1)
            v.wait_ge(s_att, 1)
            for s in range(NB):
                last = nc.vector.tensor_tensor(wa[:, s, :].rearrange("p (h c) -> p h c", c=c_head),
                                               chip.w("a1_wv").rearrange("p (h c) -> p h c", c=c_head),
                                               att[:, s, :].unsqueeze(2).to_broadcast([P, n_heads, c_head]), ALU.mult)
            last.then_inc(s_wa, 1)
            for u, (s, k, c) in enumerate(units):
                v.wait_ge(s_o, u + 1)
                v.wait_ge(s_gate, u + 1)
                gs = g[:, s, k, c * CH:(c + 1) * CH]
                nc.vector.tensor_tensor(gs, pc[:, u % 2, 0:CH], gs, ALU.mult).then_inc(s_og, 1)
            for c in range(NCH):
                v.wait_ge(s_y, NCH + c + 1)
                nc.vector.scalar_tensor_tensor(chunk(chip.h, c), pa[:, c, 0:CH], chip.w("a1_bo"), chunk(chip.h, c),
                                               ALU.add, ALU.add).then_inc(s_h, 1)


def scan_attention(chip):
    nc = chip.nc
    k_ln = chip.next_norm()
    ns = 32
    with ExitStack() as ctx:
        def sb(name, shape):
            return ctx.enter_context(nc.sbuf_tensor(name, shape, F32))
        xp = sb("a2xp", [P, 3 + TP])
        res, xcv = sb("a2res", [P, TP]), sb("a2xcv", [P, TP])
        da, cp, yc, y, zero = (sb("a2da", [ns, TP]), sb("a2cp", [ns, TP]), sb("a2yc", [ns, TP]),
                               sb("a2y", [ns, TP]), sb("a2zero", [ns, TP]))
        o = sb("a2o", [P, TP])
        acc, col = sb("a2acc", [P, 2 * NCH]), sb("a2col", [P, 6])
        s_xp, s_xps, s_res, s_ress, s_conv, s_da, s_das, s_db, s_y, s_y2, s_y2s, s_p, s_o, s_m, s_negm, s_sq, s_v, s_vl, s_rs, s_h, s_step = (
            chip.stage_sem("a2_" + n) for n in ("xp", "xp_sb", "res", "res_sb", "conv", "da", "da_sb", "db", "y", "cy",
                                                "cy_sb", "proj", "o", "mean", "neg_mean", "square", "var", "var_log",
                                                "rstd", "h", "step"))
        block = ctx.enter_context(nc.Block())
        pa, pb, pc = chip.pa, chip.pb, chip.pc

        @block.tensor
        def _(pe):
            norm_tensor(chip, k_ln, chip.h)
            chip.need(pe, 3)
            for c in range(NCH):
                pe.wait_ge(chip.ln_out, NCH * k_ln + c + 1)
                nc.tensor.matmul(pa[:, c, 0:CH], chip.w("a2_wxp"), chunk(chip.xl, c), start=True, stop=True).then_inc(s_xp, 1)
            for c in range(NCH):
                nc.tensor.matmul(pb[:, c, 0:CH], chip.w("a2_wres"), chunk(chip.xl, c), start=True, stop=True).then_inc(s_res, 1)
            pe.wait_ge(s_xps, NCH + 1)
            for c in range(NCH):
                pe.wait_ge(s_conv, c + 1)
                nc.tensor.matmul(pa[0:ns, c, 0:CH], chip.w("a2_dt"), chunk(xcv, c), start=True, stop=True).then_inc(s_da, 1)
            pe.wait_ge(s_ress, NCH)
            for c in range(NCH):
                nc.tensor.matmul(pb[0:ns, c, 0:CH], chip.w("a2_bw"), chunk(xcv, c), start=True, stop=True).then_inc(s_db, 1)
            pe.wait_ge(s_das, NCH)
            pe.wait_ge(s_y, 1)
            for c in range(NCH):
                nc.tensor.matmul(pa[:, c, 0:CH], chip.w("a2_cw", rows=ns), y[:, c * CH:(c + 1) * CH], start=True,
                                 stop=True).then_inc(s_y2, 1)
            for c in range(NCH):
                pe.wait_ge(s_y2s, c + 1)
                nc.tensor.matmul(pb[:, c, 0:CH], chip.w("a2_ow"), chunk(res, c), start=True, stop=True).then_inc(s_p, 1)
            pe.wait_ge(s_o, NCH)
            nc.tensor.matmul(pc[:, 0, 0:NCH], chip.w("chmean"), acc[:, 0:NCH], start=True, stop=True).then_inc(s_m, 1)
            pe.wait_ge(s_sq, 1)
            nc.tensor.matmul(pc[:, 1, 0:1], chip.w("chmean"), col[:, 1:2], start=True, stop=True).then_inc(s_v, 1)

        @block.scalar
        def _(act):
            norm_scalar(chip, k_ln)
            for c in range(NCH):
                act.wait_ge(s_xp, c + 1)
                nc.scalar.activation(xp[:, 3 + c * CH:3 + (c + 1) * CH], pa[:, c, 0:CH], ACT.Identity,
                                     bias=chip.w("a2_bxp")).then_inc(s_xps, 1)
            for c in range(NCH):
                act.wait_ge(s_da, c + 1)
                nc.scalar.activation(da[:, c * CH:(c + 1) * CH], pa[0:ns, c, 0:CH], ACT.Exp).then_inc(s_das, 1)
            for c in range(NCH):
                act.wait_ge(s_res, c + 1)
                nc.scalar.activation(chunk(res, c), pb[:, c, 0:CH], ACT.Silu, bias=chip.w("a2_bres")).then_inc(s_ress, 1)
            act.wait_ge(s_negm, 1)
            nc.scalar.activation(chip.xc[:, 0:NTOK], o[:, 0:NTOK], ACT.Square, bias=col[:, 0:1],
                                 accum_out=col[:, 1:2]).then_inc(s_sq, 1)
            act.wait_ge(s_v, 1)
            nc.scalar.activation(col[:, 2:3], pc[:, 1, 0:1], ACT.Ln, bias=chip.w("eps", cols=1)).then_inc(s_vl, 1)
            act.wait_ge(s_vl, 1)
            nc.scalar.activation(col[:, 3:4], col[:, 2:3], ACT.Exp, scale=-0.5).then_inc(s_rs, 1)

        @block.vector
        def _(v):
            steps = Steps(s_step)
            nc.vector.memset(xp[:, 0:3], 0.0).then_inc(s_xps, 1)
            steps.settle(v, nc.vector.memset(zero[:, :], 0.0))
            norm_vector(chip, k_ln, chip.h, chip.xl)
            chip.need(v, 3)
            for c in range(NCH):
                v.wait_ge(s_xps, c + 2)
                a = c * CH
                steps.settle(v, nc.vector.tensor_scalar(chunk(xcv, c), xp[:, a:a + CH], chip.w("a2_convw", cols=1),
                                                        chip.w("a2_convb"), ALU.mult, ALU.add))
                for k in range(1, 4):
                    i = nc.vector.scalar_tensor_tensor(chunk(xcv, c), xp[:, a + k:a + k + CH],
                                                       chip.w("a2_convw", first=k, cols=1), chunk(xcv, c),
                                                       ALU.mult, ALU.add)
                    if k < 3:
                        steps.settle(v, i)
                    else:
                        i.then_inc(s_conv, 1)
            v.wait_ge(s_das, NCH)
            steps.settle(v, nc.vector.tensor_tensor_scan(cp[:, :], da[:, :], zero[:, :], 1.0, ALU.mult, ALU.add))
            v.wait_ge(s_db, NCH)
            steps.settle(v, nc.vector.tensor_tensor(chunks(cp[:, :]), chunks(cp[:, :]), pb[0:ns, :, 0:CH], ALU.mult))
            steps.settle(v, nc.vector.tensor_tensor_scan(yc[:, :], cp[:, :], zero[:, :], 0.0, ALU.add, ALU.add))
            steps.settle(v, nc.vector.tensor_tensor(y[:, 1:TP], yc[:, 0:TP - 1], da[:, 1:TP], ALU.mult))
            steps.settle(v, nc.vector.tensor_tensor(y[:, 1:TP], yc[:, 1:TP], y[:, 1:TP], ALU.subtract))
            nc.vector.tensor_copy(y[:, 0:1], pb[0:ns, 0, 0:1]).then_inc(s_y, 1)
            v.wait_ge(s_ress, NCH)
            for c in range(NCH):
                v.wait_ge(s_y2, c + 1)
                nc.vector.tensor_tensor(chunk(res, c), pa[:, c, 0:CH], chunk(res, c), ALU.mult).then_inc(s_y2s, 1)
            for c in range(NCH):
                v.wait_ge(s_p, c + 1)
                n = LAST if c == NCH - 1 else CH
                a = c * CH
                nc.vector.scalar_tensor_tensor(o[:, a:a + n], pb[:, c, 0:n], chip.w("a2_ob"), xcv[:, a:a + n],
                                               ALU.add, ALU.add, accum_out=acc[:, c:c + 1]).then_inc(s_o, 1)
            v.wait_ge(s_m, 1)
            nc.vector.tensor_reduce(col[:, 0:1], pc[:, 0, 0:NCH], AX.X, ALU.add, negate=True).then_inc(s_negm, 1)
            v.wait_ge(s_rs, 1)
            steps.settle(v, nc.vector.tensor_tensor(col[:, 4:5], col[:, 3:4], chip.w("a2_g"), ALU.mult))
            steps.settle(v, nc.vector.tensor_scalar(col[:, 5:6], col[:, 0:1], col[:, 4:5], chip.w("a2_b"), ALU.mult, ALU.add))
            steps.settle(v, nc.vector.tensor_scalar(o[:, 0:NTOK], o[:, 0:NTOK], col[:, 4:5], col[:, 5:6], ALU.mult, ALU.add))
            nc.vector.tensor_tensor(chip.h[:, 0:NTOK], chip.h[:, 0:NTOK], o[:, 0:NTOK], ALU.add).then_inc(s_h, 1)


def experts3(chip, slab):
    nc = chip.nc
    k_ln = chip.next_norm()
    name, n_e = "f2", 6
    e2, k_rows = 2 * n_e, 3 * 2 * n_e
    nu, pairs, ring = NCH, n_e // 2, 2
    with ExitStack() as ctx:
        def sb(nm, shape, dt=F32):
            return ctx.enter_context(nc.sbuf_tensor(nm, shape, dt))
        ws = sb("f2slab", [128, 2, SLAB3])
        rh = sb("f2rh", [64, TP])
        h1, h2, hg = (sb("f2" + n, [128, ring, CH]) for n in ("h1", "h2", "hg"))
        r = route_tiles(chip, sb, name, n_e, k_rows)
        s = {x: chip.stage_sem(name + "_" + x) for x in
             ("router", "router_sb", "logits", "d", "exp", "gap", "weights", "gates", "rows", "rows_sb", "first",
              "act", "mid", "mid_act", "gated", "third", "done", "step")}
        s_slab = [chip.stage_sem(f"f2_slab{k}") for k in range(2)]
        block = ctx.enter_context(nc.Block())
        pa, pb, pc = chip.pa, chip.pb, chip.pc

        @block.sync
        def _(sp):
            for k in range(2):
                sp.dma_start(ws[:, k, :], slab[k]).then_inc(s_slab[k], 16)
            with sp.Fori(1, pairs) as i:
                for k in range(2):
                    sp.wait_ge(s["third"], 2 * nu * i + (ring + (k + 1) * nu - 2 * nu))
                    sp.dma_start(ws[:, k, :], slab[bass.ds(2 * i + k, 1)].rearrange("a p n -> p (a n)")
                                 ).then_inc(s_slab[k], 16)

        @block.tensor
        def _(pe):
            norm_tensor(chip, k_ln, chip.h)
            chip.need(pe, 3)
            for c in range(NCH):
                pe.wait_ge(chip.ln_out, NCH * k_ln + c + 1)
                nc.tensor.matmul(pa[0:64, c, 0:CH], chip.w("f2_rw1"), chunk(chip.xl, c), start=True, stop=True).then_inc(s["router"], 1)
            pe.wait_ge(s["router_sb"], NCH)
            for j in range(NT):
                last = nc.tensor.matmul(pc[0:TT, 1, e2 * j:e2 * j + e2], rh[:, TT * j:TT * j + TT],
                                        chip.w("f2_gate", rows=64), start=True, stop=True)
            last.then_inc(s["logits"], 1)
            pe.wait_ge(s["gates"], 1)
            for j in range(NT):
                last = nc.tensor.transpose(pb[0:k_rows, j // 3, TT * (j % 3):TT * (j % 3) + TT], r["tg"][:, j, :],
                                           chip.w("ident", rows=TT, cols=TT))
            last.then_inc(s["rows"], 1)
            pe.wait_ge(s["rows_sb"], 2)
            for c in range(NCH):
                nc.tensor.matmul(pa[:, c, 0:CH], chip.w("f2_b2", rows=k_rows), chunk(r["rows"], c),
                                 start=True, stop=False, skip_group_check=True)

            def first(i, n):
                k, c = divmod(n % (2 * nu), nu)
                i = i + n // (2 * nu)
                if c == 0:
                    pe.wait_ge(s_slab[k], 16 * i + 16)
                pe.wait_ge(s["act"], 2 * nu * i + (n % (2 * nu)) + 1)
                nc.tensor.matmul(pc[:, n % ring, 0:CH], ws[:, k, 0:128], chunk(chip.xl, c), start=True,
                                 stop=True).then_inc(s["first"], 1)

            def mid(i, n):
                k, c = divmod(n % (2 * nu), nu)
                i = i + n // (2 * nu)
                pe.wait_ge(s["gated"], 2 * nu * i + (n % (2 * nu)) + 1)
                nc.tensor.matmul(pb[:, 2, 0:CH], ws[0:k_rows, k, 386:450].bitcast(BF16), chunk(r["rows16"][0:k_rows], c),
                                 start=True, stop=True)
                pe.wait_ge(s["act"], 2 * nu * i + (n % (2 * nu)) + 1 + ring)
                nc.tensor.matmul(pb[:, n % ring, 0:CH], ws[:, k, 128:256], h1[:, n % ring, :], start=True,
                                 stop=True).then_inc(s["mid"], 1)

            def pair(i, last_pair):
                for n in range(2 * nu):
                    k, c = divmod(n, nu)
                    if not (last_pair and n + 2 >= 2 * nu):
                        first(i, n + 2)
                    pe.wait_ge(s["gated"], 2 * nu * i + n + 2)
                    if not (last_pair and n + 1 >= 2 * nu):
                        mid(i, n + 1)
                    nc.tensor.matmul(pa[:, c, 0:CH], ws[:, k, 256:384], hg[:, n % ring, :], start=False, stop=False,
                                     skip_group_check=True).then_inc(s["third"], 1)

            pe.sem_inc(s["mid"], ring)
            first(0, 0)
            first(0, 1)
            mid(0, 0)
            with pe.Fori(0, pairs - 1) as i:
                pair(i, False)
            pair(pairs - 1, True)

        @block.scalar
        def _(act):
            norm_scalar(chip, k_ln)
            for c in range(NCH):
                act.wait_ge(s["router"], c + 1)
                nc.scalar.activation(rh[:, c * CH:(c + 1) * CH], pa[0:64, c, 0:CH], ACT.Relu,
                                     bias=chip.w("f2_rb1", rows=64)).then_inc(s["router_sb"], 1)
            route_scalar(chip, r, "probs", s)
            act.sem_inc(s["act"], ring)
            with act.Fori(0, pairs) as i:
                for n in range(2 * nu):
                    k = n // nu
                    act.wait_ge(s["first"], 2 * nu * i + n + 1)
                    act.wait_ge(s["mid"], 2 * nu * i + n + 1)
                    nc.scalar.activation(h1[:, n % ring, :], pc[:, n % ring, 0:CH], ACT.Relu,
                                         bias=ws[:, k, 384:385]).then_inc(s["act"], 1)

        @block.vector
        def _(v):
            steps = Steps(s["step"])
            norm_vector(chip, k_ln, chip.h, chip.xl)
            chip.need(v, 3)
            route_vector(chip, steps, r, "probs", n_e, False, s)
            v.wait_ge(s["rows"], 1)
            nc.vector.tensor_copy(chunks(r["rows"][:, :]), pb[0:k_rows, :, 0:CH]).then_inc(s["rows_sb"], 1)
            nc.vector.tensor_copy(chunks(r["rows16"][0:k_rows]), pb[0:k_rows, :, 0:CH]).then_inc(s["rows_sb"], 1)
            v.sem_inc(s["gated"], 1)
            v.sem_inc(s["third"], ring)
            with v.Fori(0, pairs) as i:
                for n in range(2 * nu):
                    k = n // nu
                    v.wait_ge(s["mid"], 2 * nu * i + n + 1 + ring)
                    nc.vector.tensor_scalar(h2[:, n % ring, :], pb[:, n % ring, 0:CH], ws[:, k, 385:386], 0.0,
                                            ALU.add, ALU.max).then_inc(s["mid_act"], 1)
                    v.wait_ge(s["mid_act"], 2 * nu * i + n + 1)
                    v.wait_ge(s["third"], 2 * nu * i + n + 1)
                    nc.vector.tensor_tensor(hg[:, n % ring, :], h2[:, n % ring, :], pb[:, 2, 0:CH],
                                            ALU.mult).then_inc(s["gated"], 1)
            v.wait_ge(s["third"], n_e * nu + ring)
            nc.vector.tensor_tensor(chunks(chip.h[:, :]), chunks(chip.h[:, :]), pa[:, :, 0:CH], ALU.add).then_inc(s["done"], 1)


def mamba(chip, selbc):
    nc = chip.nc
    k_ln, k_ln1, k_ln2 = chip.next_norm(), chip.next_norm(), chip.next_norm()
    n_s = 16
    with ExitStack() as ctx:
        def sb(name, shape, dt=F32):
            return ctx.enter_context(nc.sbuf_tensor(name, shape, dt))
        sel = sb("a3sel", [128, n_s * 2 * 128], BF16)
        xs = sb("a3xs", [128, NB, 3 + TP])
        xc, z, dt, u = (sb("a3" + n, [128, NB, TP]) for n in ("xc", "z", "dt", "u"))
        t1 = sb("a3t1", [128, NB, TP])
        dbl = sb("a3dbl", [48, NB, TP])
        rem = sb("a3rem", [32, NB, TP])
        low = sb("a3low", [32, NB, TP], BF16)
        bcp = sb("a3bcp", [128, NB, TP], BF16)
        an, ddp = sb("a3an", [128, n_s]), sb("a3ddp", [128, 128])
        da, hst, cs, pr = (sb("a3" + n, [128, 2, TP]) for n in ("da", "hst", "cs", "pr"))
        dbx = sb("a3dbx", [128, 2, TP])
        m1 = sb("a3m1", [P, TP])
        r1, n1 = sb("a3r1", [P, TP]), sb("a3n1", [P, TP])
        names = ("sel_loaded", "xs", "xs_sb", "z", "z_sb", "conv", "xc", "dbl", "dbl_sb", "dt", "abs", "exp", "log",
                 "dt_pos", "dt_done", "parts", "aexp", "a", "dp", "u", "b_spread", "c_spread", "da", "dbx", "scan",
                 "c_sb", "prod", "summed", "start", "yo", "wout", "wout_sb", "wlin", "r1", "n1", "up", "up_sb",
                 "down", "r2", "n2", "h", "step")
        s = {x: chip.stage_sem("a3_" + x) for x in names}
        block = ctx.enter_context(nc.Block())
        pa, pb, pc = chip.pa, chip.pb, chip.pc
        bank = [pa, pb]
        bc = [(b, c) for b in range(NB) for c in range(NCH)]

        @block.sync
        def _(sp):
            sp.dma_start(sel[:, :], selbc.bitcast(BF16)).then_inc(s["sel_loaded"], 16)

        @block.tensor
        def _(pe):
            norm_tensor(chip, k_ln, chip.h)
            chip.need(pe, 4)
            pe.wait_ge(chip.ln_out, NCH * (k_ln + 1))
            for b, c in bc:
                nc.tensor.matmul(bank[b][:, c, 0:CH], chip.w("a3_win", first=128 * b, cols=128), chunk(chip.xl, c),
                                 start=True, stop=True).then_inc(s["xs"], 1)
            for n, (b, c) in enumerate(bc):
                pe.wait_ge(s["xs_sb"], n + 1)
                nc.tensor.matmul(bank[b][:, c, 0:CH], chip.w("a3_win", first=256 + 128 * b, cols=128),
                                 chunk(chip.xl, c), start=True, stop=True).then_inc(s["z"], 1)
            for n, (b, c) in enumerate(bc):
                pe.wait_ge(s["z_sb"], n + 1)
                pe.wait_ge(s["xc"], b + 1)
                nc.tensor.matmul(bank[b][0:48, c, 0:CH], chip.w("a3_wx"), chunk(xc[:, b], c), start=True,
                                 stop=True).then_inc(s["dbl"], 1)
            for n, (b, c) in enumerate(bc):
                pe.wait_ge(s["dbl_sb"], n + 1)
                nc.tensor.matmul(bank[b][:, c, 0:CH], chip.w("a3_wdt", rows=48), chunk(dbl[:, b], c), start=True,
                                 stop=True).then_inc(s["dt"], 1)
            pe.wait_ge(s["sel_loaded"], 16)
            pe.wait_ge(s["parts"], 2)
            pe.wait_ge(s["dp"], 1)
            pe.wait_ge(s["dt_pos"], NB)
            pe.wait_ge(s["abs"], NB)

            def spread(b, i, k):
                g = n_s * b + k
                pe.wait_ge(s["dbx"], 2 * i + g + 1)
                for c in range(NCH):
                    last = nc.tensor.matmul(pb[:, c, 0:CH], sel[:, bass.ds(i * 512 + 256 * k, 128)],
                                            chunk(bcp[:, b], c), start=True, stop=True)
                last.then_inc(s["b_spread"], 1)
                for c in range(NCH):
                    pe.wait_ge(s["c_sb"], 6 * i + 3 * g + c + 1)
                    nc.tensor.matmul(pc[:, (3 * k + c) % 2, 0:CH], sel[:, bass.ds(i * 512 + 256 * k + 128, 128)],
                                     chunk(bcp[:, b], c), start=True, stop=True).then_inc(s["c_spread"], 1)

            def add_up(b, i, k):
                pe.wait_ge(s["prod"], 2 * i + n_s * b + k + 1 + 2)
                for c in range(NCH):
                    last = nc.tensor.matmul(pa[:, c, 0:CH], chip.w("ident"), chunk(pr[:, k], c), start=False,
                                            stop=False, skip_group_check=True)
                last.then_inc(s["summed"], 1)

            for b in range(NB):
                spread(b, 0, 0)
                if b:
                    pe.wait_ge(s["yo"], b)
                for c in range(NCH):
                    nc.tensor.matmul(pa[:, c, 0:CH], ddp[:, :], chunk(xc[:, b], c), start=True, stop=False,
                                     skip_group_check=True)
                with pe.Fori(0, n_s // 2 - 1) as i:
                    spread(b, i, 1)
                    add_up(b, i, 0)
                    spread(b, i + 1, 0)
                    add_up(b, i, 1)
                i = n_s // 2 - 1
                spread(b, i, 1)
                add_up(b, i, 0)
                add_up(b, i, 1)

            for b, c in bc:
                pe.wait_ge(s["yo"], b + 1)
                nc.tensor.matmul(pb[64 * b:64 * b + 64, c, 0:CH], chip.w("a3_wout"), chunk(u[:, b], c),
                                 start=True, stop=True).then_inc(s["wout"], 1)
            for c in range(NCH):
                pe.wait_ge(s["wout_sb"], c + 1)
                nc.tensor.matmul(pa[:, c, 0:CH], chip.w("a3_wlin"), chunk(m1, c), start=True, stop=True).then_inc(s["wlin"], 1)
            norm_tensor(chip, k_ln1, r1, s["r1"])
            for b, c in bc:
                pe.wait_ge(s["n1"], NCH)
                nc.tensor.matmul(bank[b][:, c, 0:CH], chip.w("a3_wexp", first=128 * b, cols=128), chunk(n1, c),
                                 start=True, stop=True).then_inc(s["up"], 1)
            for b, c in bc:
                pe.wait_ge(s["up_sb"], 2 * NCH)
                nc.tensor.matmul(pa[64 * b:64 * b + 64, c, 0:CH], chip.w("a3_wsq"), chunk(t1[:, b], c),
                                 start=True, stop=True).then_inc(s["down"], 1)
            norm_tensor(chip, k_ln2, r1, s["r2"])

        @block.scalar
        def _(act):
            norm_scalar(chip, k_ln)
            chip.need(act, 4)
            nc.scalar.activation(an[:, :], chip.w("a3_alog"), ACT.Exp).then_inc(s["aexp"], 1)
            for n, (b, c) in enumerate(bc):
                act.wait_ge(s["xs"], n + 1)
                nc.scalar.activation(xs[:, b, 3 + c * CH:3 + (c + 1) * CH], bank[b][:, c, 0:CH], ACT.Copy
                                     ).then_inc(s["xs_sb"], 1)
            for n, (b, c) in enumerate(bc):
                act.wait_ge(s["z"], n + 1)
                nc.scalar.activation(chunk(z[:, b], c), bank[b][:, c, 0:CH], ACT.Silu).then_inc(s["z_sb"], 1)
            for b in range(NB):
                act.wait_ge(s["conv"], b + 1)
                nc.scalar.activation(xc[:, b], xc[:, b], ACT.Silu).then_inc(s["xc"], 1)
            for n, (b, c) in enumerate(bc):
                act.wait_ge(s["dbl"], n + 1)
                nc.scalar.activation(chunk(dbl[:, b], c), bank[b][0:48, c, 0:CH], ACT.Copy).then_inc(s["dbl_sb"], 1)
            for b in range(NB):
                act.wait_ge(s["dt"], NCH * (b + 1))
                nc.scalar.activation(chunks(t1[:, b]), bank[b][:, :, 0:CH], ACT.Abs, bias=chip.w("a3_bdt")).then_inc(s["abs"], 1)
            for b in range(NB):
                act.wait_ge(s["abs"], b + 1)
                nc.scalar.activation(t1[:, b], t1[:, b], ACT.Exp, scale=-1.0).then_inc(s["exp"], 1)
            for b in range(NB):
                act.wait_ge(s["exp"], b + 1)
                nc.scalar.activation(da[:, b], t1[:, b], ACT.Ln, bias=chip.w("eps", first=2, cols=1)).then_inc(s["log"], 1)
            act.wait_ge(s["a"], 1)
            act.wait_ge(s["dt_done"], NB)
            act.sem_inc(s["c_sb"], 2)
            for b in range(NB):
                with act.Fori(0, n_s // 2) as i:
                    for k in range(2):
                        g = n_s * b + k
                        act.wait_ge(s["scan"], 2 * i + g + 1)
                        nc.scalar.activation(da[:, k], dt[:, b], ACT.Exp, scale=an[:, bass.ds(2 * i + k, 1)]
                                             ).then_inc(s["da"], 1)
                        act.wait_ge(s["prod"], 2 * i + g + 1)
                        for c in range(NCH):
                            act.wait_ge(s["c_spread"], 6 * i + 3 * g + c + 1)
                            nc.scalar.activation(chunk(cs[:, k], c), pc[:, (3 * k + c) % 2, 0:CH], ACT.Copy
                                                 ).then_inc(s["c_sb"], 1)
            for c in range(NCH):
                act.wait_ge(s["wout"], NCH + c + 1)
                nc.scalar.activation(chunk(m1, c), pb[:, c, 0:CH], ACT.Copy).then_inc(s["wout_sb"], 1)
            norm_scalar(chip, k_ln1)
            for n, (b, c) in enumerate(bc):
                act.wait_ge(s["up"], n + 1)
                nc.scalar.activation(chunk(t1[:, b], c), bank[b][:, c, 0:CH], ACT.Relu, bias=chip.w("a3_bexp")
                                     ).then_inc(s["up_sb"], 1)
            norm_scalar(chip, k_ln2)

        @block.gpsimd
        def _(pool):
            pool.sem_inc(s["prod"], 2)
            for b in range(NB):
                with pool.Fori(0, n_s // 2) as i:
                    for k in range(2):
                        g = n_s * b + k
                        pool.wait_ge(s["scan"], 2 * i + g + 1 + 2)
                        pool.wait_ge(s["c_sb"], 6 * i + 3 * g + 3 + 2)
                        pool.wait_ge(s["summed"], 2 * i + g + 1)
                        nc.gpsimd.tensor_tensor(pr[:, k], hst[:, k], cs[:, k], ALU.mult).then_inc(s["prod"], 1)

        @block.vector
        def _(v):
            steps = Steps(s["step"])
            steps.settle(v, nc.vector.memset(xs[:, :, 0:3], 0.0))
            nc.vector.memset(bcp[96:128], 0.0).then_inc(s["parts"], 1)
            norm_vector(chip, k_ln, chip.h, chip.xl)
            chip.need(v, 4)
            nc.vector.tensor_scalar(ddp[:, :], chip.w("ident"), chip.w("a3_dp"), None, ALU.mult).then_inc(s["dp"], 1)
            v.wait_ge(s["aexp"], 1)
            nc.vector.tensor_scalar(an[:, :], an[:, :], -1.0, None, ALU.mult).then_inc(s["a"], 1)
            for b in range(NB):
                v.wait_ge(s["xs_sb"], NCH * (b + 1))
                steps.settle(v, nc.vector.tensor_scalar(xc[:, b], xs[:, b, 0:TP], chip.w("a3_convw", cols=1),
                                                        chip.w("a3_convb"), ALU.mult, ALU.add))
                for k in range(1, 4):
                    i = nc.vector.scalar_tensor_tensor(xc[:, b], xs[:, b, k:k + TP], chip.w("a3_convw", first=k, cols=1),
                                                       xc[:, b], ALU.mult, ALU.add)
                    if k < 3:
                        steps.settle(v, i)
                    else:
                        i.then_inc(s["conv"], 1)
            v.wait_ge(s["dbl_sb"], 2 * NCH)
            steps.settle(v, nc.vector.tensor_copy(bcp[0:32], dbl[0:32]))
            steps.settle(v, nc.vector.tensor_tensor(rem[:, :, :], dbl[0:32], bcp[0:32], ALU.subtract))
            steps.settle(v, nc.vector.tensor_copy(low[:, :, :], rem[:, :, :]))
            steps.settle(v, nc.vector.tensor_copy(bcp[32:64], low[:, :, :]))
            steps.settle(v, nc.vector.tensor_tensor(rem[:, :, :], rem[:, :, :], low[:, :, :], ALU.subtract))
            nc.vector.tensor_copy(bcp[64:96], rem[:, :, :]).then_inc(s["parts"], 1)
            for b in range(NB):
                v.wait_ge(s["abs"], b + 1)
                nc.vector.tensor_scalar(chunks(dt[:, b]), bank[b][:, :, 0:CH], chip.w("a3_bdt"), 0.0, ALU.add, ALU.max
                                        ).then_inc(s["dt_pos"], 1)
            for b in range(NB):
                e, ser, small = t1[:, b], hst[:, b], cs[:, b].bitcast(mybir.dt.uint32)
                v.wait_ge(s["exp"], b + 1)
                steps.settle(v, nc.vector.tensor_scalar(ser, e, -0.25, 1.0 / 3.0, ALU.mult, ALU.add))
                steps.settle(v, nc.vector.tensor_tensor(ser, ser, e, ALU.mult))
                for coefficient in (-0.5, 1.0):
                    steps.settle(v, nc.vector.scalar_tensor_tensor(ser, ser, coefficient, e, ALU.add, ALU.mult))
                steps.settle(v, nc.vector.tensor_scalar(small, e, SERIES_BELOW, None, ALU.is_lt))
                v.wait_ge(s["log"], b + 1)
                steps.settle(v, nc.vector.copy_predicated(da[:, b], small, ser))
                v.wait_ge(s["dt_pos"], b + 1)
                nc.vector.tensor_tensor(dt[:, b], dt[:, b], da[:, b], ALU.add).then_inc(s["dt_done"], 1)
                v.wait_ge(s["dt_done"], b + 1)
                steps.settle(v, nc.vector.tensor_tensor(u[:, b], dt[:, b], xc[:, b], ALU.mult))
            v.sem_inc(s["scan"], 2)
            v.sem_inc(s["summed"], 2)
            v.sem_inc(s["dbx"], 1)
            for b in range(NB):
                with v.Fori(0, n_s // 2) as i:
                    for k in range(2):
                        g = n_s * b + k
                        v.wait_ge(s["b_spread"], 2 * i + g + 1)
                        v.wait_ge(s["scan"], 2 * i + g + 1)
                        nc.vector.tensor_tensor(chunks(dbx[:, k]), chunks(u[:, b]), pb[:, :, 0:CH], ALU.mult
                                                ).then_inc(s["dbx"], 1)
                        v.wait_ge(s["dbx"], 2 * i + g + 2)
                        v.wait_ge(s["da"], 2 * i + g + 1)
                        v.wait_ge(s["prod"], 2 * i + g + 1)
                        nc.vector.tensor_tensor_scan(hst[:, k], da[:, k], dbx[:, k], 0.0, ALU.mult, ALU.add
                                                     ).then_inc(s["scan"], 1)
                v.wait_ge(s["summed"], n_s * (b + 1) + 2)
                nc.vector.tensor_tensor(chunks(u[:, b]), pa[:, :, 0:CH], chunks(z[:, b]), ALU.mult).then_inc(s["yo"], 1)

            for c in range(NCH):
                v.wait_ge(s["wlin"], c + 1)
                nc.vector.scalar_tensor_tensor(chunk(r1, c), pa[:, c, 0:CH], chip.w("a3_blin"), chunk(chip.xl, c),
                                               ALU.add, ALU.add).then_inc(s["r1"], 1)
            norm_vector(chip, k_ln1, r1, n1)
            for c in range(NCH):
                v.wait_ge(chip.ln_out, NCH * k_ln1 + c + 1)
                nc.vector.tensor_scalar(chunk(n1, c), chunk(n1, c), chip.w("a3_g1"), chip.w("a3_b1"), ALU.mult, ALU.add
                                        ).then_inc(s["n1"], 1)
            for c in range(NCH):
                v.wait_ge(s["down"], NCH + c + 1)
                nc.vector.scalar_tensor_tensor(chunk(r1, c), pa[:, c, 0:CH], chip.w("a3_bsq"), chunk(n1, c),
                                               ALU.add, ALU.add).then_inc(s["r2"], 1)
            norm_vector(chip, k_ln2, r1, n1)
            for c in range(NCH):
                v.wait_ge(chip.ln_out, NCH * k_ln2 + c + 1)
                steps.settle(v, nc.vector.tensor_scalar(chunk(n1, c), chunk(n1, c), chip.w("a3_g2"), chip.w("a3_b2"),
                                                        ALU.mult, ALU.add))
                nc.vector.tensor_tensor(chunk(chip.h, c), chunk(chip.h, c), chunk(n1, c), ALU.add).then_inc(s["h"], 1)


def build(nc, t, out):
    with ExitStack() as ctx:
        chip = Chip(nc, ctx)
        work = [
            lambda: tokenise(chip, t["x"], t["xedge"], t["tokw"], t["cls2"], t["small"]),
            lambda: linear_attention(chip),
            lambda: experts2(chip, "f0", t["f0_slab"], 1, 8, 2, ACT.Relu, "switch"),
            lambda: row_attention(chip),
            lambda: experts2(chip, "f1", t["f1_slab"], 1, 8, 1, ACT.Gelu, "mask"),
            lambda: scan_attention(chip),
            lambda: experts3(chip, t["f2_slab"]),
            lambda: mamba(chip, t["selbc"]),
            lambda: experts2(chip, "f3", t["f3_slab"], 4, 8, 1, ACT.Relu, "logits"),
        ]
        for stage in work:
            stage()
            chip.end_stage()
        s_out = chip.sem("out_written")
        with nc.Block() as block:
            @block.sync
            def _(sp):
                sp.dma_start(out, chip.h[:, 0:NTOK]).then_inc(s_out, 16)
                sp.wait_ge(s_out, 16)



def pack(i):
    import numpy as np
    f = np.float32
    small = np.zeros((128, NSMALL), f)

    def put(name, a, row0=0):
        at, n = COL[name]
        a = np.asarray(a)
        if a.ndim == 1:
            a = a[:, None]
        assert a.shape[1] == n, (name, a.shape)
        small[row0:row0 + a.shape[0], at:at + n] = a

    def bd(w):
        w = np.asarray(w)
        z = np.zeros((2 * w.shape[0], 2 * w.shape[1]), f)
        z[:w.shape[0], :w.shape[1]] = w
        z[w.shape[0]:, w.shape[1]:] = w
        return z

    def two(v):
        return np.concatenate([np.asarray(v), np.asarray(v)])

    def one_seq(w):
        w = np.asarray(w)
        return bd(w)

    def rep(v):
        return np.tile(two(v)[None, :], (128, 1))

    k, p = np.arange(9)[:, None], np.arange(16)[None, :]
    ang = 2 * np.pi * k * p / 16
    dft = np.concatenate([np.cos(ang), -np.sin(ang)], 0) / 4
    dft = dft.reshape(18, 2, 2, 4).transpose(0, 2, 1, 3).reshape(18, 16)
    put("dft", dft.astype(f))
    put("mean", bd(np.full((64, 64), 1 / 64, f)))
    put("eps", np.tile(np.array([[EPS, EPS * EPS, 1.0]], f), (128, 1)))
    put("ident", np.eye(128, dtype=f))
    wqkv = i["L0_attn_Wqkv"]
    put("a0_wq", bd(wqkv[:, 0:64]))
    put("a0_wk", bd(wqkv[:, 64:128]))
    put("a0_wv", bd(wqkv[:, 128:192]))
    put("a0_wproj", bd(i["L0_attn_Wproj"]))
    put("a0_wg1", bd(i["L0_attn_Wg1"]))
    put("a0_wg2", bd(i["L0_attn_Wg2"]))
    put("a0_mask", np.kron(np.eye(16), np.ones((8, 8))).astype(f))
    put("a0_g", two(i["L0_attn_ln_g"]))
    put("a0_b", two(i["L0_attn_ln_b"]))
    put("a0_bproj", two(i["L0_attn_bproj"]))
    put("a0_bg1", two(i["L0_attn_bg1"]))
    put("a0_bg2", two(i["L0_attn_bg2"]))

    def diag(v):
        return two(np.asarray(v).reshape(-1))

    def parts(b2, n):
        return np.concatenate([bd(b2)] * n, 0)

    put("f0_gate", bd(i["L0_ffn_gate_w"]))
    put("f0_gbias", rep(i["L0_ffn_gate_b"]))
    put("f0_b2", parts(i["L0_ffn_b2"], 1))
    sel = np.zeros((2, 128), f)
    sel[0, :64] = 1
    sel[1, 64:] = 1
    put("seqsel", sel, row0=32)
    put("rev8", rep(8 - np.arange(8, dtype=f)))
    put("rev6", rep(6 - np.arange(6, dtype=f)))
    shift = np.zeros((16, 16), f)
    shift[np.arange(8), 8 + np.arange(8)] = 1
    put("shift", shift)

    def dup(w):
        return np.concatenate([np.asarray(w)] * 2, 0)

    put("a1_g", diag(i["L1_attn_gamma"]))
    put("a1_b", diag(i["L1_attn_beta"]))
    put("a1_wq", dup(i["L1_attn_Wq"]))
    put("a1_wk", dup(i["L1_attn_Wk"]))
    put("a1_wv", dup(i["L1_attn_Wv"]))
    put("a1_wg", one_seq(i["L1_attn_Wg"]))
    put("a1_bg", np.asarray(i["L1_attn_bg"]).reshape(2, 128).T)
    put("a1_wo", np.asarray(i["L1_attn_Wo"]).reshape(2, 128, 64).transpose(1, 0, 2).reshape(128, 128))
    put("a1_bo", diag(i["L1_attn_bo"]))
    ones = np.ones((64, 64), f)
    put("tdiff", np.block([[ones, -ones], [-ones, ones]]))
    put("f1_gate", bd(i["L1_ffn_Wg"]))
    put("f1_gbias", rep(i["L1_ffn_bg"]))
    put("f1_b2", parts(i["L1_ffn_b2"], 1))

    inw = np.asarray(i["L2_attn_in_w"])
    put("a2_wxp", bd(inw[:64].T))
    put("a2_wres", bd(inw[64:].T))
    put("a2_bxp", diag(i["L2_attn_in_b"][:64]))
    put("a2_bres", diag(i["L2_attn_in_b"][64:]))
    put("a2_convw", dup(np.asarray(i["L2_attn_conv_w"]).reshape(64, 4)))
    put("a2_convb", diag(i["L2_attn_conv_b"]))
    put("a2_dt", bd(i["L2_attn_dt"]))
    put("a2_bw", bd(np.asarray(i["L2_attn_B_w"]).T))
    put("a2_cw", bd(np.asarray(i["L2_attn_C_w"]).T))
    put("a2_ow", bd(np.asarray(i["L2_attn_out_w"]).T))
    put("a2_ob", diag(i["L2_attn_out_b"]))
    put("a2_g", diag(i["L2_attn_gamma"]))
    put("a2_b", diag(i["L2_attn_beta"]))
    put("chmean", (np.tile(np.eye(64), (2, 2)) / (NB * NTOK)).astype(f))
    put("f2_rw1", bd(i["L2_ffn_router_w1"]))
    put("f2_rb1", diag(i["L2_ffn_router_b1"]))
    put("f2_gate", bd(i["L2_ffn_router_w2"]))
    put("f2_gbias", rep(i["L2_ffn_router_b2"]))
    put("f2_b2", parts(i["L2_ffn_expert_b3"], 3))

    win = np.asarray(i["L3_attn_W_in"])
    put("a3_win", np.concatenate([one_seq(win[:128].T), one_seq(win[128:].T)], 1))
    put("a3_convw", i["L3_attn_conv_w"])
    put("a3_convb", i["L3_attn_conv_b"])
    wx = np.asarray(i["L3_attn_W_x"])
    put("a3_wx", np.concatenate([wx[16:48], wx[:16]], 0).T)
    put("a3_wdt", np.asarray(i["L3_attn_W_dt"]).T, row0=32)
    put("a3_bdt", i["L3_attn_b_dt"])
    put("a3_alog", i["L3_attn_A_log"])
    put("a3_dp", i["L3_attn_Dp"])
    put("a3_wout", np.asarray(i["L3_attn_W_out"]).T)
    put("a3_wlin", bd(np.asarray(i["L3_attn_W_lin"]).T))
    put("a3_blin", diag(i["L3_attn_b_lin"]))
    put("a3_g1", diag(i["L3_attn_ln1_g"]))
    put("a3_b1", diag(i["L3_attn_ln1_b"]))
    put("a3_wexp", one_seq(np.asarray(i["L3_attn_W_exp"]).T))
    put("a3_bexp", i["L3_attn_b_exp"])
    put("a3_wsq", np.asarray(i["L3_attn_W_sq"]).T)
    put("a3_bsq", diag(i["L3_attn_b_sq"]))
    put("a3_g2", diag(i["L3_attn_ln2_g"]))
    put("a3_b2", diag(i["L3_attn_ln2_b"]))
    put("f3_gate", bd(i["L3_ffn_Wg"]))
    put("f3_gbias", rep(i["L3_ffn_bg"]))
    put("f3_gbias2", rep(i["L3_ffn_bias"]))
    put("f3_b2", parts(i["L3_ffn_b2"], 3))

    def bf16_bits(ones_at):
        u = np.zeros(ones_at.shape, np.uint16)
        u[ones_at] = 0x3F80
        return u.view(f)

    def slabs2(w1, b1, w2, n_parts):
        w1, b1, w2 = np.asarray(w1), np.asarray(b1), np.asarray(w2)
        e_n, _, hid = w1.shape
        hc = hid // 128
        out = np.zeros((e_n, 128, SLAB2[hc]), f)
        for e in range(e_n):
            for b in range(2):
                out[e, 64 * b:64 * b + 64, hid * b:hid * b + hid] = w1[e]
                at = np.zeros((128, 128), bool)
                for part in range(n_parts):
                    at[part * 2 * e_n + b * e_n + e] = True
                n = 2 * hid + 65 * hc + 64 * b
                out[e, :, n:n + 64] = bf16_bits(at)
            out[e, :, 2 * hid:2 * hid + 64 * hc] = w2[e].reshape(hc, 128, 64).transpose(1, 0, 2).reshape(128, -1)
            out[e, :, 2 * hid + 64 * hc:2 * hid + 65 * hc] = b1[e].reshape(hc, 128).T
        return out

    def slabs3(w1, b1, w2, b2, w3):
        e_n = w1.shape[0]
        out = np.zeros((e_n, 128, SLAB3), f)
        for e in range(e_n):
            for n, w in enumerate((w1, w2, w3)):
                out[e, :, 128 * n:128 * n + 128] = bd(w[e])
            out[e, :, 384] = diag(b1[e])
            out[e, :, 385] = diag(b2[e])
            at = np.zeros((128, 128), bool)
            for part in range(3):
                for b in range(2):
                    at[part * 2 * e_n + b * e_n + e, 64 * b:64 * b + 64] = True
            out[e, :, 386:450] = bf16_bits(at)
        return out

    def sel_bc():
        at = np.zeros((128, 16, 2, 128), bool)
        for s in range(16):
            for part in range(3):
                at[32 * part + s, s, 0] = True
                at[32 * part + 16 + s, s, 1] = True
        return bf16_bits(at.reshape(128, -1))

    x = np.asarray(i["x"]).reshape(2, 64, 16, 2, 4, 64).transpose(3, 1, 0, 2, 4, 5)
    edge = x[1, :, :, 15, 3, :]
    return {
        "x": x.reshape(128, 2, 16, 4, 64),
        "xedge": np.concatenate([edge, edge], 0),
        "tokw": np.asarray(i["L0_tok_W"]).reshape(64, 18, 64).transpose(1, 0, 2),
        "cls2": two(np.asarray(i["cls_tok"]).reshape(64))[:, None],
        "small": small,
        "f0_slab": slabs2(i["L0_ffn_w1"], i["L0_ffn_b1"], i["L0_ffn_w2"], 1),
        "f1_slab": slabs2(i["L1_ffn_W1"], i["L1_ffn_b1"], i["L1_ffn_W2"], 1),
        "f2_slab": slabs3(i["L2_ffn_expert_w1"], i["L2_ffn_expert_b1"], i["L2_ffn_expert_w2"],
                          i["L2_ffn_expert_b2"], i["L2_ffn_expert_w3"]),
        "f3_slab": slabs2(i["L3_ffn_W1"], i["L3_ffn_b1"], i["L3_ffn_W2"], 3),
        "selbc": sel_bc(),
    }


def kernel(**inputs):
    import numpy as np
    import concourse.bacc as bacc
    from concourse.bass_utils import run_bass_kernel_spmd

    nc = bacc.Bacc("TRN2", target_bir_lowering=False, num_devices=1)
    arrays, t = {}, {}
    for name, a in pack(inputs).items():
        a = np.ascontiguousarray(a)
        arrays[name + "_dram"] = a
        t[name] = nc.dram_tensor(name + "_dram", a.shape, mybir.dt.from_np(a.dtype), kind="ExternalInput").ap()
    out = nc.dram_tensor("out_dram", (P, NTOK), F32, kind="ExternalOutput").ap()
    build(nc, t, out)
    got = run_bass_kernel_spmd(nc, [arrays], core_ids=[0]).results[0]["out_dram"]
    return np.ascontiguousarray(got.reshape(NB, D, NTOK).transpose(0, 2, 1))
```

```python
import concourse.bass as bass
from concourse import mybir
from contextlib import ExitStack

F32 = mybir.dt.float32
BF16 = mybir.dt.bfloat16
F32R = mybir.dt.float32r
ALU = mybir.AluOpType
ACT = mybir.ActivationFunctionType
AX = mybir.AxisListType

NB = 2
D = 64
P = NB * D
NTOK = 1025
NCH, CH = 3, 342
TP = NCH * CH
NT, TT = 9, 114
NV, NN = 64, 16
CAPACITY = 321
EPS = 1e-5
LAST = NTOK - (NCH - 1) * CH
SERIES_BELOW = 2.0 ** -6
FLT_MAX = 3.4028234663852886e38

GROUPS = [
    [("dft", 16), ("mean", 128), ("centre", 128), ("eps", 3), ("ident", 128)],
    [("a0_wk", 128), ("a0_wq", 128), ("a0_wv", 128), ("a0_wproj", 128), ("a0_wg1", 32), ("a0_wg2", 128),
     ("a0_mask", 128), ("a0_g", 1), ("a0_b", 1), ("a0_bproj", 1), ("a0_bg1", 1), ("a0_bg2", 1),
     ("f0_gate", 16), ("f0_gbias", 16), ("f0_b2", 128), ("seqsel", 128), ("rev8", 16), ("rev6", 12), ("shift", 16)],
    [("a1_g", 1), ("a1_b", 1), ("a1_wq", 256), ("a1_wk", 256), ("a1_wv", 256), ("a1_wg", 512), ("a1_bg", 2),
     ("a1_wo", 128), ("a1_bo", 1), ("tdiff", 128), ("f1_gate", 16), ("f1_gbias", 16), ("f1_b2", 128)],
    [("a2_wxp", 128), ("a2_wres", 128), ("a2_bxp", 1), ("a2_bres", 1), ("a2_convw", 4), ("a2_convb", 1),
     ("a2_dt", 32), ("a2_bw", 32), ("a2_cw", 128), ("a2_ow", 128), ("a2_ob", 1), ("a2_g", 1), ("a2_b", 1),
     ("chmean", 128), ("f2_rw1", 64), ("f2_rb1", 1), ("f2_gate", 12), ("f2_gbias", 12), ("f2_b2", 128)],
    [("a3_win", 512), ("a3_convw", 4), ("a3_convb", 1), ("a3_wx", 48), ("a3_wdt", 128), ("a3_bdt", 1),
     ("a3_alog", 16), ("a3_dp", 1), ("a3_wout", 64), ("a3_wlin", 128), ("a3_blin", 1), ("a3_g1", 1),
     ("a3_b1", 1), ("a3_wexp", 256), ("a3_bexp", 1), ("a3_wsq", 64), ("a3_bsq", 1), ("a3_g2", 1),
     ("a3_b2", 1), ("f3_gate", 16), ("f3_gbias", 16), ("f3_gbias2", 16)],
]
COL, GROUP_SPAN = {}, []
_at = 0
for _g in GROUPS:
    _from = _at
    for _name, _n in _g:
        COL[_name] = (_at, _n)
        _at += _n
    GROUP_SPAN.append((_from, _at))
NSMALL = _at

SLAB2 = {1: 128 + 64 + 1 + 1 + 128, 2: 256 + 2 * 64 + 2 + 1 + 128}
SLAB3 = 3 * 128 + 2 + 64


class Steps:

    def __init__(self, sem):
        self.sem = sem
        self.n = 0

    def mark(self, instruction):
        self.n += 1
        instruction.then_inc(self.sem, 1)
        return self.n

    def settle(self, engine, instruction):
        engine.wait_ge(self.sem, self.mark(instruction))


class Chip:

    def __init__(self, nc, ctx):
        self.nc, self.ctx = nc, ctx

        def sb(name, shape, dt=F32):
            return ctx.enter_context(nc.sbuf_tensor(name, shape, dt))

        self.small = sb("small", [128, NSMALL])
        self.h = sb("h", [P, TP])
        self.xl = sb("xl", [P, TP])
        self.sq = sb("sq", [P, TP])
        self.rs = sb("rs", [P, TP])
        self.psum = ctx.enter_context(nc.psum_tensor("psum", [128, 8, 512], F32))
        self.pa, self.pb, self.pc = self.psum[:, 0:3], self.psum[:, 3:6], self.psum[:, 6:8]
        self.small_loaded = [self.sem(f"small_loaded{g}") for g in range(len(GROUPS))]
        self.ln_centred, self.ln_square, self.ln_var = self.sem("ln_centred"), self.sem("ln_square"), self.sem("ln_var")
        self.ln_log, self.ln_rstd, self.ln_out = self.sem("ln_log"), self.sem("ln_rstd"), self.sem("ln_out")
        self.norms = 0
        self.stage_sems, self.cleared = [], []

    def sem(self, name):
        return self.nc.alloc_semaphore(name)

    def stage_sem(self, name):
        s = self.nc.alloc_semaphore(name)
        self.stage_sems.append(s)
        return s

    def end_stage(self):
        for s in self.cleared:
            self.nc.release_semaphore(s)
        for s in self.stage_sems:
            self.nc.gpsimd.sem_clear(s)
        self.cleared, self.stage_sems = self.stage_sems, []

    def next_norm(self):
        self.norms += 1
        return self.norms - 1

    def w(self, name, rows=128, first=0, cols=None, row0=0):
        at, n = COL[name]
        return self.small[row0:row0 + rows, at + first:at + first + (n - first if cols is None else cols)]

    def need(self, engine, group):
        engine.wait_ge(self.small_loaded[group], 16)


def chunk(t, c):
    return t[:, c * CH:(c + 1) * CH]


def chunks(t):
    return t.rearrange("p (c n) -> p c n", n=CH)



def norm_tensor(chip, k, src, ready=None):
    nc, pe = chip.nc, chip.nc.tensor
    for c in range(NCH):
        if ready is not None:
            pe.wait_ge(ready, c + 1)
        nc.tensor.matmul(chip.pa[:, c, 0:CH], chip.w("centre"), chunk(src, c),
                         start=True, stop=True).then_inc(chip.ln_centred, 1)
    for c in range(NCH):
        pe.wait_ge(chip.ln_square, NCH * k + c + 1)
        nc.tensor.matmul(chip.pb[:, c, 0:CH], chip.w("mean"), chunk(chip.sq, c),
                         start=True, stop=True).then_inc(chip.ln_var, 1)


def norm_vector(chip, k, out, then=None):
    nc, v = chip.nc, chip.nc.vector
    for c in range(NCH):
        v.wait_ge(chip.ln_rstd, NCH * k + c + 1)
        nc.vector.tensor_tensor(chunk(out, c), chip.pa[:, c, 0:CH], chunk(chip.rs, c),
                                ALU.mult).then_inc(chip.ln_out, 1)
        if then is not None:
            then(c)


EXP_LN, GELU = 6, 10


def load_functions(nc, table_set):
    nc.scalar.add_instruction(mybir.InstLoadActFuncSet(
        act_func_set_id=table_set, name=nc.get_next_instruction_name(), engine=mybir.EngineType.Activation))


def norm_scalar(chip, k, twice=False):
    nc, a = chip.nc, chip.nc.scalar
    eps = chip.w("eps", first=1 if twice else 0, cols=1)
    load_functions(nc, EXP_LN)
    for c in range(NCH):
        a.wait_ge(chip.ln_centred, NCH * k + c + 1)
        nc.scalar.activation(chunk(chip.sq, c), chip.pa[:, c, 0:CH], ACT.Square).then_inc(chip.ln_square, 1)
    for c in range(NCH):
        a.wait_ge(chip.ln_var, NCH * k + c + 1)
        nc.scalar.activation(chunk(chip.sq, c), chip.pb[:, c, 0:CH], ACT.Ln, bias=eps,
                             scale=1.0 + EPS if twice else 1.0).then_inc(chip.ln_log, 1)
        a.wait_ge(chip.ln_log, NCH * k + c + 1)
        nc.scalar.activation(chunk(chip.rs, c), chunk(chip.sq, c), ACT.Exp,
                             scale=-0.5).then_inc(chip.ln_rstd, 1)



def tokenise(chip, x, xedge, tokw, cls2, small):
    nc = chip.nc
    with ExitStack() as ctx:
        def sb(name, shape):
            return ctx.enter_context(nc.sbuf_tensor(name, shape, F32))
        xt = sb("xt", [128, NB, NN, 4, NV])
        xe = sb("xe", [128, NB, NV])
        tw = sb("tw", [18, D, 64])
        wl = sb("wl", [128, 4, 2, D])
        s_x = [[chip.stage_sem(f"x_loaded{b}{j}") for j in range(2)] for b in range(NB)]
        s_e, s_w, s_cls = chip.stage_sem("edge_loaded"), chip.stage_sem("tokw_loaded"), chip.stage_sem("cls_loaded")
        s_wp, s_wl = chip.stage_sem("patch_matrix"), chip.stage_sem("patch_matrix_sb")
        s_conv, s_edge, s_lo, s_hi = (chip.stage_sem("tok_conv"), chip.stage_sem("tok_edge"), chip.stage_sem("tok_low"),
                                      chip.stage_sem("tok_high"))
        pw = chip.psum[:, 7, :]
        pe_edge = chip.psum[:, 6, 0:NB * NV]
        block = ctx.enter_context(nc.Block())

        @block.sync
        def _(sp):
            sp.dma_start(tw[:, :, :], tokw).then_inc(s_w, 16)
            a, z = GROUP_SPAN[0]
            sp.dma_start(chip.small[:, a:z], small[:, a:z]).then_inc(chip.small_loaded[0], 16)
            for b in range(NB):
                for j in range(2):
                    sp.dma_start(xt[:, b, 8 * j:8 * j + 8], x[:, b, 8 * j:8 * j + 8]).then_inc(s_x[b][j], 16)
            for g in range(1, len(GROUPS)):
                a, z = GROUP_SPAN[g]
                sp.dma_start(chip.small[:, a:z], small[:, a:z]).then_inc(chip.small_loaded[g], 16)

        @block.scalar
        def _(act):
            act.dma_start(xe[:, :, :], xedge).then_inc(s_e, 16)
            act.dma_start(chip.h[:, 0:1], cls2).then_inc(s_cls, 16)
            for b in range(NB):
                hv = chip.h[64 * b:64 * b + 64, 1:NTOK].rearrange("p (v n) -> p n v", n=NN)
                for j in range(2):
                    act.wait_ge(s_conv, 2 * b + j + 1)
                    nc.scalar.activation(hv[:, 8 * j:8 * j + 8, :],
                                         chip.psum[0:64, 2 * b + j, :].rearrange("p (m v) -> p m v", v=NV),
                                         ACT.Copy).then_inc(s_lo, 1)

        @block.tensor
        def _(pe):
            pe.wait_ge(s_w, 16)
            chip.need(pe, 0)
            dft = chip.w("dft", rows=18)
            for d in range(D):
                for half in range(2):
                    last = nc.tensor.matmul(pw[64 * half:64 * half + 64, 8 * d:8 * d + 8], tw[:, d, :],
                                            dft[:, 8 * half:8 * half + 8], start=True, stop=True)
            last.then_inc(s_wp, 1)
            pe.wait_ge(s_wl, 1)
            pe.wait_ge(s_e, 16)
            for r in range(4):
                last = nc.tensor.matmul(pe_edge, wl[:, r].rearrange("p t d -> p (t d)"),
                                        xe[:, :, :].rearrange("p b v -> p (b v)"), start=(r == 0), stop=(r == 3))
            last.then_inc(s_edge, 1)
            for b in range(NB):
                for j in range(2):
                    pe.wait_ge(s_x[b][j], 16)
                    for r in range(4):
                        last = nc.tensor.matmul(chip.psum[:, 2 * b + j, :], wl[:, r].rearrange("p t d -> p (t d)"),
                                                xt[:, b, 8 * j:8 * j + 8, r, :], start=(r == 0), stop=(r == 3))
                    last.then_inc(s_conv, 1)

        @block.vector
        def _(v):
            nc.vector.memset(chip.h[:, NTOK:TP], 0.0).then_inc(s_hi, 1)
            v.wait_ge(s_wp, 1)
            nc.vector.tensor_copy(wl[:, :, :, :], pw.rearrange("p (d t r) -> p r t d", t=2, r=4)).then_inc(s_wl, 1)
            for b in range(NB):
                hv = chip.h[64 * b:64 * b + 64, 1:NTOK].rearrange("p (v n) -> p n v", n=NN)
                v.wait_ge(s_lo, 2 * b + 2)
                for n0, n1, src in ((0, 7, chip.psum[64:128, 2 * b, NV:8 * NV]),
                                    (7, 15, chip.psum[64:128, 2 * b + 1, :])):
                    nc.vector.tensor_tensor(hv[:, n0:n1, :], src.rearrange("p (m v) -> p m v", v=NV),
                                            hv[:, n0:n1, :], ALU.add).then_inc(s_hi, 1)
                v.wait_ge(s_edge, 1)
                nc.vector.tensor_tensor(hv[:, 15, :], pe_edge[64:128, NV * b:NV * b + NV], hv[:, 15, :],
                                        ALU.add).then_inc(s_hi, 1)
            v.wait_ge(s_cls, 16)



def linear_attention(chip):
    nc = chip.nc
    k_ln = chip.next_norm()
    with ExitStack() as ctx:
        def sb(name, shape):
            return ctx.enter_context(nc.sbuf_tensor(name, shape, F32))
        xn, ke, q, g = sb("xn", [P, TP]), sb("ke", [P, TP]), sb("q", [P, TP]), sb("g", [P, TP])
        vt, kt = sb("vt", [TT, NT, 128]), sb("kt", [TT, NT, 128])
        hg = sb("hg", [32, TP])
        kmax, nmax, ksum, kinv = sb("kmax", [P, NCH]), sb("nmax", [P, 1]), sb("ksum", [P, NCH]), sb("kinv", [P, 2])
        rs2, sq2, xc = sb("rs2", [P, TP]), sb("sq2", [P, TP]), sb("centred", [P, TP])
        cx = sb("cx", [P, 128])
        (s_r2, s_k, s_xn, s_g1, s_hg, s_g2, s_v, s_vt, s_nmax, s_ke, s_q, s_qs, s_kt, s_kts, s_cx, s_cxs, s_o,
         s_og, s_p) = (chip.stage_sem("a0_" + n) for n in (
             "rstd2", "k", "xn", "gate1", "gate1_act", "gate2", "v", "v_sb", "neg_max", "kexp", "q", "q_sb",
             "kt", "kt_sb", "context", "context_sb", "out", "gated", "proj"))
        s_step = chip.stage_sem("a0_dve_step")
        s_gate = chip.stage_sem("a0_gate")
        s_log2 = chip.stage_sem("a0_log2")
        block = ctx.enter_context(nc.Block())
        pa, pb, pc = chip.pa, chip.pb, chip.pc

        @block.tensor
        def _(pe):
            norm_tensor(chip, k_ln, chip.h)
            chip.need(pe, 1)
            for c in range(NCH):
                pe.wait_ge(chip.ln_out, NCH * k_ln + c + 1)
                nc.tensor.matmul(pa[:, c, 0:CH], chip.w("a0_wk"), chunk(chip.xl, c), start=True, stop=True).then_inc(s_k, 1)
            pe.wait_ge(s_r2, NCH)
            for j in range(NT):
                last = nc.tensor.matmul(pb[0:TT, j // 3, 128 * (j % 3):128 * (j % 3) + 128],
                                        chip.xl[:, TT * j:TT * j + TT], chip.w("a0_wv"), start=True, stop=True)
            last.then_inc(s_v, 1)
            for c in range(NCH):
                pe.wait_ge(s_xn, c + 1)
                if c == 2:
                    pe.wait_ge(s_hg, 1)
                nc.tensor.matmul(pc[0:32, c % 2, 0:CH], chip.w("a0_wg1"), chunk(xn, c), start=True,
                                 stop=True).then_inc(s_g1, 1)
            pe.wait_ge(s_ke, NCH)
            for c in range(NCH):
                nc.tensor.matmul(pa[:, c, 0:CH], chip.w("a0_wq"), chunk(chip.xl, c), start=True,
                                 stop=True).then_inc(s_q, 1)
            pe.wait_ge(s_vt, 1)
            for j in range(NT):
                last = nc.tensor.transpose(pb[0:TT, j // 3, 128 * (j % 3):128 * (j % 3) + 128],
                                           ke[:, TT * j:TT * j + TT], chip.w("ident"))
            last.then_inc(s_kt, 1)
            for c in range(NCH):
                pe.wait_ge(s_hg, NCH)
                if c == 2:
                    pe.wait_ge(s_gate, 1)
                nc.tensor.matmul(pc[:, c % 2, 0:CH], chip.w("a0_wg2", rows=32), hg[:, c * CH:(c + 1) * CH],
                                 start=True, stop=True).then_inc(s_g2, 1)
            pe.wait_ge(s_kts, 1)
            pe.wait_ge(s_gate, NCH)
            for j in range(NT):
                last = nc.tensor.matmul(pc[:, 0, 0:128], kt[:, j, :], vt[:, j, :], start=(j == 0), stop=(j == NT - 1))
            last.then_inc(s_cx, 1)
            pe.wait_ge(s_cxs, 1)
            pe.wait_ge(s_qs, NCH)
            for c in range(NCH):
                nc.tensor.matmul(pa[:, c, 0:CH], cx[:, :], chunk(q, c), start=True, stop=True).then_inc(s_o, 1)
            for c in range(NCH):
                pe.wait_ge(s_og, c + 1)
                nc.tensor.matmul(pb[:, c, 0:CH], chip.w("a0_wproj"), chunk(ke, c), start=True, stop=True).then_inc(s_p, 1)

        @block.scalar
        def _(act):
            norm_scalar(chip, k_ln)
            for c in range(NCH):
                nc.scalar.activation(chunk(sq2, c), pb[:, c, 0:CH], ACT.Ln, bias=chip.w("eps", first=1, cols=1),
                                     scale=1.0 + EPS).then_inc(s_log2, 1)
                act.wait_ge(s_log2, c + 1)
                nc.scalar.activation(chunk(rs2, c), chunk(sq2, c), ACT.Exp, scale=-0.5).then_inc(s_r2, 1)
            act.wait_ge(s_nmax, 1)
            for c in range(NCH):
                n = LAST if c == NCH - 1 else CH
                nc.scalar.activation(ke[:, c * CH:c * CH + n], pa[:, c, 0:n], ACT.Exp, bias=nmax[:, :],
                                     accum_out=ksum[:, c:c + 1]).then_inc(s_ke, 1)
            for c in range(NCH):
                act.wait_ge(s_g1, c + 1)
                nc.scalar.activation(hg[:, c * CH:(c + 1) * CH], pc[0:32, c % 2, 0:CH], ACT.Gelu,
                                     bias=chip.w("a0_bg1", rows=32)).then_inc(s_hg, 1)
            act.wait_ge(s_kt, 1)
            nc.scalar.activation(kt[:, :, :].rearrange("p (c j) n -> p c j n", c=3), pb[0:TT, :, 0:384].rearrange("p c (j n) -> p c j n", n=128),
                                 ACT.Copy).then_inc(s_kts, 1)
            for c in range(NCH):
                act.wait_ge(s_g2, c + 1)
                nc.scalar.activation(chunk(g, c), pc[:, c % 2, 0:CH], ACT.Sigmoid,
                                     bias=chip.w("a0_bg2")).then_inc(s_gate, 1)

        @block.vector
        def _(v):
            steps = Steps(s_step)
            for c in range(NCH):
                v.wait_ge(chip.ln_square, NCH * k_ln + c + 1)
                last = steps.mark(nc.vector.tensor_copy(chunk(xc, c), pa[:, c, 0:CH]))
            norm_vector(chip, k_ln, chip.xl)
            chip.need(v, 1)
            v.wait_ge(s_step, last)
            for c in range(NCH):
                v.wait_ge(s_k, c + 1)
                n = LAST if c == NCH - 1 else CH
                last = steps.mark(nc.vector.reduce_max(kmax[:, c:c + 1], pa[:, c, 0:n], AX.X))
            v.wait_ge(s_step, last)
            nc.vector.tensor_reduce(nmax[:, :], kmax[:, :], AX.X, ALU.max, negate=True).then_inc(s_nmax, 1)
            for c in range(NCH):
                v.wait_ge(s_r2, c + 1)
                steps.settle(v, nc.vector.tensor_tensor(chunk(xn, c), chunk(xc, c), chunk(rs2, c), ALU.mult))
                nc.vector.tensor_scalar(chunk(xn, c), chunk(xn, c), chip.w("a0_g"), chip.w("a0_b"),
                                        ALU.mult, ALU.add).then_inc(s_xn, 1)
            nc.vector.memset(ke[:, NTOK:TP], 0.0).then_inc(s_ke, 1)
            v.wait_ge(s_v, 1)
            nc.vector.tensor_copy(vt[:, :, :].rearrange("p (c j) n -> p c j n", c=3), pb[0:TT, :, 0:384].rearrange("p c (j n) -> p c j n", n=128)
                                  ).then_inc(s_vt, 1)
            v.wait_ge(s_ke, NCH + 1)
            steps.settle(v, nc.vector.reduce_sum(kinv[:, 0:1], ksum[:, :], AX.X))
            steps.settle(v, nc.vector.reciprocal(kinv[:, 1:2], kinv[:, 0:1]))
            for c in range(NCH):
                v.wait_ge(s_q, c + 1)
                nc.vector.tensor_copy(chunk(q, c), pa[:, c, 0:CH]).then_inc(s_qs, 1)
            v.wait_ge(s_cx, 1)
            nc.vector.scalar_tensor_tensor(cx[:, :], pc[:, 0, 0:128], kinv[:, 1:2], chip.w("a0_mask"),
                                           ALU.mult, ALU.mult).then_inc(s_cxs, 1)
            for c in range(NCH):
                v.wait_ge(s_o, c + 1)
                v.wait_ge(s_gate, NCH)
                nc.vector.tensor_tensor(chunk(ke, c), pa[:, c, 0:CH], chunk(g, c), ALU.mult).then_inc(s_og, 1)
            for c in range(NCH):
                v.wait_ge(s_p, c + 1)
                nc.vector.scalar_tensor_tensor(chunk(chip.h, c), pb[:, c, 0:CH], chip.w("a0_bproj"),
                                               chunk(chip.h, c), ALU.add, ALU.add).then_inc(s_step, 1)



def route_vector(chip, steps, r, kind, n_e, group_bias2, s):
    nc, v = chip.nc, chip.nc.vector
    e2 = 2 * n_e
    lg, eq, cand, o1, o2 = r["lg"], r["eq"], r["cand"], r["o1"], r["o2"]
    m1, m2, mm, ssum, w1, w2, dd = (r[x] for x in ("m1", "m2", "mm", "ssum", "w1", "w2", "dd"))

    def by_tile(t):
        return t[:, :, :].rearrange("p (j b) e -> p j (b e)", b=2)

    def over_tiles(row):
        return row[0:TT].unsqueeze(1).to_broadcast([TT, NT, e2])

    def over_experts(m):
        return m[:, :].unsqueeze(2).to_broadcast([TT, 2 * NT, n_e])

    def first_best(src, best, one_hot):
        steps.settle(v, nc.vector.tensor_reduce(best[:, :], src[:, :, :], AX.X, ALU.max))
        steps.settle(v, nc.vector.tensor_tensor(eq[:, :, :], src[:, :, :], over_experts(best), ALU.is_equal))
        steps.settle(v, nc.vector.tensor_tensor(by_tile(cand), by_tile(eq), over_tiles(chip.w(f"rev{n_e}")), ALU.mult))
        steps.settle(v, nc.vector.tensor_reduce(mm[:, :], cand[:, :, :], AX.X, ALU.max))
        steps.settle(v, nc.vector.tensor_tensor(one_hot[:, :, :], cand[:, :, :], over_experts(mm), ALU.is_equal))

    v.wait_ge(s["logits"], 1)
    steps.settle(v, nc.vector.tensor_tensor(
        by_tile(lg), chip.pc[0:TT, 1, 0:NT * e2].rearrange("p (j n) -> p j n", n=e2),
        over_tiles(chip.w(r["name"] + "_gbias")), ALU.add))
    if group_bias2:
        steps.settle(v, nc.vector.tensor_tensor(by_tile(lg), by_tile(lg), over_tiles(chip.w(r["name"] + "_gbias2")), ALU.add))
    first_best(lg, m1, o1)
    tg = r["tg"]

    def spread():
        nc.vector.tensor_tensor(r["d"][:, :, :], lg[:, :, :], over_experts(m1), ALU.subtract).then_inc(s["d"], 1)

    if kind == "switch":
        spread()
        nc.vector.memset(tg[:, :, e2:32], 0.0).then_inc(s["gates"], 1)
        nc.vector.tensor_copy(tg[:, :, 0:e2], by_tile(o1)).then_inc(s["gates"], 1)
        v.wait_ge(s["exp"], 1)
        steps.settle(v, nc.vector.tensor_reduce(ssum[:, :], r["ex"][:, :, :], AX.X, ALU.add))
        steps.settle(v, nc.vector.reciprocal(w1[:, :], ssum[:, :]))
        nc.vector.tensor_copy(tg[:, :, 32:34], w1[:, :].rearrange("p (j b) -> p j b", b=2)).then_inc(s["gates"], 1)
        return 3
    steps.settle(v, nc.vector.scalar_tensor_tensor(r["lg2"][:, :, :], o1[:, :, :], -1e30, lg[:, :, :], ALU.mult, ALU.add))
    first_best(r["lg2"], m2, o2)
    if kind == "mask":
        nc.vector.tensor_tensor(tg[:, :, 0:e2], by_tile(o1), by_tile(o2), ALU.add).then_inc(s["gates"], 1)
        return 1
    steps.settle(v, nc.vector.tensor_tensor(dd[:, 0:2 * NT], m2[:, :], m1[:, :], ALU.subtract))
    if kind == "probs":
        spread()
        nc.vector.tensor_copy(dd[:, 2 * NT:4 * NT], dd[:, 0:2 * NT]).then_inc(s["d"], 1)
        v.wait_ge(s["exp"], 2)
        steps.settle(v, nc.vector.tensor_reduce(ssum[:, :], r["ex"][:, :, :], AX.X, ALU.add))
        steps.settle(v, nc.vector.reciprocal(w1[:, :], ssum[:, :]))
        steps.settle(v, nc.vector.tensor_scalar(dd[:, 0:2 * NT], dd[:, 2 * NT:4 * NT], 1.0, None, ALU.subtract))
        nc.vector.tensor_tensor(r["gap"][:, :], dd[:, 0:2 * NT], w1[:, :], ALU.mult).then_inc(s["gap"], 1)
    else:
        nc.vector.tensor_copy(r["gap"][:, :], dd[:, 0:2 * NT]).then_inc(s["gap"], 1)
    v.wait_ge(s["weights"], 2)
    steps.settle(v, nc.vector.tensor_tensor(o1[:, :, :], o1[:, :, :], over_experts(r["s1"]), ALU.mult))
    steps.settle(v, nc.vector.tensor_tensor(o2[:, :, :], o2[:, :, :], over_experts(r["s2"]), ALU.mult))
    steps.settle(v, nc.vector.tensor_tensor(o1[:, :, :], o1[:, :, :], o2[:, :, :], ALU.add))
    for part in range(3):
        at = tg[:, :, part * e2:part * e2 + e2]
        steps.settle(v, nc.vector.tensor_copy(r["low"][:, :, :], by_tile(o1)))
        steps.settle(v, nc.vector.tensor_copy(at, r["low"][:, :, :]))
        if part < 2:
            steps.settle(v, nc.vector.tensor_tensor(by_tile(o1), by_tile(o1), at, ALU.subtract))
    nc.vector.memset(r["scrap"][:, :], 0.0).then_inc(s["gates"], 1)
    return 1


def route_scalar(chip, r, kind, s):
    nc, act = chip.nc, chip.nc.scalar
    if kind in ("switch", "probs"):
        act.wait_ge(s["d"], 1)
        nc.scalar.activation(r["ex"][:, :, :], r["d"][:, :, :], ACT.Exp).then_inc(s["exp"], 1)
    if kind == "probs":
        act.wait_ge(s["d"], 2)
        nc.scalar.activation(r["dd"][:, 2 * NT:4 * NT], r["dd"][:, 2 * NT:4 * NT], ACT.Exp).then_inc(s["exp"], 1)
    if kind in ("probs", "logits"):
        act.wait_ge(s["gap"], 1)
        nc.scalar.activation(r["s1"][:, :], r["gap"][:, :], ACT.Sigmoid, scale=-1.0).then_inc(s["weights"], 1)
        nc.scalar.activation(r["s2"][:, :], r["gap"][:, :], ACT.Sigmoid).then_inc(s["weights"], 1)


def route_tiles(chip, sb, name, n_e, n_rows):
    r = {x: sb(name + x, [TT, 2 * NT, n_e]) for x in ("lg", "lg2", "eq", "cand", "o1", "o2", "d", "ex")}
    r.update({x: sb(name + x, [TT, 2 * NT]) for x in ("m1", "m2", "mm", "ssum", "w1", "w2", "s1", "s2", "gap")})
    r["dd"] = sb(name + "dd", [TT, 4 * NT])
    r["scrap"] = sb(name + "scrap", [TT, 1])
    r["low"] = sb(name + "low", [TT, NT, 2 * n_e], BF16)
    r["tg"] = sb(name + "tg", [TT, NT, n_rows])
    r["rows"] = sb(name + "rows", [n_rows, TP])
    r["rows16"] = sb(name + "rows16", [128, TP], BF16)
    r["name"] = name
    return r


HS_RING = 3
LEAD = 2
BARRED_WORD = (40 + 127) << 7


def experts2(chip, name, slab, group, n_e, hc, func, kind):
    nc = chip.nc
    k_ln = chip.next_norm()
    hid = 128 * hc
    nu = NCH * hc
    pairs = n_e // 2
    e2 = 2 * n_e
    weighted = kind == "logits"
    k_rows = 3 * e2 if weighted else e2
    n_rows = 34 if kind == "switch" else k_rows
    sel_rows = 128 if weighted else k_rows
    with ExitStack() as ctx:
        def sb(nm, shape, dt=F32):
            return ctx.enter_context(nc.sbuf_tensor(nm, shape, dt))
        wide = SLAB2[hc]
        ws = sb(name + "slab", [128, n_e * wide])
        wsp = sb(name + "wsplit", [128, 2, 2, hid], F32R)
        second_w = sb(name + "second_w", [128, 2, 65 * hc + 1])
        xsp = sb(name + "xsplit", [128, NB, TP], F32R)
        hs = sb(name + "hs", [128, HS_RING, NB, CH])
        gs, ge = sb(name + "gs", [P, HS_RING, CH]), sb(name + "ge", [P, 2, CH])
        r = route_tiles(chip, sb, name, n_e, n_rows)
        s = {x: chip.stage_sem(name + "_" + x) for x in
             ("logits", "d", "exp", "gap", "weights", "gates", "rows", "rows_sb", "total", "high", "low", "wsplit", "wsplit_high",
              "first", "act", "second", "slab", "w2", "spread", "spread_sb", "scaled", "added", "done", "step", "prob",
              "prob_sb")}
        if kind == "switch":
            cnt, zero, thr = sb("cnt", [e2, TP]), sb("zero", [e2, TP]), sb("thr", [e2, 1])
            big = sb("big", [128, 2])
            yp, yn = sb("yp", [P, TP]), sb("yn", [P, TP])
            probs = sb("probs", [P, TP])
            mk = sb("mk", [P, TP], mybir.dt.uint32)
        block = ctx.enter_context(nc.Block())
        pa, pb, pc = chip.pa, chip.pb, chip.pc
        n_gates = 3 if kind == "switch" else 1
        hidden = [chip.psum[:, 3:5], chip.psum[:, 5:7]]
        gate_bank = [chip.psum[:, 2], chip.psum[:, 7]]

        def of_expert(i, k, first, n):
            return ws[:, bass.ds(i * (2 * wide) + (k * wide + first), n)]

        def col(k, n):
            return second_w[:, k, 64 * hc + n:64 * hc + n + 1]

        def sel(i, k, b):
            n = hid + 65 * hc + 1 + 64 * b
            return ws[:, :].bitcast(BF16)[0:sel_rows, bass.ds(i * (4 * wide) + 2 * (k * wide + n), 128)]

        def unit(n):
            k, m = divmod(n, nu)
            return (k, *divmod(m, hc))

        @block.sync
        def _(sp):
            sp.dma_start(ws[:, :], slab).then_inc(s["slab"], 16)

        @block.tensor
        def _(pe):
            norm_tensor(chip, k_ln, chip.h)
            chip.need(pe, group)
            for j in range(NT):
                if j % 3 == 0:
                    pe.wait_ge(chip.ln_out, NCH * k_ln + j // 3 + 1)
                last = nc.tensor.matmul(pc[0:TT, 1, e2 * j:e2 * j + e2], chip.xl[:, TT * j:TT * j + TT],
                                        chip.w(name + "_gate"), start=True, stop=True)
            last.then_inc(s["logits"], 1)
            pe.wait_ge(s["gates"], n_gates)
            for j in range(NT):
                last = nc.tensor.transpose(pb[0:n_rows, j // 3, TT * (j % 3):TT * (j % 3) + TT], r["tg"][:, j, :],
                                           chip.w("ident", rows=TT, cols=TT))
            last.then_inc(s["rows"], 1)
            if kind == "switch":
                pe.wait_ge(s["total"], 1)
                nc.tensor.matmul(pc[0:e2, 0, 0:1], chip.w("shift", rows=e2), cnt[:, NTOK - 1:NTOK],
                                 start=True, stop=True).then_inc(s["total"], 1)
            pe.wait_ge(s["rows_sb"], 2)
            if not weighted:
                for c in range(NCH):
                    nc.tensor.matmul(pa[:, c, 0:CH], chip.w(name + "_b2", rows=k_rows), chunk(r["rows"][0:k_rows], c),
                                     start=True, stop=False, skip_group_check=True)
            pe.wait_ge(s["low"], NB)

            def first(i, n):
                k, c, h = unit(n % (2 * nu))
                i, m = i + n // (2 * nu), n % (2 * nu)
                if m % nu == 0:
                    pe.wait_ge(s["wsplit"], 2 * i + k + 1)
                pe.wait_ge(s["act"], 2 * nu * i + m + 1)
                for b in range(NB):
                    out = hidden[m % 2][:, b, 0:CH]
                    for part in range(2):
                        last = nc.tensor.matmul(out, wsp[:, k, part, 128 * h:128 * h + 128], chunk(xsp[:, b], c),
                                                start=(part == 0), stop=(part == 1 and weighted))
                    if not weighted:
                        last = nc.tensor.matmul(out, sel(i, k, b), chunk(r["rows16"][0:sel_rows], c), start=False, stop=True)
                last.then_inc(s["first"], 1)
                if weighted:
                    pe.wait_ge(s["spread_sb"], 2 * nu * i + m + 1)
                    nc.tensor.matmul(gate_bank[m % 2][:, 0:CH], sel(i, k, 0), chunk(r["rows16"][0:sel_rows], c),
                                     start=True, stop=True).then_inc(s["spread"], 1)

            def second(i, n):
                k, c, h = unit(n)
                if n % nu == 0:
                    pe.wait_ge(s["w2"], 2 * i + k + 1)
                if weighted:
                    pe.wait_ge(s["scaled"], 2 * nu * i + n + 1 + (HS_RING - 2))
                pe.wait_ge(s["act"], 2 * nu * i + n + 1 + LEAD)
                out = pa[:, n % 2] if weighted else pa[:, c]
                for b in range(NB):
                    last = nc.tensor.matmul(out[64 * b:64 * b + 64, 0:CH], second_w[:, k, 64 * h:64 * h + 64], hs[:, n % HS_RING, b, :],
                                            start=weighted, stop=weighted, skip_group_check=True)
                last.then_inc(s["second"], 1)

            def pair(i, last_pair):
                for n in range(2 * nu):
                    if not (last_pair and n + LEAD >= 2 * nu):
                        first(i, n + LEAD)
                    second(i, n)

            for n in range(LEAD):
                first(0, n)
            with pe.Fori(0, pairs - 1) as i:
                pair(i, False)
            pair(pairs - 1, True)
            if kind == "switch":
                for c in range(NCH):
                    nc.tensor.matmul(pb[:, c, 0:CH], chip.w("seqsel", rows=2, row0=32), r["rows"][32:34, c * CH:(c + 1) * CH],
                                     start=True, stop=True).then_inc(s["prob"], 1)

        @block.scalar
        def _(act):
            norm_scalar(chip, k_ln)
            act.wait_ge(chip.ln_out, NCH * (k_ln + 1))
            for b in range(NB):
                half = slice(64 * b, 64 * b + 64)
                nc.scalar.activation(xsp[half, b], chip.xl[half, :], ACT.Copy).then_inc(s["high"], 1)
            route_scalar(chip, r, kind, s)
            act.sem_inc(s["act"], LEAD)
            if weighted:
                act.sem_inc(s["spread_sb"], 2)
            if func == ACT.Gelu:
                load_functions(nc, GELU)
            with act.Fori(0, pairs) as i:
                for n in range(2 * nu):
                    k, c, h = unit(n)
                    if weighted:
                        act.wait_ge(s["spread"], 2 * nu * i + n + 1)
                        act.wait_ge(s["scaled"], 2 * nu * i + n + 1)
                        nc.scalar.activation(gs[:, n % HS_RING], gate_bank[n % 2][:, 0:CH], ACT.Copy
                                             ).then_inc(s["spread_sb"], 1)
                    if n % nu == 0:
                        act.wait_ge(s["w2"], 2 * i + k + 1)
                    act.wait_ge(s["first"], 2 * nu * i + n + 1 + 2 * nu)
                    act.wait_ge(s["second"], 2 * nu * i + n + 1 + (2 * nu - HS_RING))
                    nc.scalar.activation(hs[:, n % HS_RING], hidden[n % 2][:, :, 0:CH], func,
                                         bias=col(k, h)).then_inc(s["act"], 1)
            if kind == "switch":
                for c in range(NCH):
                    act.wait_ge(s["prob"], c + 1)
                    nc.scalar.activation(chunk(probs, c), pb[:, c, 0:CH], ACT.Copy).then_inc(s["prob_sb"], 1)

        @block.vector
        def _(v):
            steps = Steps(s["step"])
            norm_vector(chip, k_ln, chip.xl)
            chip.need(v, group)
            assert route_vector(chip, steps, r, kind, n_e, name == "f3", s) == n_gates
            v.wait_ge(s["high"], NB)
            for b in range(NB):
                own, other = slice(64 * b, 64 * b + 64), slice(64 - 64 * b, 128 - 64 * b)
                nc.vector.tensor_tensor(xsp[other, b], chip.xl[own, :], xsp[own, b].bitcast(F32),
                                        ALU.subtract).then_inc(s["low"], 1)
            v.wait_ge(s["rows"], 1)
            if kind == "switch":
                steps.settle(v, nc.vector.memset(zero[:, :], 0.0))
                steps.settle(v, nc.vector.tensor_copy(chunks(r["rows"][0:34]), pb[0:34, :, 0:CH]))
                steps.settle(v, nc.vector.tensor_tensor_scan(cnt[:, :], r["rows"][0:e2, :], zero[:, :], 0.0, ALU.add, ALU.add))
                v.sem_inc(s["total"], 1)
                v.wait_ge(s["total"], 2)
                steps.settle(v, nc.vector.tensor_scalar(thr[:, :], pc[0:e2, 0, 0:1], -1.0, float(CAPACITY), ALU.mult, ALU.add))
                steps.settle(v, nc.vector.scalar_tensor_tensor(cnt[:, :], cnt[:, :], thr[:, :], r["rows"][0:e2, :],
                                                               ALU.is_le, ALU.mult))
                nc.vector.tensor_copy(r["rows"][0:e2, :], cnt[:, :]).then_inc(s["rows_sb"], 1)
                nc.vector.tensor_scalar(r["rows16"][0:e2, :], cnt[:, :], 1.0, None, ALU.subtract).then_inc(s["rows_sb"], 1)
            else:
                if weighted:
                    v.sem_inc(s["rows_sb"], 1)
                    steps.settle(v, nc.vector.memset(r["rows16"][:, :], 0.0))
                    nc.vector.tensor_copy(chunks(r["rows16"][0:k_rows]), pb[0:k_rows, :, 0:CH]).then_inc(s["rows_sb"], 1)
                else:
                    nc.vector.tensor_copy(chunks(r["rows"][0:k_rows]), pb[0:k_rows, :, 0:CH]).then_inc(s["rows_sb"], 1)
                    nc.vector.tensor_scalar(chunks(r["rows16"][0:k_rows]), pb[0:k_rows, :, 0:CH], 1.0, None,
                                            ALU.subtract).then_inc(s["rows_sb"], 1)
            v.sem_inc(s["second"], 2 * nu)
            v.sem_inc(s["first"], 2 * nu)
            if weighted:
                v.sem_inc(s["scaled"], HS_RING)
            v.wait_ge(s["slab"], 16)

            def split_weights(i, k):
                v.wait_ge(s["first"], 2 * nu * i + (k + 1) * nu)
                nc.vector.tensor_copy(wsp[:, k, 0], of_expert(i, k, 0, hid)).then_inc(s["wsplit_high"], 1)
                v.wait_ge(s["wsplit_high"], 2 * i + k + 1)
                nc.vector.tensor_tensor(wsp[:, k, 1], of_expert(i, k, 0, hid), wsp[:, k, 0].bitcast(F32),
                                        ALU.subtract).then_inc(s["wsplit"], 1)
                v.wait_ge(s["second"], 2 * nu * i + (k + 1) * nu)
                nc.vector.tensor_copy(second_w[:, k], of_expert(i, k, hid, 65 * hc + 1)).then_inc(s["w2"], 1)

            def scale(i, n):
                k, c, h = unit(n)
                v.wait_ge(s["second"], 2 * nu * i + n + 1 + 2 * nu)
                v.wait_ge(s["spread_sb"], 2 * nu * i + n + 1 + 2)
                v.wait_ge(s["added"], 2 * nu * i + n + 1)
                nc.vector.scalar_tensor_tensor(ge[:, n % 2], pa[:, n % 2, 0:CH], col(k, hc), gs[:, n % HS_RING],
                                               ALU.add, ALU.mult).then_inc(s["scaled"], 1)
                v.wait_ge(s["scaled"], 2 * nu * i + n + 1 + HS_RING)
                nc.vector.tensor_tensor(chunk(chip.h, c), chunk(chip.h, c), ge[:, n % 2], ALU.add
                                        ).then_inc(s["added"], 1)

            if weighted:
                v.sem_inc(s["added"], 2)
                split_weights(0, 0)
                split_weights(0, 1)
                with v.Fori(0, pairs - 1) as i:
                    for n in range(2 * nu):
                        scale(i, n)
                        if (n + 1) % nu == 0:
                            split_weights(i + 1, n // nu)
                for n in range(2 * nu):
                    scale(pairs - 1, n)
                return
            with v.Fori(0, pairs) as i:
                for k in range(2):
                    split_weights(i, k)
            v.wait_ge(s["second"], n_e * nu + 2 * nu)
            if kind == "mask":
                nc.vector.tensor_tensor(chunks(chip.h[:, :]), chunks(chip.h[:, :]), pa[:, :, 0:CH], ALU.add
                                        ).then_inc(s["done"], 1)
                return
            v.wait_ge(s["prob_sb"], NCH)
            nc.vector.memset(big[:, 0:1], 1e4).then_inc(s["done"], 1)
            nc.vector.memset(big[:, 1:2], -1e4).then_inc(s["done"], 1)
            steps.settle(v, nc.vector.tensor_tensor(chunks(probs[:, :]), pa[:, :, 0:CH], chunks(probs[:, :]), ALU.mult))
            steps.settle(v, nc.vector.tensor_scalar(yp[:, :], probs[:, :], 0.0, None, ALU.max))
            steps.settle(v, nc.vector.tensor_scalar(yn[:, :], probs[:, :], 0.0, None, ALU.min))
            steps.settle(v, nc.vector.tensor_scalar(mk[:, :], yp[:, :], FLT_MAX, None, ALU.is_gt))
            steps.settle(v, nc.vector.copy_predicated(yp[:, :], mk[:, :], big[:, 0:1].to_broadcast([P, TP])))
            steps.settle(v, nc.vector.tensor_scalar(mk[:, :], yn[:, :], -FLT_MAX, None, ALU.is_lt))
            steps.settle(v, nc.vector.copy_predicated(yn[:, :], mk[:, :], big[:, 1:2].to_broadcast([P, TP])))
            steps.settle(v, nc.vector.tensor_tensor(yp[:, :], yp[:, :], yn[:, :], ALU.add))
            nc.vector.tensor_tensor(chip.h[:, :], chip.h[:, :], yp[:, :], ALU.add).then_inc(s["done"], 1)


def row_attention(chip):
    nc = chip.nc
    k_ln = chip.next_norm()
    n_heads, c_head = 8, 32
    hc = n_heads * c_head
    scale = 1.0 / (c_head * NTOK) ** 0.5
    with ExitStack() as ctx:
        def sb(name, shape):
            return ctx.enter_context(nc.sbuf_tensor(name, shape, F32))
        mn = sb("a1mn", [P, TP])
        mt = sb("a1mt", [TT, NT, 128])
        gram = sb("a1gram", [P, P])
        prod = sb("a1prod", [P, NB, hc])
        red = sb("a1red", [P, NB, n_heads])
        att = sb("a1att", [P, NB, n_heads])
        wa = sb("a1wa", [P, NB, hc])
        g = sb("a1g", [128, NB, 2, TP])
        s_mn, s_t, s_ts, s_g, s_gs, s_a, s_red, s_d, s_att, s_wa, s_gp, s_gate, s_o, s_og, s_y, s_h, s_step = (
            chip.stage_sem("a1_" + n) for n in ("mn", "mt", "mt_sb", "gram", "gram_sb", "scores", "summed", "diff",
                                                "att", "wv", "gate_in", "gate", "out", "gated", "proj", "h", "step"))
        block = ctx.enter_context(nc.Block())
        pa, pb, pc = chip.pa, chip.pb, chip.pc
        units = [(s, k, c) for s in range(NB) for k in range(2) for c in range(NCH)]

        @block.tensor
        def _(pe):
            norm_tensor(chip, k_ln, chip.h)
            chip.need(pe, 2)
            for j in range(NT):
                pe.wait_ge(s_mn, 4)
                last = nc.tensor.transpose(pa[0:TT, j // 3, 128 * (j % 3):128 * (j % 3) + 128],
                                           mn[:, TT * j:TT * j + TT], chip.w("ident"))
            last.then_inc(s_t, 1)

            def gate(u):
                s, k, c = units[u]
                if u >= 3:
                    pe.wait_ge(s_gate, u - 2)
                nc.tensor.matmul(pb[:, u % 3, 0:CH], chip.w("a1_wg", first=hc * s + 128 * k, cols=128), chunk(mn, c),
                                 start=True, stop=True).then_inc(s_gp, 1)

            for u in range(3):
                gate(u)
            pe.wait_ge(s_ts, 1)
            for j in range(NT):
                last = nc.tensor.matmul(pc[:, 0, 0:128], mt[:, j, :], mt[:, j, :], start=(j == 0), stop=(j == NT - 1))
            last.then_inc(s_g, 1)
            for u in range(3, 6):
                gate(u)
            pe.wait_ge(s_gs, 1)
            for s in range(NB):
                nc.tensor.matmul(pa[:, s, 0:hc], gram[64 * s:64 * s + 64, :], chip.w("a1_wq", rows=64, row0=64 * s),
                                 start=True, stop=True).then_inc(s_a, 1)
            for u in range(6, 9):
                gate(u)
            pe.wait_ge(s_red, 1)
            nc.tensor.matmul(pc[:, 1, 0:NB * n_heads], chip.w("tdiff"), red[:, :, :].rearrange("p s h -> p (s h)"),
                             start=True, stop=True).then_inc(s_d, 1)
            for u in range(9, 12):
                gate(u)
            pe.wait_ge(s_wa, 1)
            out_banks = [pc[:, 0], pc[:, 1]]
            for u, (s, k, c) in enumerate(units):
                if u >= 2:
                    pe.wait_ge(s_og, u - 1)
                nc.tensor.matmul(out_banks[u % 2][:, 0:CH], wa[:, s, 128 * k:128 * k + 128], chunk(mn, c),
                                 start=True, stop=True).then_inc(s_o, 1)
            for s in range(NB):
                for c in range(NCH):
                    for k in range(2):
                        pe.wait_ge(s_og, 6 * s + 3 * k + c + 1)
                        last = nc.tensor.matmul(pa[64 * s:64 * s + 64, c, 0:CH], chip.w("a1_wo", first=64 * k, cols=64),
                                                g[:, s, k, c * CH:(c + 1) * CH], start=(k == 0), stop=(k == 1))
                    last.then_inc(s_y, 1)

        @block.scalar
        def _(act):
            norm_scalar(chip, k_ln, twice=True)
            chip.need(act, 2)
            for u, (s, k, c) in enumerate(units):
                if u == 3:
                    act.wait_ge(s_g, 1)
                    nc.scalar.activation(gram[:, :], pc[:, 0, 0:128], ACT.Copy).then_inc(s_gs, 1)
                if u == 9:
                    act.wait_ge(s_d, 1)
                    nc.scalar.activation(att[:, :, :], pc[:, 1, 0:NB * n_heads].rearrange("p (s h) -> p s h", s=NB),
                                         ACT.Sigmoid, scale=scale).then_inc(s_att, 1)
                act.wait_ge(s_gp, u + 1)
                nc.scalar.activation(g[:, s, k, c * CH:(c + 1) * CH], pb[:, u % 3, 0:CH], ACT.Sigmoid,
                                     bias=chip.w("a1_bg", first=k, cols=1)).then_inc(s_gate, 1)

        @block.vector
        def _(v):
            steps = Steps(s_step)
            norm_vector(chip, k_ln, chip.xl)
            chip.need(v, 2)
            for c in range(NCH):
                v.wait_ge(chip.ln_out, NCH * k_ln + c + 1)
                nc.vector.tensor_scalar(chunk(mn, c), chunk(chip.xl, c), chip.w("a1_g"), chip.w("a1_b"),
                                        ALU.mult, ALU.add).then_inc(s_mn, 1)
            v.wait_ge(s_mn, 3)
            nc.vector.memset(mn[:, NTOK:TP], 0.0).then_inc(s_mn, 1)
            v.wait_ge(s_t, 1)
            nc.vector.tensor_copy(mt[:, :, :].rearrange("p (c j) n -> p c j n", c=3),
                                  pa[0:TT, :, 0:384].rearrange("p c (j n) -> p c j n", n=128)).then_inc(s_ts, 1)
            for s in range(NB):
                v.wait_ge(s_a, s + 1)
                steps.settle(v, nc.vector.tensor_tensor(prod[:, s, :], pa[:, s, 0:hc], chip.w("a1_wk"), ALU.mult))
            nc.vector.tensor_reduce(red[:, :, :], prod[:, :, :].rearrange("p s (h c) -> p s h c", c=c_head), AX.X,
                                    ALU.add).then_inc(s_red, 1)
            v.wait_ge(s_att, 1)
            for s in range(NB):
                last = nc.vector.tensor_tensor(wa[:, s, :].rearrange("p (h c) -> p h c", c=c_head),
                                               chip.w("a1_wv").rearrange("p (h c) -> p h c", c=c_head),
                                               att[:, s, :].unsqueeze(2).to_broadcast([P, n_heads, c_head]), ALU.mult)
            last.then_inc(s_wa, 1)
            for u, (s, k, c) in enumerate(units):
                v.wait_ge(s_o, u + 1)
                v.wait_ge(s_gate, u + 1)
                gs = g[:, s, k, c * CH:(c + 1) * CH]
                nc.vector.tensor_tensor(gs, pc[:, u % 2, 0:CH], gs, ALU.mult).then_inc(s_og, 1)
            for c in range(NCH):
                v.wait_ge(s_y, NCH + c + 1)
                nc.vector.scalar_tensor_tensor(chunk(chip.h, c), pa[:, c, 0:CH], chip.w("a1_bo"), chunk(chip.h, c),
                                               ALU.add, ALU.add).then_inc(s_h, 1)


def scan_attention(chip):
    nc = chip.nc
    k_ln = chip.next_norm()
    ns = 32
    with ExitStack() as ctx:
        def sb(name, shape):
            return ctx.enter_context(nc.sbuf_tensor(name, shape, F32))
        xp = sb("a2xp", [P, 3 + TP])
        res, xcv = sb("a2res", [P, TP]), sb("a2xcv", [P, TP])
        da, cp, yc, y, zero = (sb("a2da", [ns, TP]), sb("a2cp", [ns, TP]), sb("a2yc", [ns, TP]),
                               sb("a2y", [ns, TP]), sb("a2zero", [ns, TP]))
        o = sb("a2o", [P, TP])
        acc, col = sb("a2acc", [P, 2 * NCH]), sb("a2col", [P, 6])
        s_xp, s_xps, s_res, s_ress, s_conv, s_da, s_das, s_db, s_y, s_y2, s_y2s, s_p, s_o, s_m, s_negm, s_sq, s_v, s_vl, s_rs, s_h, s_step = (
            chip.stage_sem("a2_" + n) for n in ("xp", "xp_sb", "res", "res_sb", "conv", "da", "da_sb", "db", "y", "cy",
                                                "cy_sb", "proj", "o", "mean", "neg_mean", "square", "var", "var_log",
                                                "rstd", "h", "step"))
        block = ctx.enter_context(nc.Block())
        pa, pb, pc = chip.pa, chip.pb, chip.pc

        @block.tensor
        def _(pe):
            norm_tensor(chip, k_ln, chip.h)
            chip.need(pe, 3)
            for c in range(NCH):
                pe.wait_ge(chip.ln_out, NCH * k_ln + c + 1)
                nc.tensor.matmul(pa[:, c, 0:CH], chip.w("a2_wxp"), chunk(chip.xl, c), start=True, stop=True).then_inc(s_xp, 1)
            for c in range(NCH):
                nc.tensor.matmul(pb[:, c, 0:CH], chip.w("a2_wres"), chunk(chip.xl, c), start=True, stop=True).then_inc(s_res, 1)
            pe.wait_ge(s_xps, NCH + 1)
            for c in range(NCH):
                pe.wait_ge(s_conv, c + 1)
                nc.tensor.matmul(pa[0:ns, c, 0:CH], chip.w("a2_dt"), chunk(xcv, c), start=True, stop=True).then_inc(s_da, 1)
            pe.wait_ge(s_ress, NCH)
            for c in range(NCH):
                nc.tensor.matmul(pb[0:ns, c, 0:CH], chip.w("a2_bw"), chunk(xcv, c), start=True, stop=True).then_inc(s_db, 1)
            pe.wait_ge(s_das, NCH)
            pe.wait_ge(s_y, 1)
            for c in range(NCH):
                nc.tensor.matmul(pa[:, c, 0:CH], chip.w("a2_cw", rows=ns), y[:, c * CH:(c + 1) * CH], start=True,
                                 stop=True).then_inc(s_y2, 1)
            for c in range(NCH):
                pe.wait_ge(s_y2s, c + 1)
                nc.tensor.matmul(pb[:, c, 0:CH], chip.w("a2_ow"), chunk(res, c), start=True, stop=True).then_inc(s_p, 1)
            pe.wait_ge(s_o, NCH)
            nc.tensor.matmul(pc[:, 0, 0:NCH], chip.w("chmean"), acc[:, 0:NCH], start=True, stop=True).then_inc(s_m, 1)
            pe.wait_ge(s_sq, 1)
            nc.tensor.matmul(pc[:, 1, 0:1], chip.w("chmean"), col[:, 1:2], start=True, stop=True).then_inc(s_v, 1)

        @block.scalar
        def _(act):
            norm_scalar(chip, k_ln)
            for c in range(NCH):
                act.wait_ge(s_xp, c + 1)
                nc.scalar.activation(xp[:, 3 + c * CH:3 + (c + 1) * CH], pa[:, c, 0:CH], ACT.Identity,
                                     bias=chip.w("a2_bxp")).then_inc(s_xps, 1)
            for c in range(NCH):
                act.wait_ge(s_da, c + 1)
                nc.scalar.activation(da[:, c * CH:(c + 1) * CH], pa[0:ns, c, 0:CH], ACT.Exp).then_inc(s_das, 1)
            for c in range(NCH):
                act.wait_ge(s_res, c + 1)
                nc.scalar.activation(chunk(res, c), pb[:, c, 0:CH], ACT.Silu, bias=chip.w("a2_bres")).then_inc(s_ress, 1)
            act.wait_ge(s_negm, 1)
            nc.scalar.activation(chip.sq[:, 0:NTOK], o[:, 0:NTOK], ACT.Square, bias=col[:, 0:1],
                                 accum_out=col[:, 1:2]).then_inc(s_sq, 1)
            act.wait_ge(s_v, 1)
            nc.scalar.activation(col[:, 2:3], pc[:, 1, 0:1], ACT.Ln, bias=chip.w("eps", cols=1)).then_inc(s_vl, 1)
            act.wait_ge(s_vl, 1)
            nc.scalar.activation(col[:, 3:4], col[:, 2:3], ACT.Exp, scale=-0.5).then_inc(s_rs, 1)

        @block.vector
        def _(v):
            steps = Steps(s_step)
            nc.vector.memset(xp[:, 0:3], 0.0).then_inc(s_xps, 1)
            steps.settle(v, nc.vector.memset(zero[:, :], 0.0))
            norm_vector(chip, k_ln, chip.xl)
            chip.need(v, 3)
            for c in range(NCH):
                v.wait_ge(s_xps, c + 2)
                a = c * CH
                steps.settle(v, nc.vector.tensor_scalar(chunk(xcv, c), xp[:, a:a + CH], chip.w("a2_convw", cols=1),
                                                        chip.w("a2_convb"), ALU.mult, ALU.add))
                for k in range(1, 4):
                    i = nc.vector.scalar_tensor_tensor(chunk(xcv, c), xp[:, a + k:a + k + CH],
                                                       chip.w("a2_convw", first=k, cols=1), chunk(xcv, c),
                                                       ALU.mult, ALU.add)
                    if k < 3:
                        steps.settle(v, i)
                    else:
                        i.then_inc(s_conv, 1)
            v.wait_ge(s_das, NCH)
            steps.settle(v, nc.vector.tensor_tensor_scan(cp[:, :], da[:, :], zero[:, :], 1.0, ALU.mult, ALU.add))
            v.wait_ge(s_db, NCH)
            steps.settle(v, nc.vector.tensor_tensor(chunks(cp[:, :]), chunks(cp[:, :]), pb[0:ns, :, 0:CH], ALU.mult))
            steps.settle(v, nc.vector.tensor_tensor_scan(yc[:, :], cp[:, :], zero[:, :], 0.0, ALU.add, ALU.add))
            steps.settle(v, nc.vector.tensor_tensor(y[:, 1:TP], yc[:, 0:TP - 1], da[:, 1:TP], ALU.mult))
            steps.settle(v, nc.vector.tensor_tensor(y[:, 1:TP], yc[:, 1:TP], y[:, 1:TP], ALU.subtract))
            nc.vector.tensor_copy(y[:, 0:1], pb[0:ns, 0, 0:1]).then_inc(s_y, 1)
            v.wait_ge(s_ress, NCH)
            for c in range(NCH):
                v.wait_ge(s_y2, c + 1)
                nc.vector.tensor_tensor(chunk(res, c), pa[:, c, 0:CH], chunk(res, c), ALU.mult).then_inc(s_y2s, 1)
            for c in range(NCH):
                v.wait_ge(s_p, c + 1)
                n = LAST if c == NCH - 1 else CH
                a = c * CH
                nc.vector.scalar_tensor_tensor(o[:, a:a + n], pb[:, c, 0:n], chip.w("a2_ob"), xcv[:, a:a + n],
                                               ALU.add, ALU.add, accum_out=acc[:, c:c + 1]).then_inc(s_o, 1)
            v.wait_ge(s_m, 1)
            nc.vector.tensor_reduce(col[:, 0:1], pc[:, 0, 0:NCH], AX.X, ALU.add, negate=True).then_inc(s_negm, 1)
            v.wait_ge(s_rs, 1)
            steps.settle(v, nc.vector.tensor_tensor(col[:, 4:5], col[:, 3:4], chip.w("a2_g"), ALU.mult))
            steps.settle(v, nc.vector.tensor_scalar(col[:, 5:6], col[:, 0:1], col[:, 4:5], chip.w("a2_b"), ALU.mult, ALU.add))
            steps.settle(v, nc.vector.tensor_scalar(o[:, 0:NTOK], o[:, 0:NTOK], col[:, 4:5], col[:, 5:6], ALU.mult, ALU.add))
            nc.vector.tensor_tensor(chip.h[:, 0:NTOK], chip.h[:, 0:NTOK], o[:, 0:NTOK], ALU.add).then_inc(s_h, 1)


def experts3(chip, slab):
    nc = chip.nc
    k_ln = chip.next_norm()
    name, n_e = "f2", 6
    e2, k_rows = 2 * n_e, 3 * 2 * n_e
    nu, pairs, ring = NCH, n_e // 2, 2
    with ExitStack() as ctx:
        def sb(nm, shape, dt=F32):
            return ctx.enter_context(nc.sbuf_tensor(nm, shape, dt))
        ws = sb("f2slab", [128, 2, SLAB3])
        rh = sb("f2rh", [64, TP])
        h1, h2, hg = (sb("f2" + n, [128, ring, CH]) for n in ("h1", "h2", "hg"))
        r = route_tiles(chip, sb, name, n_e, k_rows)
        s = {x: chip.stage_sem(name + "_" + x) for x in
             ("router", "router_sb", "logits", "d", "exp", "gap", "weights", "gates", "rows", "rows_sb", "first",
              "act", "mid", "mid_act", "gated", "third", "done", "step")}
        s_slab = [chip.stage_sem(f"f2_slab{k}") for k in range(2)]
        block = ctx.enter_context(nc.Block())
        pa, pb, pc = chip.pa, chip.pb, chip.pc

        @block.sync
        def _(sp):
            for k in range(2):
                sp.dma_start(ws[:, k, :], slab[k]).then_inc(s_slab[k], 16)
            with sp.Fori(1, pairs) as i:
                for k in range(2):
                    sp.wait_ge(s["third"], 2 * nu * i + (ring + (k + 1) * nu - 2 * nu))
                    sp.dma_start(ws[:, k, :], slab[bass.ds(2 * i + k, 1)].rearrange("a p n -> p (a n)")
                                 ).then_inc(s_slab[k], 16)

        @block.tensor
        def _(pe):
            norm_tensor(chip, k_ln, chip.h)
            chip.need(pe, 3)
            for c in range(NCH):
                pe.wait_ge(chip.ln_out, NCH * k_ln + c + 1)
                nc.tensor.matmul(pa[0:64, c, 0:CH], chip.w("f2_rw1"), chunk(chip.xl, c), start=True, stop=True).then_inc(s["router"], 1)
            pe.wait_ge(s["router_sb"], NCH)
            for j in range(NT):
                last = nc.tensor.matmul(pc[0:TT, 1, e2 * j:e2 * j + e2], rh[:, TT * j:TT * j + TT],
                                        chip.w("f2_gate", rows=64), start=True, stop=True)
            last.then_inc(s["logits"], 1)
            pe.wait_ge(s["gates"], 1)
            for j in range(NT):
                last = nc.tensor.transpose(pb[0:k_rows, j // 3, TT * (j % 3):TT * (j % 3) + TT], r["tg"][:, j, :],
                                           chip.w("ident", rows=TT, cols=TT))
            last.then_inc(s["rows"], 1)
            pe.wait_ge(s["rows_sb"], 2)
            for c in range(NCH):
                nc.tensor.matmul(pa[:, c, 0:CH], chip.w("f2_b2", rows=k_rows), chunk(r["rows"], c),
                                 start=True, stop=False, skip_group_check=True)

            def first(i, n):
                k, c = divmod(n % (2 * nu), nu)
                i = i + n // (2 * nu)
                if c == 0:
                    pe.wait_ge(s_slab[k], 16 * i + 16)
                pe.wait_ge(s["act"], 2 * nu * i + (n % (2 * nu)) + 1)
                nc.tensor.matmul(pc[:, n % ring, 0:CH], ws[:, k, 0:128], chunk(chip.xl, c), start=True,
                                 stop=True).then_inc(s["first"], 1)

            def mid(i, n):
                k, c = divmod(n % (2 * nu), nu)
                i = i + n // (2 * nu)
                pe.wait_ge(s["gated"], 2 * nu * i + (n % (2 * nu)) + 1)
                nc.tensor.matmul(pb[:, 2, 0:CH], ws[0:k_rows, k, 386:450].bitcast(BF16), chunk(r["rows16"][0:k_rows], c),
                                 start=True, stop=True)
                pe.wait_ge(s["act"], 2 * nu * i + (n % (2 * nu)) + 1 + ring)
                nc.tensor.matmul(pb[:, n % ring, 0:CH], ws[:, k, 128:256], h1[:, n % ring, :], start=True,
                                 stop=True).then_inc(s["mid"], 1)

            def pair(i, last_pair):
                for n in range(2 * nu):
                    k, c = divmod(n, nu)
                    if not (last_pair and n + 2 >= 2 * nu):
                        first(i, n + 2)
                    pe.wait_ge(s["gated"], 2 * nu * i + n + 2)
                    if not (last_pair and n + 1 >= 2 * nu):
                        mid(i, n + 1)
                    nc.tensor.matmul(pa[:, c, 0:CH], ws[:, k, 256:384], hg[:, n % ring, :], start=False, stop=False,
                                     skip_group_check=True).then_inc(s["third"], 1)

            pe.sem_inc(s["mid"], ring)
            first(0, 0)
            first(0, 1)
            mid(0, 0)
            with pe.Fori(0, pairs - 1) as i:
                pair(i, False)
            pair(pairs - 1, True)

        @block.scalar
        def _(act):
            norm_scalar(chip, k_ln)
            for c in range(NCH):
                act.wait_ge(s["router"], c + 1)
                nc.scalar.activation(rh[:, c * CH:(c + 1) * CH], pa[0:64, c, 0:CH], ACT.Relu,
                                     bias=chip.w("f2_rb1", rows=64)).then_inc(s["router_sb"], 1)
            route_scalar(chip, r, "probs", s)
            act.sem_inc(s["act"], ring)
            with act.Fori(0, pairs) as i:
                for n in range(2 * nu):
                    k = n // nu
                    act.wait_ge(s["first"], 2 * nu * i + n + 1)
                    act.wait_ge(s["mid"], 2 * nu * i + n + 1)
                    nc.scalar.activation(h1[:, n % ring, :], pc[:, n % ring, 0:CH], ACT.Relu,
                                         bias=ws[:, k, 384:385]).then_inc(s["act"], 1)

        @block.vector
        def _(v):
            steps = Steps(s["step"])
            norm_vector(chip, k_ln, chip.xl)
            chip.need(v, 3)
            route_vector(chip, steps, r, "probs", n_e, False, s)
            v.wait_ge(s["rows"], 1)
            nc.vector.tensor_copy(chunks(r["rows"][:, :]), pb[0:k_rows, :, 0:CH]).then_inc(s["rows_sb"], 1)
            nc.vector.tensor_copy(chunks(r["rows16"][0:k_rows]), pb[0:k_rows, :, 0:CH]).then_inc(s["rows_sb"], 1)
            v.sem_inc(s["gated"], 1)
            v.sem_inc(s["third"], ring)
            with v.Fori(0, pairs) as i:
                for n in range(2 * nu):
                    k = n // nu
                    v.wait_ge(s["mid"], 2 * nu * i + n + 1 + ring)
                    nc.vector.tensor_scalar(h2[:, n % ring, :], pb[:, n % ring, 0:CH], ws[:, k, 385:386], 0.0,
                                            ALU.add, ALU.max).then_inc(s["mid_act"], 1)
                    v.wait_ge(s["mid_act"], 2 * nu * i + n + 1)
                    v.wait_ge(s["third"], 2 * nu * i + n + 1)
                    nc.vector.tensor_tensor(hg[:, n % ring, :], h2[:, n % ring, :], pb[:, 2, 0:CH],
                                            ALU.mult).then_inc(s["gated"], 1)
            v.wait_ge(s["third"], n_e * nu + ring)
            nc.vector.tensor_tensor(chunks(chip.h[:, :]), chunks(chip.h[:, :]), pa[:, :, 0:CH], ALU.add).then_inc(s["done"], 1)


def mamba(chip, selbc):
    nc = chip.nc
    k_ln, k_ln1, k_ln2 = chip.next_norm(), chip.next_norm(), chip.next_norm()
    n_s = 16
    with ExitStack() as ctx:
        def sb(name, shape, dt=F32):
            return ctx.enter_context(nc.sbuf_tensor(name, shape, dt))
        sel = sb("a3sel", [128, n_s * 2 * 128], BF16)
        xs = sb("a3xs", [128, NB, 3 + TP])
        xc, z, dt, u = (sb("a3" + n, [128, NB, TP]) for n in ("xc", "z", "dt", "u"))
        t1 = sb("a3t1", [128, NB, TP])
        dbl = sb("a3dbl", [48, NB, TP])
        rem = sb("a3rem", [32, NB, TP])
        low = sb("a3low", [32, NB, TP], BF16)
        bcp = sb("a3bcp", [128, NB, TP], BF16)
        an, ddp = sb("a3an", [128, n_s]), sb("a3ddp", [128, 128])
        da, hst, cs, pr = (sb("a3" + n, [128, 2, TP]) for n in ("da", "hst", "cs", "pr"))
        dbx = sb("a3dbx", [128, 2, TP])
        m1 = sb("a3m1", [P, TP])
        r1, n1 = sb("a3r1", [P, TP]), sb("a3n1", [P, TP])
        names = ("sel_loaded", "xs", "xs_sb", "z", "z_sb", "conv", "xc", "dbl", "dbl_sb", "dt", "abs", "exp", "log",
                 "dt_pos", "dt_done", "parts", "aexp", "a", "dp", "u", "b_spread", "c_spread", "da", "dbx", "scan",
                 "c_sb", "prod", "summed", "start", "yo", "wout", "wout_sb", "wlin", "r1", "n1", "up", "up_sb",
                 "down", "r2", "n2", "h", "step")
        s = {x: chip.stage_sem("a3_" + x) for x in names}
        block = ctx.enter_context(nc.Block())
        pa, pb, pc = chip.pa, chip.pb, chip.pc
        bank = [pa, pb]
        bc = [(b, c) for b in range(NB) for c in range(NCH)]
        cb = [(c, b) for c in range(NCH) for b in range(NB)]

        @block.sync
        def _(sp):
            sp.dma_start(sel[:, :], selbc.bitcast(BF16)).then_inc(s["sel_loaded"], 16)

        @block.tensor
        def _(pe):
            norm_tensor(chip, k_ln, chip.h)
            chip.need(pe, 4)
            pe.wait_ge(chip.ln_out, NCH * (k_ln + 1))
            for b, c in bc:
                nc.tensor.matmul(bank[b][:, c, 0:CH], chip.w("a3_win", first=128 * b, cols=128), chunk(chip.xl, c),
                                 start=True, stop=True).then_inc(s["xs"], 1)
            for n, (b, c) in enumerate(bc):
                pe.wait_ge(s["xs_sb"], n + 1)
                nc.tensor.matmul(bank[b][:, c, 0:CH], chip.w("a3_win", first=256 + 128 * b, cols=128),
                                 chunk(chip.xl, c), start=True, stop=True).then_inc(s["z"], 1)
            for n, (b, c) in enumerate(bc):
                pe.wait_ge(s["z_sb"], n + 1)
                pe.wait_ge(s["xc"], b + 1)
                nc.tensor.matmul(bank[b][0:48, c, 0:CH], chip.w("a3_wx"), chunk(xc[:, b], c), start=True,
                                 stop=True).then_inc(s["dbl"], 1)
            for n, (b, c) in enumerate(bc):
                pe.wait_ge(s["dbl_sb"], n + 1)
                nc.tensor.matmul(bank[b][:, c, 0:CH], chip.w("a3_wdt", rows=48), chunk(dbl[:, b], c), start=True,
                                 stop=True).then_inc(s["dt"], 1)
            pe.wait_ge(s["sel_loaded"], 16)
            pe.wait_ge(s["parts"], 2)
            pe.wait_ge(s["dp"], 1)
            pe.wait_ge(s["dt_pos"], NB)
            pe.wait_ge(s["abs"], NB)

            def spread_b(b, i, k):
                g = n_s * b + k
                pe.wait_ge(s["dbx"], 2 * i + g + 1)
                for c in range(NCH):
                    last = nc.tensor.matmul(pb[:, c, 0:CH], sel[:, bass.ds(i * 512 + 256 * k, 128)],
                                            chunk(bcp[:, b], c), start=True, stop=True)
                last.then_inc(s["b_spread"], 1)

            def spread_c(b, i, k, c):
                g = n_s * b + k
                pe.wait_ge(s["c_sb"], 6 * i + 3 * g + c + 1)
                nc.tensor.matmul(pc[:, (3 * k + c) % 2, 0:CH], sel[:, bass.ds(i * 512 + 256 * k + 128, 128)],
                                 chunk(bcp[:, b], c), start=True, stop=True).then_inc(s["c_spread"], 1)

            def add_up(b, i, k, c):
                if c == 0:
                    pe.wait_ge(s["prod"], 2 * i + n_s * b + k + 1 + 2)
                last = nc.tensor.matmul(pa[:, c, 0:CH], chip.w("ident"), chunk(pr[:, k], c), start=False,
                                        stop=False, skip_group_check=True)
                if c == NCH - 1:
                    last.then_inc(s["summed"], 1)

            for b in range(NB):
                for k in range(2):
                    spread_b(b, 0, k)
                    for c in range(NCH):
                        spread_c(b, 0, k, c)
                if b:
                    pe.wait_ge(s["yo"], b)
                for c in range(NCH):
                    nc.tensor.matmul(pa[:, c, 0:CH], ddp[:, :], chunk(xc[:, b], c), start=True, stop=False,
                                     skip_group_check=True)
                with pe.Fori(0, n_s // 2 - 1) as i:
                    for k in range(2):
                        spread_b(b, i + 1, k)
                        spread_c(b, i + 1, k, 0)
                        spread_c(b, i + 1, k, 1)
                        add_up(b, i, k, 0)
                        spread_c(b, i + 1, k, 2)
                        add_up(b, i, k, 1)
                        add_up(b, i, k, 2)
                for k in range(2):
                    for c in range(NCH):
                        add_up(b, n_s // 2 - 1, k, c)

            for b, c in bc:
                pe.wait_ge(s["yo"], b + 1)
                nc.tensor.matmul(pb[64 * b:64 * b + 64, c, 0:CH], chip.w("a3_wout"), chunk(u[:, b], c),
                                 start=True, stop=True).then_inc(s["wout"], 1)
            for c in range(NCH):
                pe.wait_ge(s["wout_sb"], c + 1)
                nc.tensor.matmul(pa[:, c, 0:CH], chip.w("a3_wlin"), chunk(m1, c), start=True, stop=True).then_inc(s["wlin"], 1)
            norm_tensor(chip, k_ln1, r1, s["r1"])
            for c, b in cb:
                pe.wait_ge(s["n1"], c + 1)
                nc.tensor.matmul(bank[b][:, c, 0:CH], chip.w("a3_wexp", first=128 * b, cols=128), chunk(n1, c),
                                 start=True, stop=True).then_inc(s["up"], 1)
            for c, b in cb:
                pe.wait_ge(s["up_sb"], 2 * (c + 1))
                nc.tensor.matmul(pa[64 * b:64 * b + 64, c, 0:CH], chip.w("a3_wsq"), chunk(t1[:, b], c),
                                 start=True, stop=True).then_inc(s["down"], 1)
            norm_tensor(chip, k_ln2, r1, s["r2"])

        @block.scalar
        def _(act):
            norm_scalar(chip, k_ln)
            chip.need(act, 4)
            nc.scalar.activation(an[:, :], chip.w("a3_alog"), ACT.Exp).then_inc(s["aexp"], 1)
            for n, (b, c) in enumerate(bc):
                act.wait_ge(s["xs"], n + 1)
                nc.scalar.activation(xs[:, b, 3 + c * CH:3 + (c + 1) * CH], bank[b][:, c, 0:CH], ACT.Copy
                                     ).then_inc(s["xs_sb"], 1)
            for n, (b, c) in enumerate(bc):
                act.wait_ge(s["z"], n + 1)
                nc.scalar.activation(chunk(z[:, b], c), bank[b][:, c, 0:CH], ACT.Silu).then_inc(s["z_sb"], 1)
            for b in range(NB):
                act.wait_ge(s["conv"], b + 1)
                nc.scalar.activation(xc[:, b], xc[:, b], ACT.Silu).then_inc(s["xc"], 1)
            for n, (b, c) in enumerate(bc):
                act.wait_ge(s["dbl"], n + 1)
                nc.scalar.activation(chunk(dbl[:, b], c), bank[b][0:48, c, 0:CH], ACT.Copy).then_inc(s["dbl_sb"], 1)
            for b in range(NB):
                act.wait_ge(s["dt"], NCH * (b + 1))
                nc.scalar.activation(chunks(t1[:, b]), bank[b][:, :, 0:CH], ACT.Abs, bias=chip.w("a3_bdt")).then_inc(s["abs"], 1)
            load_functions(nc, EXP_LN)
            for b in range(NB):
                act.wait_ge(s["abs"], b + 1)
                nc.scalar.activation(t1[:, b], t1[:, b], ACT.Exp, scale=-1.0).then_inc(s["exp"], 1)
            for b in range(NB):
                act.wait_ge(s["exp"], b + 1)
                nc.scalar.activation(da[:, b], t1[:, b], ACT.Ln, bias=chip.w("eps", first=2, cols=1)).then_inc(s["log"], 1)
            act.wait_ge(s["a"], 1)
            act.wait_ge(s["dt_done"], NB)
            act.sem_inc(s["c_sb"], 2)
            for b in range(NB):
                with act.Fori(0, n_s // 2) as i:
                    for k in range(2):
                        g = n_s * b + k
                        act.wait_ge(s["scan"], 2 * i + g + 1)
                        nc.scalar.activation(da[:, k], dt[:, b], ACT.Exp, scale=an[:, bass.ds(2 * i + k, 1)]
                                             ).then_inc(s["da"], 1)
                        act.wait_ge(s["prod"], 2 * i + g + 1)
                        for c in range(NCH):
                            act.wait_ge(s["c_spread"], 6 * i + 3 * g + c + 1)
                            nc.scalar.activation(chunk(cs[:, k], c), pc[:, (3 * k + c) % 2, 0:CH], ACT.Copy
                                                 ).then_inc(s["c_sb"], 1)
            for c in range(NCH):
                act.wait_ge(s["wout"], NCH + c + 1)
                nc.scalar.activation(chunk(m1, c), pb[:, c, 0:CH], ACT.Copy).then_inc(s["wout_sb"], 1)
            norm_scalar(chip, k_ln1)
            for n, (c, b) in enumerate(cb):
                act.wait_ge(s["up"], n + 1)
                nc.scalar.activation(chunk(t1[:, b], c), bank[b][:, c, 0:CH], ACT.Relu, bias=chip.w("a3_bexp")
                                     ).then_inc(s["up_sb"], 1)
            norm_scalar(chip, k_ln2)

        @block.gpsimd
        def _(pool):
            pool.sem_inc(s["prod"], 2)
            for b in range(NB):
                with pool.Fori(0, n_s // 2) as i:
                    for k in range(2):
                        g = n_s * b + k
                        pool.wait_ge(s["scan"], 2 * i + g + 1 + 2)
                        pool.wait_ge(s["c_sb"], 6 * i + 3 * g + 3 + 2)
                        pool.wait_ge(s["summed"], 2 * i + g + 1)
                        nc.gpsimd.tensor_tensor(pr[:, k], hst[:, k], cs[:, k], ALU.mult).then_inc(s["prod"], 1)

        @block.vector
        def _(v):
            steps = Steps(s["step"])
            steps.settle(v, nc.vector.memset(xs[:, :, 0:3], 0.0))
            nc.vector.memset(bcp[96:128], 0.0).then_inc(s["parts"], 1)
            norm_vector(chip, k_ln, chip.xl)
            chip.need(v, 4)
            nc.vector.tensor_scalar(ddp[:, :], chip.w("ident"), chip.w("a3_dp"), None, ALU.mult).then_inc(s["dp"], 1)
            v.wait_ge(s["aexp"], 1)
            nc.vector.tensor_scalar(an[:, :], an[:, :], -1.0, None, ALU.mult).then_inc(s["a"], 1)
            for b in range(NB):
                v.wait_ge(s["xs_sb"], NCH * (b + 1))
                steps.settle(v, nc.vector.tensor_scalar(xc[:, b], xs[:, b, 0:TP], chip.w("a3_convw", cols=1),
                                                        chip.w("a3_convb"), ALU.mult, ALU.add))
                for k in range(1, 4):
                    i = nc.vector.scalar_tensor_tensor(xc[:, b], xs[:, b, k:k + TP], chip.w("a3_convw", first=k, cols=1),
                                                       xc[:, b], ALU.mult, ALU.add)
                    if k < 3:
                        steps.settle(v, i)
                    else:
                        i.then_inc(s["conv"], 1)
            v.wait_ge(s["dbl_sb"], 2 * NCH)
            steps.settle(v, nc.vector.tensor_copy(bcp[0:32], dbl[0:32]))
            steps.settle(v, nc.vector.tensor_tensor(rem[:, :, :], dbl[0:32], bcp[0:32], ALU.subtract))
            steps.settle(v, nc.vector.tensor_copy(low[:, :, :], rem[:, :, :]))
            steps.settle(v, nc.vector.tensor_copy(bcp[32:64], low[:, :, :]))
            steps.settle(v, nc.vector.tensor_tensor(rem[:, :, :], rem[:, :, :], low[:, :, :], ALU.subtract))
            nc.vector.tensor_copy(bcp[64:96], rem[:, :, :]).then_inc(s["parts"], 1)
            for b in range(NB):
                v.wait_ge(s["abs"], b + 1)
                nc.vector.tensor_scalar(chunks(dt[:, b]), bank[b][:, :, 0:CH], chip.w("a3_bdt"), 0.0, ALU.add, ALU.max
                                        ).then_inc(s["dt_pos"], 1)
            for b in range(NB):
                e, ser, small = t1[:, b], hst[:, b], cs[:, b].bitcast(mybir.dt.uint32)
                v.wait_ge(s["exp"], b + 1)
                steps.settle(v, nc.vector.tensor_scalar(ser, e, -0.25, 1.0 / 3.0, ALU.mult, ALU.add))
                steps.settle(v, nc.vector.tensor_tensor(ser, ser, e, ALU.mult))
                for coefficient in (-0.5, 1.0):
                    steps.settle(v, nc.vector.scalar_tensor_tensor(ser, ser, coefficient, e, ALU.add, ALU.mult))
                steps.settle(v, nc.vector.tensor_scalar(small, e, SERIES_BELOW, None, ALU.is_lt))
                v.wait_ge(s["log"], b + 1)
                steps.settle(v, nc.vector.copy_predicated(da[:, b], small, ser))
                v.wait_ge(s["dt_pos"], b + 1)
                nc.vector.tensor_tensor(dt[:, b], dt[:, b], da[:, b], ALU.add).then_inc(s["dt_done"], 1)
                v.wait_ge(s["dt_done"], b + 1)
                steps.settle(v, nc.vector.tensor_tensor(u[:, b], dt[:, b], xc[:, b], ALU.mult))
            v.sem_inc(s["scan"], 2)
            v.sem_inc(s["summed"], 2)
            v.sem_inc(s["dbx"], 1)
            for b in range(NB):
                with v.Fori(0, n_s // 2) as i:
                    for k in range(2):
                        g = n_s * b + k
                        v.wait_ge(s["b_spread"], 2 * i + g + 1)
                        v.wait_ge(s["scan"], 2 * i + g + 1)
                        nc.vector.tensor_tensor(chunks(dbx[:, k]), chunks(u[:, b]), pb[:, :, 0:CH], ALU.mult
                                                ).then_inc(s["dbx"], 1)
                        v.wait_ge(s["dbx"], 2 * i + g + 2)
                        v.wait_ge(s["da"], 2 * i + g + 1)
                        v.wait_ge(s["prod"], 2 * i + g + 1)
                        nc.vector.tensor_tensor_scan(hst[:, k], da[:, k], dbx[:, k], 0.0, ALU.mult, ALU.add
                                                     ).then_inc(s["scan"], 1)
                v.wait_ge(s["summed"], n_s * (b + 1) + 2)
                nc.vector.tensor_tensor(chunks(u[:, b]), pa[:, :, 0:CH], chunks(z[:, b]), ALU.mult).then_inc(s["yo"], 1)

            for c in range(NCH):
                v.wait_ge(s["wlin"], c + 1)
                nc.vector.scalar_tensor_tensor(chunk(r1, c), pa[:, c, 0:CH], chip.w("a3_blin"), chunk(chip.xl, c),
                                               ALU.add, ALU.add).then_inc(s["r1"], 1)

            def affine1(c):
                v.wait_ge(chip.ln_out, NCH * k_ln1 + c + 1)
                nc.vector.tensor_scalar(chunk(n1, c), chunk(n1, c), chip.w("a3_g1"), chip.w("a3_b1"), ALU.mult, ALU.add
                                        ).then_inc(s["n1"], 1)

            norm_vector(chip, k_ln1, n1, affine1)
            for c in range(NCH):
                v.wait_ge(s["down"], 2 * (c + 1))
                nc.vector.scalar_tensor_tensor(chunk(r1, c), pa[:, c, 0:CH], chip.w("a3_bsq"), chunk(n1, c),
                                               ALU.add, ALU.add).then_inc(s["r2"], 1)

            def affine2(c):
                v.wait_ge(chip.ln_out, NCH * k_ln2 + c + 1)
                steps.settle(v, nc.vector.tensor_scalar(chunk(n1, c), chunk(n1, c), chip.w("a3_g2"), chip.w("a3_b2"),
                                                        ALU.mult, ALU.add))
                nc.vector.tensor_tensor(chunk(chip.h, c), chunk(chip.h, c), chunk(n1, c), ALU.add).then_inc(s["h"], 1)

            norm_vector(chip, k_ln2, n1, affine2)


def build(nc, t, out):
    with ExitStack() as ctx:
        chip = Chip(nc, ctx)
        work = [
            lambda: tokenise(chip, t["x"], t["xedge"], t["tokw"], t["cls2"], t["small"]),
            lambda: linear_attention(chip),
            lambda: experts2(chip, "f0", t["f0_slab"], 1, 8, 2, ACT.Relu, "switch"),
            lambda: row_attention(chip),
            lambda: experts2(chip, "f1", t["f1_slab"], 1, 8, 1, ACT.Gelu, "mask"),
            lambda: scan_attention(chip),
            lambda: experts3(chip, t["f2_slab"]),
            lambda: mamba(chip, t["selbc"]),
            lambda: experts2(chip, "f3", t["f3_slab"], 4, 8, 1, ACT.Relu, "logits"),
        ]
        for stage in work:
            stage()
            chip.end_stage()
        s_out = chip.sem("out_written")
        with nc.Block() as block:
            @block.sync
            def _(sp):
                sp.dma_start(out, chip.h[:, 0:NTOK]).then_inc(s_out, 16)
                sp.wait_ge(s_out, 16)



def pack(i):
    import numpy as np
    f = np.float32
    small = np.zeros((128, NSMALL), f)

    def put(name, a, row0=0):
        at, n = COL[name]
        a = np.asarray(a)
        if a.ndim == 1:
            a = a[:, None]
        assert a.shape[1] == n, (name, a.shape)
        small[row0:row0 + a.shape[0], at:at + n] = a

    def bd(w):
        w = np.asarray(w)
        z = np.zeros((2 * w.shape[0], 2 * w.shape[1]), f)
        z[:w.shape[0], :w.shape[1]] = w
        z[w.shape[0]:, w.shape[1]:] = w
        return z

    def two(v):
        return np.concatenate([np.asarray(v), np.asarray(v)])

    def one_seq(w):
        w = np.asarray(w)
        return bd(w)

    def rep(v):
        return np.tile(two(v)[None, :], (128, 1))

    k, p = np.arange(9)[:, None], np.arange(16)[None, :]
    ang = 2 * np.pi * k * p / 16
    dft = np.concatenate([np.cos(ang), -np.sin(ang)], 0) / 4
    dft = dft.reshape(18, 2, 2, 4).transpose(0, 2, 1, 3).reshape(18, 16)
    put("dft", dft.astype(f))
    put("mean", bd(np.full((64, 64), 1 / 64, f)))
    put("centre", bd(np.eye(64, dtype=f) - f(1 / 64)))
    put("eps", np.tile(np.array([[EPS, EPS * EPS, 1.0]], f), (128, 1)))
    put("ident", np.eye(128, dtype=f))
    wqkv = i["L0_attn_Wqkv"]
    put("a0_wq", bd(wqkv[:, 0:64]))
    put("a0_wk", bd(wqkv[:, 64:128]))
    put("a0_wv", bd(wqkv[:, 128:192]))
    put("a0_wproj", bd(i["L0_attn_Wproj"]))
    put("a0_wg1", bd(i["L0_attn_Wg1"]))
    put("a0_wg2", bd(i["L0_attn_Wg2"]))
    put("a0_mask", np.kron(np.eye(16), np.ones((8, 8))).astype(f))
    put("a0_g", two(i["L0_attn_ln_g"]))
    put("a0_b", two(i["L0_attn_ln_b"]))
    put("a0_bproj", two(i["L0_attn_bproj"]))
    put("a0_bg1", two(i["L0_attn_bg1"]))
    put("a0_bg2", two(i["L0_attn_bg2"]))

    def diag(v):
        return two(np.asarray(v).reshape(-1))

    def parts(b2, n):
        return np.concatenate([bd(b2)] * n, 0)

    put("f0_gate", bd(i["L0_ffn_gate_w"]))
    put("f0_gbias", rep(i["L0_ffn_gate_b"]))
    put("f0_b2", parts(i["L0_ffn_b2"], 1))
    sel = np.zeros((2, 128), f)
    sel[0, :64] = 1
    sel[1, 64:] = 1
    put("seqsel", sel, row0=32)
    put("rev8", rep(8 - np.arange(8, dtype=f)))
    put("rev6", rep(6 - np.arange(6, dtype=f)))
    shift = np.zeros((16, 16), f)
    shift[np.arange(8), 8 + np.arange(8)] = 1
    put("shift", shift)

    def dup(w):
        return np.concatenate([np.asarray(w)] * 2, 0)

    put("a1_g", diag(i["L1_attn_gamma"]))
    put("a1_b", diag(i["L1_attn_beta"]))
    put("a1_wq", dup(i["L1_attn_Wq"]))
    put("a1_wk", dup(i["L1_attn_Wk"]))
    put("a1_wv", dup(i["L1_attn_Wv"]))
    put("a1_wg", one_seq(i["L1_attn_Wg"]))
    put("a1_bg", np.asarray(i["L1_attn_bg"]).reshape(2, 128).T)
    put("a1_wo", np.asarray(i["L1_attn_Wo"]).reshape(2, 128, 64).transpose(1, 0, 2).reshape(128, 128))
    put("a1_bo", diag(i["L1_attn_bo"]))
    ones = np.ones((64, 64), f)
    put("tdiff", np.block([[ones, -ones], [-ones, ones]]))
    put("f1_gate", bd(i["L1_ffn_Wg"]))
    put("f1_gbias", rep(i["L1_ffn_bg"]))
    put("f1_b2", parts(i["L1_ffn_b2"], 1))

    inw = np.asarray(i["L2_attn_in_w"])
    put("a2_wxp", bd(inw[:64].T))
    put("a2_wres", bd(inw[64:].T))
    put("a2_bxp", diag(i["L2_attn_in_b"][:64]))
    put("a2_bres", diag(i["L2_attn_in_b"][64:]))
    put("a2_convw", dup(np.asarray(i["L2_attn_conv_w"]).reshape(64, 4)))
    put("a2_convb", diag(i["L2_attn_conv_b"]))
    put("a2_dt", bd(i["L2_attn_dt"]))
    put("a2_bw", bd(np.asarray(i["L2_attn_B_w"]).T))
    put("a2_cw", bd(np.asarray(i["L2_attn_C_w"]).T))
    put("a2_ow", bd(np.asarray(i["L2_attn_out_w"]).T))
    put("a2_ob", diag(i["L2_attn_out_b"]))
    put("a2_g", diag(i["L2_attn_gamma"]))
    put("a2_b", diag(i["L2_attn_beta"]))
    put("chmean", (np.tile(np.eye(64), (2, 2)) / (NB * NTOK)).astype(f))
    put("f2_rw1", bd(i["L2_ffn_router_w1"]))
    put("f2_rb1", diag(i["L2_ffn_router_b1"]))
    put("f2_gate", bd(i["L2_ffn_router_w2"]))
    put("f2_gbias", rep(i["L2_ffn_router_b2"]))
    put("f2_b2", parts(i["L2_ffn_expert_b3"], 3))

    win = np.asarray(i["L3_attn_W_in"])
    put("a3_win", np.concatenate([one_seq(win[:128].T), one_seq(win[128:].T)], 1))
    put("a3_convw", i["L3_attn_conv_w"])
    put("a3_convb", i["L3_attn_conv_b"])
    wx = np.asarray(i["L3_attn_W_x"])
    put("a3_wx", np.concatenate([wx[16:48], wx[:16]], 0).T)
    put("a3_wdt", np.asarray(i["L3_attn_W_dt"]).T, row0=32)
    put("a3_bdt", i["L3_attn_b_dt"])
    put("a3_alog", i["L3_attn_A_log"])
    put("a3_dp", i["L3_attn_Dp"])
    put("a3_wout", np.asarray(i["L3_attn_W_out"]).T)
    put("a3_wlin", bd(np.asarray(i["L3_attn_W_lin"]).T))
    put("a3_blin", diag(i["L3_attn_b_lin"]))
    put("a3_g1", diag(i["L3_attn_ln1_g"]))
    put("a3_b1", diag(i["L3_attn_ln1_b"]))
    put("a3_wexp", one_seq(np.asarray(i["L3_attn_W_exp"]).T))
    put("a3_bexp", i["L3_attn_b_exp"])
    put("a3_wsq", np.asarray(i["L3_attn_W_sq"]).T)
    put("a3_bsq", diag(i["L3_attn_b_sq"]))
    put("a3_g2", diag(i["L3_attn_ln2_g"]))
    put("a3_b2", diag(i["L3_attn_ln2_b"]))
    put("f3_gate", bd(i["L3_ffn_Wg"]))
    put("f3_gbias", rep(i["L3_ffn_bg"]))
    put("f3_gbias2", rep(i["L3_ffn_bias"]))

    def bf16_bits(ones_at, word=0x3F80):
        u = np.zeros(ones_at.shape, np.uint16)
        u[ones_at] = word
        return u.view(f)

    def slabs2(w1, b1, w2, b2, weighted):
        w1, b1, w2 = np.asarray(w1), np.asarray(b1), np.asarray(w2)
        e_n, _, hid = w1.shape
        hc = hid // 128
        out = np.zeros((e_n, 128, SLAB2[hc]), f)
        for e in range(e_n):
            out[e, :, 0:hid] = dup(w1[e])
            out[e, :, hid:hid + 64 * hc] = w2[e].reshape(hc, 128, 64).transpose(1, 0, 2).reshape(128, -1)
            out[e, :, hid + 64 * hc:hid + 65 * hc] = b1[e].reshape(hc, 128).T
            out[e, :, hid + 65 * hc] = diag(b2[e])
            n = hid + 65 * hc + 1
            for b in range(2):
                at = np.zeros((128, 128), bool)
                if not weighted:
                    at[b * e_n + e] = True
                    out[e, :, n + 64 * b:n + 64 * b + 64] = bf16_bits(at, BARRED_WORD)
            if weighted:
                for part in range(3):
                    for b in range(2):
                        at[part * 2 * e_n + b * e_n + e, 64 * b:64 * b + 64] = True
                out[e, :, n:n + 64] = bf16_bits(at)
        return out.transpose(1, 0, 2).reshape(128, -1)

    def slabs3(w1, b1, w2, b2, w3):
        e_n = w1.shape[0]
        out = np.zeros((e_n, 128, SLAB3), f)
        for e in range(e_n):
            for n, w in enumerate((w1, w2, w3)):
                out[e, :, 128 * n:128 * n + 128] = bd(w[e])
            out[e, :, 384] = diag(b1[e])
            out[e, :, 385] = diag(b2[e])
            at = np.zeros((128, 128), bool)
            for part in range(3):
                for b in range(2):
                    at[part * 2 * e_n + b * e_n + e, 64 * b:64 * b + 64] = True
            out[e, :, 386:450] = bf16_bits(at)
        return out

    def sel_bc():
        at = np.zeros((128, 16, 2, 128), bool)
        for s in range(16):
            for part in range(3):
                at[32 * part + s, s, 0] = True
                at[32 * part + 16 + s, s, 1] = True
        return bf16_bits(at.reshape(128, -1))

    x = np.asarray(i["x"]).reshape(2, 64, 16, 2, 4, 64).transpose(3, 1, 0, 2, 4, 5)
    edge = x[1, :, :, 15, 3, :]
    return {
        "x": x.reshape(128, 2, 16, 4, 64),
        "xedge": np.concatenate([edge, edge], 0),
        "tokw": np.asarray(i["L0_tok_W"]).reshape(64, 18, 64).transpose(1, 0, 2),
        "cls2": two(np.asarray(i["cls_tok"]).reshape(64))[:, None],
        "small": small,
        "f0_slab": slabs2(i["L0_ffn_w1"], i["L0_ffn_b1"], i["L0_ffn_w2"], i["L0_ffn_b2"], False),
        "f1_slab": slabs2(i["L1_ffn_W1"], i["L1_ffn_b1"], i["L1_ffn_W2"], i["L1_ffn_b2"], False),
        "f2_slab": slabs3(i["L2_ffn_expert_w1"], i["L2_ffn_expert_b1"], i["L2_ffn_expert_w2"],
                          i["L2_ffn_expert_b2"], i["L2_ffn_expert_w3"]),
        "f3_slab": slabs2(i["L3_ffn_W1"], i["L3_ffn_b1"], i["L3_ffn_W2"], i["L3_ffn_b2"], True),
        "selbc": sel_bc(),
    }


def kernel(**inputs):
    import numpy as np
    import concourse.bacc as bacc
    from concourse.bass_utils import run_bass_kernel_spmd

    nc = bacc.Bacc("TRN2", target_bir_lowering=False, num_devices=1)
    arrays, t = {}, {}
    for name, a in pack(inputs).items():
        a = np.ascontiguousarray(a)
        arrays[name + "_dram"] = a
        t[name] = nc.dram_tensor(name + "_dram", a.shape, mybir.dt.from_np(a.dtype), kind="ExternalInput").ap()
    out = nc.dram_tensor("out_dram", (P, NTOK), F32, kind="ExternalOutput").ap()
    build(nc, t, out)
    got = run_bass_kernel_spmd(nc, [arrays], core_ids=[0]).results[0]["out_dram"]
    return np.ascontiguousarray(got.reshape(NB, D, NTOK).transpose(0, 2, 1))
```

```python
import concourse.bass as bass
from concourse import mybir
from contextlib import ExitStack

F32 = mybir.dt.float32
BF16 = mybir.dt.bfloat16
F32R = mybir.dt.float32r
ALU = mybir.AluOpType
ACT = mybir.ActivationFunctionType
AX = mybir.AxisListType

NB = 2
D = 64
P = NB * D
NTOK = 1025
NCH, CH = 3, 342
TP = NCH * CH
NT, TT = 9, 114
NV, NN = 64, 16
CAPACITY = 321
EPS = 1e-5
LAST = NTOK - (NCH - 1) * CH
SERIES_BELOW = 2.0 ** -6

GROUPS = [
    [("dft", 16), ("mean", 128), ("centre", 128), ("eps", 3), ("ident", 128)],
    [("a0_wk", 128), ("a0_wq", 128), ("a0_wv", 128), ("a0_wproj", 128), ("a0_wg1", 32), ("a0_wg2", 128),
     ("a0_mask", 128), ("a0_g", 1), ("a0_b", 1), ("a0_bproj", 1), ("a0_bg1", 1), ("a0_bg2", 1),
     ("f0_gate", 16), ("f0_gbias", 16), ("f0_b2", 128), ("seqsel", 128), ("rev8", 16), ("rev6", 12), ("shift", 16)],
    [("a1_g", 1), ("a1_b", 1), ("a1_wq", 256), ("a1_wk", 256), ("a1_wv", 256), ("a1_wg", 512), ("a1_bg", 2),
     ("a1_wo", 128), ("a1_bo", 1), ("tdiff", 128), ("f1_gate", 16), ("f1_gbias", 16)],
    [("a2_wxp", 128), ("a2_wres", 128), ("a2_bxp", 1), ("a2_bres", 1), ("a2_convw", 4), ("a2_convb", 1),
     ("a2_dt", 32), ("a2_bw", 32), ("a2_cw", 128), ("a2_ow", 128), ("a2_ob", 1), ("a2_g", 1), ("a2_b", 1),
     ("chmean", 128), ("f2_rw1", 64), ("f2_rb1", 1), ("f2_gate", 12), ("f2_gbias", 12), ("f2_b2", 128)],
    [("a3_win", 512), ("a3_convw", 4), ("a3_convb", 1), ("a3_wx", 48), ("a3_wdt", 128), ("a3_bdt", 1),
     ("a3_alog", 16), ("a3_dp", 1), ("a3_wout", 64), ("a3_wlin", 128), ("a3_blin", 1), ("a3_g1", 1),
     ("a3_b1", 1), ("a3_wexp", 256), ("a3_bexp", 1), ("a3_wsq", 64), ("a3_bsq", 1), ("a3_g2", 1),
     ("a3_b2", 1), ("f3_gate", 16), ("f3_gbias", 16), ("f3_gbias2", 16)],
]
COL, GROUP_SPAN = {}, []
_at = 0
for _g in GROUPS:
    _from = _at
    for _name, _n in _g:
        COL[_name] = (_at, _n)
        _at += _n
    GROUP_SPAN.append((_from, _at))
NSMALL = _at

SLAB2 = {1: 128 + 64 + 1 + 1 + 64, 2: 256 + 2 * 64 + 2 + 1 + 64}
SLAB3 = 3 * 128 + 2 + 64


class Steps:

    def __init__(self, sem):
        self.sem = sem
        self.n = 0

    def mark(self, instruction):
        self.n += 1
        instruction.then_inc(self.sem, 1)
        return self.n

    def settle(self, engine, instruction):
        engine.wait_ge(self.sem, self.mark(instruction))


class Chip:

    def __init__(self, nc, ctx):
        self.nc, self.ctx = nc, ctx

        def sb(name, shape, dt=F32):
            return ctx.enter_context(nc.sbuf_tensor(name, shape, dt))

        self.small = sb("small", [128, NSMALL])
        self.h = sb("h", [P, TP])
        self.xl = sb("xl", [P, TP])
        self.sq = sb("sq", [P, TP])
        self.rs = sb("rs", [P, TP])
        self.psum = ctx.enter_context(nc.psum_tensor("psum", [128, 8, 512], F32))
        self.pa, self.pb, self.pc = self.psum[:, 0:3], self.psum[:, 3:6], self.psum[:, 6:8]
        self.small_loaded = [self.sem(f"small_loaded{g}") for g in range(len(GROUPS))]
        self.ln_centred, self.ln_square, self.ln_var = self.sem("ln_centred"), self.sem("ln_square"), self.sem("ln_var")
        self.ln_log, self.ln_rstd, self.ln_out = self.sem("ln_log"), self.sem("ln_rstd"), self.sem("ln_out")
        self.norms = 0
        self.stage_sems, self.cleared = [], []

    def sem(self, name):
        return self.nc.alloc_semaphore(name)

    def stage_sem(self, name):
        s = self.nc.alloc_semaphore(name)
        self.stage_sems.append(s)
        return s

    def end_stage(self):
        for s in self.cleared:
            self.nc.release_semaphore(s)
        for s in self.stage_sems:
            self.nc.gpsimd.sem_clear(s)
        self.cleared, self.stage_sems = self.stage_sems, []

    def next_norm(self):
        self.norms += 1
        return self.norms - 1

    def w(self, name, rows=128, first=0, cols=None, row0=0):
        at, n = COL[name]
        return self.small[row0:row0 + rows, at + first:at + first + (n - first if cols is None else cols)]

    def need(self, engine, group):
        engine.wait_ge(self.small_loaded[group], 16)


def chunk(t, c):
    return t[:, c * CH:(c + 1) * CH]


def chunks(t):
    return t.rearrange("p (c n) -> p c n", n=CH)



def norm_tensor(chip, k, src, ready=None):
    nc, pe = chip.nc, chip.nc.tensor
    for c in range(NCH):
        if ready is not None:
            pe.wait_ge(ready, c + 1)
        nc.tensor.matmul(chip.pa[:, c, 0:CH], chip.w("centre"), chunk(src, c),
                         start=True, stop=True).then_inc(chip.ln_centred, 1)
    for c in range(NCH):
        pe.wait_ge(chip.ln_square, NCH * k + c + 1)
        nc.tensor.matmul(chip.pb[:, c, 0:CH], chip.w("mean"), chunk(chip.sq, c),
                         start=True, stop=True).then_inc(chip.ln_var, 1)
    keep_clock(chip, chip.psum[:, 7], 1)


def norm_vector(chip, k, out, then=None):
    nc, v = chip.nc, chip.nc.vector
    for c in range(NCH):
        v.wait_ge(chip.ln_rstd, NCH * k + c + 1)
        nc.vector.tensor_tensor(chunk(out, c), chip.pa[:, c, 0:CH], chunk(chip.rs, c),
                                ALU.mult).then_inc(chip.ln_out, 1)
        if then is not None:
            then(c)


def keep_clock(chip, bank, n):
    for _ in range(n):
        chip.nc.tensor.matmul(bank[:, 0:CH], chip.w("ident"), chip.small[:, 0:CH], start=True, stop=True,
                              skip_group_check=True)


EXP_LN, GELU = 6, 10


def load_functions(nc, table_set):
    nc.scalar.add_instruction(mybir.InstLoadActFuncSet(
        act_func_set_id=table_set, name=nc.get_next_instruction_name(), engine=mybir.EngineType.Activation))


def norm_scalar(chip, k, twice=False, loaded=False):
    nc, a = chip.nc, chip.nc.scalar
    eps = chip.w("eps", first=1 if twice else 0, cols=1)
    if not loaded:
        load_functions(nc, EXP_LN)
    for c in range(NCH):
        a.wait_ge(chip.ln_centred, NCH * k + c + 1)
        nc.scalar.activation(chunk(chip.sq, c), chip.pa[:, c, 0:CH], ACT.Square).then_inc(chip.ln_square, 1)
    for c in range(NCH):
        a.wait_ge(chip.ln_var, NCH * k + c + 1)
        nc.scalar.activation(chunk(chip.sq, c), chip.pb[:, c, 0:CH], ACT.Ln, bias=eps,
                             scale=1.0 + EPS if twice else 1.0).then_inc(chip.ln_log, 1)
        a.wait_ge(chip.ln_log, NCH * k + c + 1)
        nc.scalar.activation(chunk(chip.rs, c), chunk(chip.sq, c), ACT.Exp,
                             scale=-0.5).then_inc(chip.ln_rstd, 1)



def tokenise(chip, x, xedge, tokw, cls2, small):
    nc = chip.nc
    with ExitStack() as ctx:
        def sb(name, shape):
            return ctx.enter_context(nc.sbuf_tensor(name, shape, F32))
        xt = sb("xt", [128, NB, NN, 4, NV])
        xe = sb("xe", [128, NB, NV])
        tw = sb("tw", [18, D, 64])
        wl = sb("wl", [128, 4, 2, D])
        s_x = [[chip.stage_sem(f"x_loaded{b}{j}") for j in range(2)] for b in range(NB)]
        s_e, s_w, s_cls = chip.stage_sem("edge_loaded"), chip.stage_sem("tokw_loaded"), chip.stage_sem("cls_loaded")
        s_wp, s_wl = chip.stage_sem("patch_matrix"), chip.stage_sem("patch_matrix_sb")
        s_conv, s_edge, s_lo, s_hi = (chip.stage_sem("tok_conv"), chip.stage_sem("tok_edge"), chip.stage_sem("tok_low"),
                                      chip.stage_sem("tok_high"))
        pw = chip.psum[:, 7, :]
        pe_edge = chip.psum[:, 6, 0:NB * NV]
        block = ctx.enter_context(nc.Block())

        @block.sync
        def _(sp):
            sp.dma_start(tw[:, :, :], tokw).then_inc(s_w, 16)
            a, z = GROUP_SPAN[0]
            sp.dma_start(chip.small[:, a:z], small[:, a:z]).then_inc(chip.small_loaded[0], 16)
            for b in range(NB):
                for j in range(2):
                    sp.dma_start(xt[:, b, 8 * j:8 * j + 8], x[:, b, 8 * j:8 * j + 8]).then_inc(s_x[b][j], 16)
            for g in range(1, len(GROUPS)):
                a, z = GROUP_SPAN[g]
                sp.dma_start(chip.small[:, a:z], small[:, a:z]).then_inc(chip.small_loaded[g], 16)

        @block.scalar
        def _(act):
            act.dma_start(xe[:, :, :], xedge).then_inc(s_e, 16)
            act.dma_start(chip.h[:, 0:1], cls2).then_inc(s_cls, 16)
            for b in range(NB):
                hv = chip.h[64 * b:64 * b + 64, 1:NTOK].rearrange("p (v n) -> p n v", n=NN)
                for j in range(2):
                    act.wait_ge(s_conv, 2 * b + j + 1)
                    nc.scalar.activation(hv[:, 8 * j:8 * j + 8, :],
                                         chip.psum[0:64, 2 * b + j, :].rearrange("p (m v) -> p m v", v=NV),
                                         ACT.Copy).then_inc(s_lo, 1)

        @block.tensor
        def _(pe):
            pe.wait_ge(s_w, 16)
            chip.need(pe, 0)
            dft = chip.w("dft", rows=18)
            for k in range(D // 2):
                last = nc.tensor.matmul(pw[:, 16 * k:16 * k + 16], tw[:, 2 * k:2 * k + 2, :].rearrange("p d c -> p (d c)"),
                                        dft, start=True, stop=True)
            last.then_inc(s_wp, 1)
            pe.wait_ge(s_wl, 4)
            pe.wait_ge(s_e, 16)
            for r in range(4):
                last = nc.tensor.matmul(pe_edge, wl[:, r].rearrange("p t d -> p (t d)"),
                                        xe[:, :, :].rearrange("p b v -> p (b v)"), start=(r == 0), stop=(r == 3))
            last.then_inc(s_edge, 1)
            for b in range(NB):
                for j in range(2):
                    pe.wait_ge(s_x[b][j], 16)
                    for r in range(4):
                        last = nc.tensor.matmul(chip.psum[:, 2 * b + j, :], wl[:, r].rearrange("p t d -> p (t d)"),
                                                xt[:, b, 8 * j:8 * j + 8, r, :], start=(r == 0), stop=(r == 3))
                    last.then_inc(s_conv, 1)

        @block.vector
        def _(v):
            nc.vector.memset(chip.h[:, NTOK:TP], 0.0).then_inc(s_hi, 1)
            v.wait_ge(s_wp, 1)
            for odd in range(2):
                of_parity = wl[:, :, :, :].rearrange("p r t (k two) -> p two t r k", two=2)
                for half in range(2):
                    nc.vector.tensor_copy(
                        of_parity[64 * half:64 * half + 64, odd],
                        pw[64 * odd:64 * odd + 64, :].rearrange("p (k h t r) -> p h t r k", h=2, t=2, r=4)[:, half]
                    ).then_inc(s_wl, 1)
            for b in range(NB):
                hv = chip.h[64 * b:64 * b + 64, 1:NTOK].rearrange("p (v n) -> p n v", n=NN)
                v.wait_ge(s_lo, 2 * b + 2)
                for n0, n1, src in ((0, 7, chip.psum[64:128, 2 * b, NV:8 * NV]),
                                    (7, 15, chip.psum[64:128, 2 * b + 1, :])):
                    nc.vector.tensor_tensor(hv[:, n0:n1, :], src.rearrange("p (m v) -> p m v", v=NV),
                                            hv[:, n0:n1, :], ALU.add).then_inc(s_hi, 1)
                v.wait_ge(s_edge, 1)
                nc.vector.tensor_tensor(hv[:, 15, :], pe_edge[64:128, NV * b:NV * b + NV], hv[:, 15, :],
                                        ALU.add).then_inc(s_hi, 1)
            v.wait_ge(s_cls, 16)



def linear_attention(chip):
    nc = chip.nc
    k_ln = chip.next_norm()
    with ExitStack() as ctx:
        def sb(name, shape):
            return ctx.enter_context(nc.sbuf_tensor(name, shape, F32))
        xn, ke, q, g = sb("xn", [P, TP]), sb("ke", [P, TP]), sb("q", [P, TP]), sb("g", [P, TP])
        vt, kt = sb("vt", [TT, NT, 128]), sb("kt", [TT, NT, 128])
        hg = sb("hg", [32, TP])
        kmax, nmax, ksum, kinv = sb("kmax", [P, NCH]), sb("nmax", [P, 1]), sb("ksum", [P, NCH]), sb("kinv", [P, 2])
        rs2, sq2, xc = sb("rs2", [P, TP]), sb("sq2", [P, TP]), sb("centred", [P, TP])
        cx = sb("cx", [P, 128])
        (s_r2, s_k, s_xn, s_g1, s_hg, s_g2, s_v, s_vt, s_nmax, s_ke, s_q, s_qs, s_kt, s_kts, s_cx, s_cxs, s_o,
         s_og, s_p) = (chip.stage_sem("a0_" + n) for n in (
             "rstd2", "k", "xn", "gate1", "gate1_act", "gate2", "v", "v_sb", "neg_max", "kexp", "q", "q_sb",
             "kt", "kt_sb", "context", "context_sb", "out", "gated", "proj"))
        s_step = chip.stage_sem("a0_dve_step")
        s_gate = chip.stage_sem("a0_gate")
        s_log2 = chip.stage_sem("a0_log2")
        block = ctx.enter_context(nc.Block())
        pa, pb, pc = chip.pa, chip.pb, chip.pc

        @block.tensor
        def _(pe):
            norm_tensor(chip, k_ln, chip.h)
            chip.need(pe, 1)
            for c in range(NCH):
                pe.wait_ge(chip.ln_out, NCH * k_ln + c + 1)
                nc.tensor.matmul(pa[:, c, 0:CH], chip.w("a0_wk"), chunk(chip.xl, c), start=True, stop=True).then_inc(s_k, 1)
            keep_clock(chip, pc[:, 1], 2)
            pe.wait_ge(s_r2, NCH)
            for j in range(NT):
                last = nc.tensor.matmul(pb[0:TT, j // 3, 128 * (j % 3):128 * (j % 3) + 128],
                                        chip.xl[:, TT * j:TT * j + TT], chip.w("a0_wv"), start=True, stop=True)
            last.then_inc(s_v, 1)
            for c in range(NCH):
                pe.wait_ge(s_xn, c + 1)
                if c == 2:
                    pe.wait_ge(s_hg, 1)
                nc.tensor.matmul(pc[0:32, c % 2, 0:CH], chip.w("a0_wg1"), chunk(xn, c), start=True,
                                 stop=True).then_inc(s_g1, 1)
            pe.wait_ge(s_ke, NCH)
            for c in range(NCH):
                nc.tensor.matmul(pa[:, c, 0:CH], chip.w("a0_wq"), chunk(chip.xl, c), start=True,
                                 stop=True).then_inc(s_q, 1)
            pe.wait_ge(s_vt, 1)
            for j in range(NT):
                last = nc.tensor.transpose(pb[0:TT, j // 3, 128 * (j % 3):128 * (j % 3) + 128],
                                           ke[:, TT * j:TT * j + TT], chip.w("ident"))
            last.then_inc(s_kt, 1)
            for c in range(NCH):
                pe.wait_ge(s_hg, NCH)
                if c == 2:
                    pe.wait_ge(s_qs, NCH)
                    keep_clock(chip, pa[:, 0], 3)
                    pe.wait_ge(s_gate, 1)
                nc.tensor.matmul(pc[:, c % 2, 0:CH], chip.w("a0_wg2", rows=32), hg[:, c * CH:(c + 1) * CH],
                                 start=True, stop=True).then_inc(s_g2, 1)
            pe.wait_ge(s_kts, 1)
            pe.wait_ge(s_gate, NCH)
            for j in range(NT):
                last = nc.tensor.matmul(pc[:, 0, 0:128], kt[:, j, :], vt[:, j, :], start=(j == 0), stop=(j == NT - 1))
            last.then_inc(s_cx, 1)
            pe.wait_ge(s_cxs, 1)
            pe.wait_ge(s_qs, NCH)
            for c in range(NCH):
                nc.tensor.matmul(pa[:, c, 0:CH], cx[:, :], chunk(q, c), start=True, stop=True).then_inc(s_o, 1)
            for c in range(NCH):
                pe.wait_ge(s_og, c + 1)
                nc.tensor.matmul(pb[:, c, 0:CH], chip.w("a0_wproj"), chunk(ke, c), start=True, stop=True).then_inc(s_p, 1)

        @block.scalar
        def _(act):
            norm_scalar(chip, k_ln)
            for c in range(NCH):
                nc.scalar.activation(chunk(sq2, c), pb[:, c, 0:CH], ACT.Ln, bias=chip.w("eps", first=1, cols=1),
                                     scale=1.0 + EPS).then_inc(s_log2, 1)
                act.wait_ge(s_log2, c + 1)
                nc.scalar.activation(chunk(rs2, c), chunk(sq2, c), ACT.Exp, scale=-0.5).then_inc(s_r2, 1)
            act.wait_ge(s_nmax, 1)
            for c in range(NCH):
                n = LAST if c == NCH - 1 else CH
                nc.scalar.activation(ke[:, c * CH:c * CH + n], pa[:, c, 0:n], ACT.Exp, bias=nmax[:, :],
                                     accum_out=ksum[:, c:c + 1]).then_inc(s_ke, 1)
            for c in range(NCH):
                act.wait_ge(s_g1, c + 1)
                nc.scalar.activation(hg[:, c * CH:(c + 1) * CH], pc[0:32, c % 2, 0:CH], ACT.Gelu,
                                     bias=chip.w("a0_bg1", rows=32)).then_inc(s_hg, 1)
            act.wait_ge(s_kt, 1)
            nc.scalar.activation(kt[:, :, :].rearrange("p (c j) n -> p c j n", c=3), pb[0:TT, :, 0:384].rearrange("p c (j n) -> p c j n", n=128),
                                 ACT.Copy).then_inc(s_kts, 1)
            for c in range(NCH):
                act.wait_ge(s_g2, c + 1)
                nc.scalar.activation(chunk(g, c), pc[:, c % 2, 0:CH], ACT.Sigmoid,
                                     bias=chip.w("a0_bg2")).then_inc(s_gate, 1)

        @block.vector
        def _(v):
            steps = Steps(s_step)
            for c in range(NCH):
                v.wait_ge(chip.ln_square, NCH * k_ln + c + 1)
                last = steps.mark(nc.vector.tensor_copy(chunk(xc, c), pa[:, c, 0:CH]))
            norm_vector(chip, k_ln, chip.xl)
            chip.need(v, 1)
            v.wait_ge(s_step, last)
            for c in range(NCH):
                v.wait_ge(s_k, c + 1)
                n = LAST if c == NCH - 1 else CH
                last = steps.mark(nc.vector.reduce_max(kmax[:, c:c + 1], pa[:, c, 0:n], AX.X))
            v.wait_ge(s_step, last)
            nc.vector.tensor_reduce(nmax[:, :], kmax[:, :], AX.X, ALU.max, negate=True).then_inc(s_nmax, 1)
            for c in range(NCH):
                v.wait_ge(s_r2, c + 1)
                steps.settle(v, nc.vector.tensor_tensor(chunk(xn, c), chunk(xc, c), chunk(rs2, c), ALU.mult))
                nc.vector.tensor_scalar(chunk(xn, c), chunk(xn, c), chip.w("a0_g"), chip.w("a0_b"),
                                        ALU.mult, ALU.add).then_inc(s_xn, 1)
            nc.vector.memset(ke[:, NTOK:TP], 0.0).then_inc(s_ke, 1)
            v.wait_ge(s_v, 1)
            nc.vector.tensor_copy(vt[:, :, :].rearrange("p (c j) n -> p c j n", c=3), pb[0:TT, :, 0:384].rearrange("p c (j n) -> p c j n", n=128)
                                  ).then_inc(s_vt, 1)
            v.wait_ge(s_ke, NCH + 1)
            steps.settle(v, nc.vector.reduce_sum(kinv[:, 0:1], ksum[:, :], AX.X))
            steps.settle(v, nc.vector.reciprocal(kinv[:, 1:2], kinv[:, 0:1]))
            for c in range(NCH):
                v.wait_ge(s_q, c + 1)
                nc.vector.tensor_copy(chunk(q, c), pa[:, c, 0:CH]).then_inc(s_qs, 1)
            v.wait_ge(s_cx, 1)
            nc.vector.scalar_tensor_tensor(cx[:, :], pc[:, 0, 0:128], kinv[:, 1:2], chip.w("a0_mask"),
                                           ALU.mult, ALU.mult).then_inc(s_cxs, 1)
            for c in range(NCH):
                v.wait_ge(s_o, c + 1)
                v.wait_ge(s_gate, NCH)
                nc.vector.tensor_tensor(chunk(ke, c), pa[:, c, 0:CH], chunk(g, c), ALU.mult).then_inc(s_og, 1)
            for c in range(NCH):
                v.wait_ge(s_p, c + 1)
                nc.vector.scalar_tensor_tensor(chunk(chip.h, c), pb[:, c, 0:CH], chip.w("a0_bproj"),
                                               chunk(chip.h, c), ALU.add, ALU.add).then_inc(s_step, 1)



def route_vector(chip, steps, r, kind, n_e, group_bias2, s):
    nc, v = chip.nc, chip.nc.vector
    e2 = 2 * n_e
    lg, eq, cand, o1, o2 = r["lg"], r["eq"], r["cand"], r["o1"], r["o2"]
    m1, m2, mm, ssum, w1, w2, dd = (r[x] for x in ("m1", "m2", "mm", "ssum", "w1", "w2", "dd"))

    def by_tile(t):
        return t[:, :, :].rearrange("p (j b) e -> p j (b e)", b=2)

    def over_tiles(row):
        return row[0:TT].unsqueeze(1).to_broadcast([TT, NT, e2])

    def over_experts(m):
        return m[:, :].unsqueeze(2).to_broadcast([TT, 2 * NT, n_e])

    def first_best(src, best, one_hot):
        steps.settle(v, nc.vector.tensor_reduce(best[:, :], src[:, :, :], AX.X, ALU.max))
        steps.settle(v, nc.vector.tensor_tensor(eq[:, :, :], src[:, :, :], over_experts(best), ALU.is_equal))
        steps.settle(v, nc.vector.tensor_tensor(by_tile(cand), by_tile(eq), over_tiles(chip.w(f"rev{n_e}")), ALU.mult))
        steps.settle(v, nc.vector.tensor_reduce(mm[:, :], cand[:, :, :], AX.X, ALU.max))
        steps.settle(v, nc.vector.tensor_tensor(one_hot[:, :, :], cand[:, :, :], over_experts(mm), ALU.is_equal))

    v.wait_ge(s["logits"], 1)
    steps.settle(v, nc.vector.tensor_tensor(
        by_tile(lg), chip.pc[0:TT, 1, 0:NT * e2].rearrange("p (j n) -> p j n", n=e2),
        over_tiles(chip.w(r["name"] + "_gbias")), ALU.add))
    if group_bias2:
        steps.settle(v, nc.vector.tensor_tensor(by_tile(lg), by_tile(lg), over_tiles(chip.w(r["name"] + "_gbias2")), ALU.add))
    first_best(lg, m1, o1)
    tg = r["tg"]

    def spread():
        nc.vector.tensor_tensor(r["d"][:, :, :], lg[:, :, :], over_experts(m1), ALU.subtract).then_inc(s["d"], 1)

    if kind == "switch":
        spread()
        nc.vector.memset(tg[:, :, e2:32], 0.0).then_inc(s["gates"], 1)
        nc.vector.tensor_copy(tg[:, :, 0:e2], by_tile(o1)).then_inc(s["gates"], 1)
        v.wait_ge(s["exp"], 1)
        steps.settle(v, nc.vector.tensor_reduce(ssum[:, :], r["ex"][:, :, :], AX.X, ALU.add))
        steps.settle(v, nc.vector.reciprocal(w1[:, :], ssum[:, :]))
        nc.vector.tensor_copy(tg[:, :, 32:34], w1[:, :].rearrange("p (j b) -> p j b", b=2)).then_inc(s["gates"], 1)
        return 3
    steps.settle(v, nc.vector.scalar_tensor_tensor(r["lg2"][:, :, :], o1[:, :, :], -1e30, lg[:, :, :], ALU.mult, ALU.add))
    first_best(r["lg2"], m2, o2)
    if kind == "mask":
        nc.vector.tensor_tensor(tg[:, :, 0:e2], by_tile(o1), by_tile(o2), ALU.add).then_inc(s["gates"], 1)
        return 1
    steps.settle(v, nc.vector.tensor_tensor(dd[:, 0:2 * NT], m2[:, :], m1[:, :], ALU.subtract))
    if kind == "probs":
        spread()
        nc.vector.tensor_copy(dd[:, 2 * NT:4 * NT], dd[:, 0:2 * NT]).then_inc(s["d"], 1)
        v.wait_ge(s["exp"], 2)
        steps.settle(v, nc.vector.tensor_reduce(ssum[:, :], r["ex"][:, :, :], AX.X, ALU.add))
        steps.settle(v, nc.vector.reciprocal(w1[:, :], ssum[:, :]))
        steps.settle(v, nc.vector.tensor_scalar(dd[:, 0:2 * NT], dd[:, 2 * NT:4 * NT], 1.0, None, ALU.subtract))
        nc.vector.tensor_tensor(r["gap"][:, :], dd[:, 0:2 * NT], w1[:, :], ALU.mult).then_inc(s["gap"], 1)
    else:
        nc.vector.tensor_copy(r["gap"][:, :], dd[:, 0:2 * NT]).then_inc(s["gap"], 1)
    v.wait_ge(s["weights"], 2)
    steps.settle(v, nc.vector.tensor_tensor(o1[:, :, :], o1[:, :, :], over_experts(r["s1"]), ALU.mult))
    steps.settle(v, nc.vector.tensor_tensor(o2[:, :, :], o2[:, :, :], over_experts(r["s2"]), ALU.mult))
    steps.settle(v, nc.vector.tensor_tensor(o1[:, :, :], o1[:, :, :], o2[:, :, :], ALU.add))
    for part in range(3):
        at = tg[:, :, part * e2:part * e2 + e2]
        steps.settle(v, nc.vector.tensor_copy(r["low"][:, :, :], by_tile(o1)))
        copied = nc.vector.tensor_copy(at, r["low"][:, :, :])
        if part == 2:
            copied.then_inc(s["gates"], 1)
        else:
            steps.settle(v, copied)
            steps.settle(v, nc.vector.tensor_tensor(by_tile(o1), by_tile(o1), at, ALU.subtract))
    return 1


def route_scalar(chip, r, kind, s):
    nc, act = chip.nc, chip.nc.scalar
    if kind in ("switch", "probs"):
        act.wait_ge(s["d"], 1)
        nc.scalar.activation(r["ex"][:, :, :], r["d"][:, :, :], ACT.Exp).then_inc(s["exp"], 1)
    if kind == "probs":
        act.wait_ge(s["d"], 2)
        nc.scalar.activation(r["dd"][:, 2 * NT:4 * NT], r["dd"][:, 2 * NT:4 * NT], ACT.Exp).then_inc(s["exp"], 1)
    if kind in ("probs", "logits"):
        act.wait_ge(s["gap"], 1)
        nc.scalar.activation(r["s1"][:, :], r["gap"][:, :], ACT.Sigmoid, scale=-1.0).then_inc(s["weights"], 1)
        nc.scalar.activation(r["s2"][:, :], r["gap"][:, :], ACT.Sigmoid).then_inc(s["weights"], 1)


def route_tiles(chip, sb, name, n_e, n_rows):
    r = {x: sb(name + x, [TT, 2 * NT, n_e]) for x in ("lg", "lg2", "eq", "cand", "o1", "o2", "d", "ex")}
    r.update({x: sb(name + x, [TT, 2 * NT]) for x in ("m1", "m2", "mm", "ssum", "w1", "w2", "s1", "s2", "gap")})
    r["dd"] = sb(name + "dd", [TT, 4 * NT])
    r["low"] = sb(name + "low", [TT, NT, 2 * n_e], BF16)
    r["tg"] = sb(name + "tg", [TT, NT, n_rows])
    r["rows"] = sb(name + "rows", [n_rows, TP])
    r["rows16"] = sb(name + "rows16", [128, TP], BF16)
    r["name"] = name
    return r


ROUTE_FILL = {"switch": 6, "mask": 7, "probs": 14, "logits": 14}
HS_RING = 3
LEAD = 2


def experts2(chip, name, slab, group, n_e, hc, func, kind, out=None):
    nc = chip.nc
    k_ln = chip.next_norm()
    hid = 128 * hc
    nu = NCH * hc
    pairs = n_e // 2
    e2 = 2 * n_e
    nq = 2 * NCH
    switch = kind == "switch"
    k_rows = 3 * e2 if kind == "logits" else e2
    n_rows = 34 if switch else k_rows
    with ExitStack() as ctx:
        def sb(nm, shape, dt=F32):
            return ctx.enter_context(nc.sbuf_tensor(nm, shape, dt))
        wide = SLAB2[hc]
        ws = sb(name + "slab", [128, n_e * wide])
        wsp = sb(name + "wsplit", [128, 2, 2, hid], F32R)
        second_w = sb(name + "second_w", [128, 2, 65 * hc + 1])
        xsp = sb(name + "xsplit", [128, NB, TP], F32R)
        hs = sb(name + "hs", [128, HS_RING, NB, CH])
        gs, ge = sb(name + "gs", [P, HS_RING, CH]), sb(name + "ge", [P, 2, CH])
        r = route_tiles(chip, sb, name, n_e, n_rows)
        s = {x: chip.stage_sem(name + "_" + x) for x in
             ("logits", "d", "exp", "gap", "weights", "gates", "rows", "rows_sb", "total", "high", "low",
              "wsplit", "wsplit_high", "first", "act", "second", "zero", "slab", "w2", "spread", "spread_sb",
              "scaled", "added", "const", "const_sb", "pick", "written", "done", "step")}
        if switch:
            cnt, zero, thr = sb("cnt", [e2, TP]), sb("zero", [e2, TP]), sb("thr", [e2, 1])
            picked, yp, yn, bias = (sb("switch" + x, [P, TP]) for x in ("picked", "positive", "clipped", "bias"))
            probs = sb("probs", [P, TP])
            mk = sb("mk", [P, TP], mybir.dt.uint32)
        block = ctx.enter_context(nc.Block())
        pa, pb, pc = chip.pa, chip.pb, chip.pc
        n_gates = 3 if switch else 1
        hidden = [chip.psum[:, 3:5], chip.psum[:, 5:7]]
        gate_bank = [chip.psum[:, 2], chip.psum[:, 7]]
        const_bank = [chip.psum[:, n] for n in (0, 1, 2, 7, 0, 1)]

        def of_expert(i, k, first, n):
            return ws[:, bass.ds(i * (2 * wide) + (k * wide + first), n)]

        def col(k, n):
            return second_w[:, k, 64 * hc + n:64 * hc + n + 1]

        def sel(i, k):
            n = hid + 65 * hc + 1
            return ws[:, :].bitcast(BF16)[:, bass.ds(i * (4 * wide) + 2 * (k * wide + n), 128)]

        def unit(n):
            k, m = divmod(n, nu)
            return (k, *divmod(m, hc))

        @block.sync
        def _(sp):
            sp.dma_start(ws[:, :], slab).then_inc(s["slab"], 16)
            if out is not None:
                for c in range(NCH):
                    n = LAST if c == NCH - 1 else CH
                    sp.wait_ge(s["added"], nq * pairs - NCH + c + 1 + 2)
                    sp.dma_start(out[:, c * CH:c * CH + n], chip.h[:, c * CH:c * CH + n]).then_inc(s["written"], 16)
                sp.wait_ge(s["written"], 16 * NCH)

        @block.tensor
        def _(pe):
            norm_tensor(chip, k_ln, chip.h)
            chip.need(pe, group)
            for j in range(NT):
                if j % 3 == 0:
                    pe.wait_ge(chip.ln_out, NCH * k_ln + j // 3 + 1)
                last = nc.tensor.matmul(pc[0:TT, 1, e2 * j:e2 * j + e2], chip.xl[:, TT * j:TT * j + TT],
                                        chip.w(name + "_gate"), start=True, stop=True)
            last.then_inc(s["logits"], 1)
            keep_clock(chip, chip.psum[:, 6], ROUTE_FILL[kind])
            pe.wait_ge(s["gates"], n_gates)
            for j in range(NT):
                last = nc.tensor.transpose(pb[0:n_rows, j // 3, TT * (j % 3):TT * (j % 3) + TT], r["tg"][:, j, :],
                                           chip.w("ident", rows=TT, cols=TT))
            last.then_inc(s["rows"], 1)
            keep_clock(chip, chip.psum[:, 2], 6 if switch else 4)
            if switch:
                pe.wait_ge(s["total"], 1)
                nc.tensor.matmul(pc[0:e2, 0, 0:1], chip.w("shift", rows=e2), cnt[:, NTOK - 1:NTOK],
                                 start=True, stop=True).then_inc(s["total"], 1)
                keep_clock(chip, chip.psum[:, 2], 4)
            pe.wait_ge(s["rows_sb"], 2 if switch else 1)
            pe.wait_ge(s["low"], NB)

            if switch:
                for n in range(2 * NCH):
                    c = n % NCH
                    if n > NCH:
                        pe.wait_ge(s["const_sb"], n - NCH)
                    if n < NCH:
                        rows, weights = r["rows"][32:34, c * CH:(c + 1) * CH], chip.w("seqsel", rows=2, row0=32)
                    else:
                        rows, weights = chunk(r["rows"][0:k_rows], c), chip.w(name + "_b2", rows=k_rows)
                    nc.tensor.matmul(const_bank[n][:, 0:CH], weights, rows, start=True, stop=True).then_inc(s["const"], 1)
                pe.wait_ge(s["const_sb"], 2 * NCH)

            def first(i, n):
                k, c, h = unit(n % (2 * nu))
                i, m = i + n // (2 * nu), n % (2 * nu)
                if m % nu == 0:
                    pe.wait_ge(s["wsplit"], 2 * i + k + 1)
                pe.wait_ge(s["act"], 2 * nu * i + m + 1)
                for b in range(NB):
                    out = hidden[m % 2][:, b, 0:CH]
                    for part in range(2):
                        last = nc.tensor.matmul(out, wsp[:, k, part, 128 * h:128 * h + 128], chunk(xsp[:, b], c),
                                                start=(part == 0), stop=(part == 1))
                last.then_inc(s["first"], 1)
                if h == 0:
                    q = m // hc
                    pe.wait_ge(s["spread_sb"], nq * i + q + 1)
                    nc.tensor.matmul(gate_bank[q % 2][:, 0:CH], sel(i, k), chunk(r["rows16"], c),
                                     start=True, stop=True).then_inc(s["spread"], 1)

            def second(i, n):
                k, c, h = unit(n)
                q = n // hc
                if n % nu == 0:
                    pe.wait_ge(s["w2"], 2 * i + k + 1)
                if h == 0:
                    pe.wait_ge(s["scaled"], nq * i + q + 1 + (HS_RING - 2))
                pe.wait_ge(s["act"], 2 * nu * i + n + 1 + LEAD)
                for b in range(NB):
                    last = nc.tensor.matmul(pa[64 * b:64 * b + 64, q % 2, 0:CH], second_w[:, k, 64 * h:64 * h + 64],
                                            hs[:, n % HS_RING, b, :], start=(h == 0), stop=(h == hc - 1),
                                            skip_group_check=True)
                last.then_inc(s["second"], 1)

            def pair(i, last_pair):
                for n in range(2 * nu):
                    if not (last_pair and n + LEAD >= 2 * nu):
                        first(i, n + LEAD)
                    second(i, n)

            for n in range(LEAD):
                first(0, n)
            with pe.Fori(0, pairs - 1) as i:
                pair(i, False)
            pair(pairs - 1, True)
            if switch:
                keep_clock(chip, chip.psum[:, 6], 14)

        @block.scalar
        def _(act):
            norm_scalar(chip, k_ln)
            act.wait_ge(chip.ln_out, NCH * (k_ln + 1))
            for b in range(NB):
                half = slice(64 * b, 64 * b + 64)
                nc.scalar.activation(xsp[half, b], chip.xl[half, :], ACT.Copy).then_inc(s["high"], 1)
            route_scalar(chip, r, kind, s)
            if switch:
                for n in range(2 * NCH):
                    act.wait_ge(s["const"], n + 1)
                    nc.scalar.activation(chunk(probs if n < NCH else bias, n % NCH), const_bank[n][:, 0:CH], ACT.Copy
                                         ).then_inc(s["const_sb"], 1)
            act.sem_inc(s["act"], LEAD)
            act.sem_inc(s["spread_sb"], 2)
            if func == ACT.Gelu:
                load_functions(nc, GELU)
            with act.Fori(0, pairs) as i:
                for n in range(2 * nu):
                    k, c, h = unit(n)
                    if h == 0:
                        q = n // hc
                        act.wait_ge(s["spread"], nq * i + q + 1)
                        act.wait_ge(s["scaled"], nq * i + q + 1)
                        nc.scalar.activation(gs[:, q % HS_RING], gate_bank[q % 2][:, 0:CH], ACT.Copy
                                             ).then_inc(s["spread_sb"], 1)
                    if n % nu == 0:
                        act.wait_ge(s["w2"], 2 * i + k + 1)
                    act.wait_ge(s["first"], 2 * nu * i + n + 1 + 2 * nu)
                    act.wait_ge(s["second"], 2 * nu * i + n + 1 + (2 * nu - HS_RING))
                    nc.scalar.activation(hs[:, n % HS_RING], hidden[n % 2][:, :, 0:CH], func,
                                         bias=col(k, h)).then_inc(s["act"], 1)
        @block.gpsimd
        def _(pool):
            zeroed = [r["rows16"]] + ([zero, picked] if switch else [])
            for n, t in enumerate(zeroed):
                nc.gpsimd.memset(t[:, :], 0.0).then_inc(s["zero"], 1)
                pool.wait_ge(s["zero"], n + 1)
            for b in range(NB):
                pool.wait_ge(s["high"], b + 1)
                own, other = slice(64 * b, 64 * b + 64), slice(64 - 64 * b, 128 - 64 * b)
                nc.gpsimd.tensor_tensor(xsp[other, b], chip.xl[own, :], xsp[own, b].bitcast(F32),
                                        ALU.subtract).then_inc(s["low"], 1)

        @block.vector
        def _(v):
            steps = Steps(s["step"])
            norm_vector(chip, k_ln, chip.xl)
            chip.need(v, group)
            assert route_vector(chip, steps, r, kind, n_e, name == "f3", s) == n_gates
            v.wait_ge(s["rows"], 1)
            v.wait_ge(s["zero"], 3 if switch else 1)
            if switch:
                steps.settle(v, nc.vector.tensor_copy(chunks(r["rows"][0:34]), pb[0:34, :, 0:CH]))
                steps.settle(v, nc.vector.tensor_tensor_scan(cnt[:, :], r["rows"][0:e2, :], zero[:, :], 0.0, ALU.add, ALU.add))
                v.sem_inc(s["total"], 1)
                v.wait_ge(s["total"], 2)
                steps.settle(v, nc.vector.tensor_scalar(thr[:, :], pc[0:e2, 0, 0:1], -1.0, float(CAPACITY), ALU.mult, ALU.add))
                steps.settle(v, nc.vector.scalar_tensor_tensor(cnt[:, :], cnt[:, :], thr[:, :], r["rows"][0:e2, :],
                                                               ALU.is_le, ALU.mult))
                nc.vector.tensor_copy(r["rows"][0:e2, :], cnt[:, :]).then_inc(s["rows_sb"], 1)
                nc.vector.tensor_copy(r["rows16"][0:e2, :], cnt[:, :]).then_inc(s["rows_sb"], 1)
            else:
                nc.vector.tensor_copy(chunks(r["rows16"][0:k_rows]), pb[0:k_rows, :, 0:CH]).then_inc(s["rows_sb"], 1)
            v.sem_inc(s["second"], 2 * nu)
            v.sem_inc(s["first"], 2 * nu)
            v.sem_inc(s["scaled"], HS_RING)
            v.sem_inc(s["added"], 2)
            v.wait_ge(s["slab"], 16)

            def split_weights(i, k):
                v.wait_ge(s["first"], 2 * nu * i + (k + 1) * nu)
                nc.vector.tensor_copy(wsp[:, k, 0], of_expert(i, k, 0, hid)).then_inc(s["wsplit_high"], 1)
                v.wait_ge(s["wsplit_high"], 2 * i + k + 1)
                nc.vector.tensor_tensor(wsp[:, k, 1], of_expert(i, k, 0, hid), wsp[:, k, 0].bitcast(F32),
                                        ALU.subtract).then_inc(s["wsplit"], 1)
                v.wait_ge(s["second"], 2 * nu * i + (k + 1) * nu)
                nc.vector.tensor_copy(second_w[:, k], of_expert(i, k, hid, 65 * hc + 1)).then_inc(s["w2"], 1)

            def gated(i, q):
                k, c = divmod(q, NCH)
                v.wait_ge(s["second"], 2 * nu * i + hc * (q + 1) + 2 * nu)
                v.wait_ge(s["spread_sb"], nq * i + q + 1 + 2)
                if switch:
                    v.wait_ge(s["scaled"], nq * i + q + 1)
                    v.sem_inc(s["pick"], 1)
                    nc.vector.copy_predicated(chunk(picked, c), gs[:, q % HS_RING].bitcast(mybir.dt.uint32),
                                              pa[:, q % 2, 0:CH]).then_inc(s["scaled"], 1)
                    return
                v.wait_ge(s["added"], nq * i + q + 1)
                nc.vector.scalar_tensor_tensor(ge[:, q % 2], pa[:, q % 2, 0:CH], col(k, hc), gs[:, q % HS_RING],
                                               ALU.add, ALU.mult).then_inc(s["scaled"], 1)
                v.wait_ge(s["scaled"], nq * i + q + 1 + HS_RING)
                nc.vector.tensor_tensor(chunk(chip.h, c), chunk(chip.h, c), ge[:, q % 2], ALU.add
                                        ).then_inc(s["added"], 1)

            split_weights(0, 0)
            split_weights(0, 1)
            with v.Fori(0, pairs - 1) as i:
                for q in range(nq):
                    gated(i, q)
                    if (q + 1) % NCH == 0:
                        split_weights(i + 1, q // NCH)

            def finish(c):
                y, mask, clipped, finite = (chunk(t, c) for t in (picked, mk, yn, yp))
                v.wait_ge(s["scaled"], nq * (pairs - 1) + NCH + c + 1 + HS_RING)
                steps.settle(v, nc.vector.tensor_tensor(y, y, chunk(bias, c), ALU.add))
                steps.settle(v, nc.vector.tensor_tensor(y, y, chunk(probs, c), ALU.mult))
                steps.mark(nc.vector.tensor_scalar(finite, y, 0.0, None, ALU.max))
                steps.settle(v, nc.vector.tensor_scalar(clipped, y, 1e4, -1e4, ALU.min, ALU.max))
                steps.settle(v, nc.vector.scalar_tensor_tensor(finite, y, 0.0, finite, ALU.min, ALU.add))
                steps.settle(v, nc.vector.tensor_scalar(mask, finite, 0.0, 0.0, ALU.mult, ALU.is_equal))
                steps.settle(v, nc.vector.copy_predicated(clipped, mask, finite))
                nc.vector.tensor_tensor(chunk(chip.h, c), chunk(chip.h, c), clipped, ALU.add).then_inc(s["done"], 1)

            for q in range(nq):
                gated(pairs - 1, q)
                if switch and q >= NCH:
                    finish(q - NCH)


def row_attention(chip):
    nc = chip.nc
    k_ln = chip.next_norm()
    n_heads, c_head = 8, 32
    hc = n_heads * c_head
    scale = 1.0 / (c_head * NTOK) ** 0.5
    with ExitStack() as ctx:
        def sb(name, shape):
            return ctx.enter_context(nc.sbuf_tensor(name, shape, F32))
        mn = sb("a1mn", [P, TP])
        mt = sb("a1mt", [TT, NT, 128])
        gram = sb("a1gram", [P, P])
        prod = sb("a1prod", [P, NB, hc])
        red = sb("a1red", [P, NB, n_heads])
        att = sb("a1att", [P, NB, n_heads])
        wa = sb("a1wa", [P, NB, hc])
        g = sb("a1g", [128, NB, 2, TP])
        s_mn, s_t, s_ts, s_g, s_gs, s_a, s_red, s_d, s_att, s_wa, s_gp, s_gate, s_o, s_og, s_y, s_h, s_step = (
            chip.stage_sem("a1_" + n) for n in ("mn", "mt", "mt_sb", "gram", "gram_sb", "scores", "summed", "diff",
                                                "att", "wv", "gate_in", "gate", "out", "gated", "proj", "h", "step"))
        block = ctx.enter_context(nc.Block())
        pa, pb, pc = chip.pa, chip.pb, chip.pc
        units = [(s, k, c) for s in range(NB) for k in range(2) for c in range(NCH)]
        out_banks = [chip.psum[:, n] for n in (3, 4, 5, 6, 7)]

        @block.tensor
        def _(pe):
            norm_tensor(chip, k_ln, chip.h)
            chip.need(pe, 2)
            keep_clock(chip, pc[:, 1], 6)
            for j in range(NT):
                pe.wait_ge(s_mn, 4)
                last = nc.tensor.transpose(pa[0:TT, j // 3, 128 * (j % 3):128 * (j % 3) + 128],
                                           mn[:, TT * j:TT * j + TT], chip.w("ident"))
            last.then_inc(s_t, 1)

            def gate(u):
                s, k, c = units[u]
                if u >= 3:
                    pe.wait_ge(s_gate, u - 2)
                nc.tensor.matmul(pb[:, u % 3, 0:CH], chip.w("a1_wg", first=hc * s + 128 * k, cols=128), chunk(mn, c),
                                 start=True, stop=True).then_inc(s_gp, 1)

            for u in range(3):
                gate(u)
            pe.wait_ge(s_ts, 1)
            for j in range(NT):
                last = nc.tensor.matmul(pc[:, 0, 0:128], mt[:, j, :], mt[:, j, :], start=(j == 0), stop=(j == NT - 1))
            last.then_inc(s_g, 1)
            for u in range(3, 6):
                gate(u)
            pe.wait_ge(s_gs, 1)
            for s in range(NB):
                nc.tensor.matmul(pa[:, s, 0:hc], gram[64 * s:64 * s + 64, :], chip.w("a1_wq", rows=64, row0=64 * s),
                                 start=True, stop=True).then_inc(s_a, 1)
            for u in range(6, 9):
                gate(u)
            pe.wait_ge(s_red, 1)
            nc.tensor.matmul(pc[:, 1, 0:NB * n_heads], chip.w("tdiff"), red[:, :, :].rearrange("p s h -> p (s h)"),
                             start=True, stop=True).then_inc(s_d, 1)
            for u in range(9, 12):
                gate(u)
            pe.wait_ge(s_wa, 1)
            pe.wait_ge(s_gate, len(units))
            for u, (s, k, c) in enumerate(units):
                if u >= 5:
                    pe.wait_ge(s_og, u - 4)
                nc.tensor.matmul(out_banks[u % 5][:, 0:CH], wa[:, s, 128 * k:128 * k + 128], chunk(mn, c),
                                 start=True, stop=True).then_inc(s_o, 1)
            for s in range(NB):
                for c in range(NCH):
                    for k in range(2):
                        pe.wait_ge(s_og, 6 * s + 3 * k + c + 1)
                        last = nc.tensor.matmul(pa[64 * s:64 * s + 64, c, 0:CH], chip.w("a1_wo", first=64 * k, cols=64),
                                                g[:, s, k, c * CH:(c + 1) * CH], start=(k == 0), stop=(k == 1))
                    last.then_inc(s_y, 1)

        @block.scalar
        def _(act):
            norm_scalar(chip, k_ln, twice=True)
            chip.need(act, 2)
            for u, (s, k, c) in enumerate(units):
                if u == 3:
                    act.wait_ge(s_g, 1)
                    nc.scalar.activation(gram[:, :], pc[:, 0, 0:128], ACT.Copy).then_inc(s_gs, 1)
                if u == 9:
                    act.wait_ge(s_d, 1)
                    nc.scalar.activation(att[:, :, :], pc[:, 1, 0:NB * n_heads].rearrange("p (s h) -> p s h", s=NB),
                                         ACT.Sigmoid, scale=scale).then_inc(s_att, 1)
                act.wait_ge(s_gp, u + 1)
                nc.scalar.activation(g[:, s, k, c * CH:(c + 1) * CH], pb[:, u % 3, 0:CH], ACT.Sigmoid,
                                     bias=chip.w("a1_bg", first=k, cols=1)).then_inc(s_gate, 1)

        @block.vector
        def _(v):
            steps = Steps(s_step)
            norm_vector(chip, k_ln, chip.xl)
            chip.need(v, 2)
            for c in range(NCH):
                v.wait_ge(chip.ln_out, NCH * k_ln + c + 1)
                nc.vector.tensor_scalar(chunk(mn, c), chunk(chip.xl, c), chip.w("a1_g"), chip.w("a1_b"),
                                        ALU.mult, ALU.add).then_inc(s_mn, 1)
            v.wait_ge(s_mn, 3)
            nc.vector.memset(mn[:, NTOK:TP], 0.0).then_inc(s_mn, 1)
            v.wait_ge(s_t, 1)
            nc.vector.tensor_copy(mt[:, :, :].rearrange("p (c j) n -> p c j n", c=3),
                                  pa[0:TT, :, 0:384].rearrange("p c (j n) -> p c j n", n=128)).then_inc(s_ts, 1)
            for s in range(NB):
                v.wait_ge(s_a, s + 1)
                steps.settle(v, nc.vector.tensor_tensor(prod[:, s, :], pa[:, s, 0:hc], chip.w("a1_wk"), ALU.mult))
            nc.vector.tensor_reduce(red[:, :, :], prod[:, :, :].rearrange("p s (h c) -> p s h c", c=c_head), AX.X,
                                    ALU.add).then_inc(s_red, 1)
            v.wait_ge(s_att, 1)
            for s in range(NB):
                last = nc.vector.tensor_tensor(wa[:, s, :].rearrange("p (h c) -> p h c", c=c_head),
                                               chip.w("a1_wv").rearrange("p (h c) -> p h c", c=c_head),
                                               att[:, s, :].unsqueeze(2).to_broadcast([P, n_heads, c_head]), ALU.mult)
            last.then_inc(s_wa, 1)
            for u, (s, k, c) in enumerate(units):
                v.wait_ge(s_o, u + 1)
                v.wait_ge(s_gate, u + 1)
                gs = g[:, s, k, c * CH:(c + 1) * CH]
                nc.vector.tensor_tensor(gs, out_banks[u % 5][:, 0:CH], gs, ALU.mult).then_inc(s_og, 1)
            for c in range(NCH):
                v.wait_ge(s_y, NCH + c + 1)
                nc.vector.scalar_tensor_tensor(chunk(chip.h, c), pa[:, c, 0:CH], chip.w("a1_bo"), chunk(chip.h, c),
                                               ALU.add, ALU.add).then_inc(s_h, 1)


def scan_attention(chip):
    nc = chip.nc
    k_ln = chip.next_norm()
    ns = 32
    with ExitStack() as ctx:
        def sb(name, shape):
            return ctx.enter_context(nc.sbuf_tensor(name, shape, F32))
        xp = sb("a2xp", [P, 3 + TP])
        res, xcv = sb("a2res", [P, TP]), sb("a2xcv", [P, TP])
        da, cp, yc, y, zero = (sb("a2da", [ns, TP]), sb("a2cp", [ns, TP]), sb("a2yc", [ns, TP]),
                               sb("a2y", [ns, TP]), sb("a2zero", [ns, TP]))
        o = sb("a2o", [P, TP])
        acc, col = sb("a2acc", [P, 2 * NCH]), sb("a2col", [P, 6])
        s_xp, s_xps, s_res, s_ress, s_conv, s_da, s_das, s_db, s_y, s_y2, s_y2s, s_p, s_o, s_m, s_negm, s_sq, s_v, s_vl, s_rs, s_h, s_step = (
            chip.stage_sem("a2_" + n) for n in ("xp", "xp_sb", "res", "res_sb", "conv", "da", "da_sb", "db", "y", "cy",
                                                "cy_sb", "proj", "o", "mean", "neg_mean", "square", "var", "var_log",
                                                "rstd", "h", "step"))
        block = ctx.enter_context(nc.Block())
        pa, pb, pc = chip.pa, chip.pb, chip.pc

        @block.tensor
        def _(pe):
            norm_tensor(chip, k_ln, chip.h)
            chip.need(pe, 3)
            for c in range(NCH):
                pe.wait_ge(chip.ln_out, NCH * k_ln + c + 1)
                nc.tensor.matmul(pa[:, c, 0:CH], chip.w("a2_wxp"), chunk(chip.xl, c), start=True, stop=True).then_inc(s_xp, 1)
            for c in range(NCH):
                nc.tensor.matmul(pb[:, c, 0:CH], chip.w("a2_wres"), chunk(chip.xl, c), start=True, stop=True).then_inc(s_res, 1)
            pe.wait_ge(s_xps, NCH + 1)
            for c in range(NCH):
                pe.wait_ge(s_conv, c + 1)
                nc.tensor.matmul(pa[0:ns, c, 0:CH], chip.w("a2_dt"), chunk(xcv, c), start=True, stop=True).then_inc(s_da, 1)
                keep_clock(chip, pc[:, 1], 2 if c < NCH - 1 else 0)
            pe.wait_ge(s_ress, NCH)
            for c in range(NCH):
                nc.tensor.matmul(pb[0:ns, c, 0:CH], chip.w("a2_bw"), chunk(xcv, c), start=True, stop=True).then_inc(s_db, 1)
            keep_clock(chip, pc[:, 1], 8)
            pe.wait_ge(s_das, NCH)
            pe.wait_ge(s_y, 1)
            for c in range(NCH):
                nc.tensor.matmul(pa[:, c, 0:CH], chip.w("a2_cw", rows=ns), y[:, c * CH:(c + 1) * CH], start=True,
                                 stop=True).then_inc(s_y2, 1)
            for c in range(NCH):
                pe.wait_ge(s_y2s, c + 1)
                nc.tensor.matmul(pb[:, c, 0:CH], chip.w("a2_ow"), chunk(res, c), start=True, stop=True).then_inc(s_p, 1)
            pe.wait_ge(s_o, NCH)
            nc.tensor.matmul(pc[:, 0, 0:NCH], chip.w("chmean"), acc[:, 0:NCH], start=True, stop=True).then_inc(s_m, 1)
            pe.wait_ge(s_sq, 1)
            nc.tensor.matmul(pc[:, 1, 0:1], chip.w("chmean"), col[:, 1:2], start=True, stop=True).then_inc(s_v, 1)
            keep_clock(chip, pb[:, 0], 6)

        @block.scalar
        def _(act):
            norm_scalar(chip, k_ln)
            for c in range(NCH):
                act.wait_ge(s_xp, c + 1)
                nc.scalar.activation(xp[:, 3 + c * CH:3 + (c + 1) * CH], pa[:, c, 0:CH], ACT.Identity,
                                     bias=chip.w("a2_bxp")).then_inc(s_xps, 1)
            for c in range(NCH):
                act.wait_ge(s_res, c + 1)
                nc.scalar.activation(chunk(res, c), pb[:, c, 0:CH], ACT.Silu, bias=chip.w("a2_bres")).then_inc(s_ress, 1)
            load_functions(nc, EXP_LN)
            for c in range(NCH):
                act.wait_ge(s_da, c + 1)
                nc.scalar.activation(da[:, c * CH:(c + 1) * CH], pa[0:ns, c, 0:CH], ACT.Exp).then_inc(s_das, 1)
            act.wait_ge(s_negm, 1)
            nc.scalar.activation(chip.sq[:, 0:NTOK], o[:, 0:NTOK], ACT.Square, bias=col[:, 0:1],
                                 accum_out=col[:, 1:2]).then_inc(s_sq, 1)
            act.wait_ge(s_v, 1)
            nc.scalar.activation(col[:, 2:3], pc[:, 1, 0:1], ACT.Ln, bias=chip.w("eps", cols=1)).then_inc(s_vl, 1)
            act.wait_ge(s_vl, 1)
            nc.scalar.activation(col[:, 3:4], col[:, 2:3], ACT.Exp, scale=-0.5).then_inc(s_rs, 1)

        @block.vector
        def _(v):
            steps = Steps(s_step)
            nc.vector.memset(xp[:, 0:3], 0.0).then_inc(s_xps, 1)
            steps.settle(v, nc.vector.memset(zero[:, :], 0.0))
            norm_vector(chip, k_ln, chip.xl)
            chip.need(v, 3)
            for c in range(NCH):
                v.wait_ge(s_xps, c + 2)
                a = c * CH
                steps.settle(v, nc.vector.tensor_scalar(chunk(xcv, c), xp[:, a:a + CH], chip.w("a2_convw", cols=1),
                                                        chip.w("a2_convb"), ALU.mult, ALU.add))
                for k in range(1, 4):
                    i = nc.vector.scalar_tensor_tensor(chunk(xcv, c), xp[:, a + k:a + k + CH],
                                                       chip.w("a2_convw", first=k, cols=1), chunk(xcv, c),
                                                       ALU.mult, ALU.add)
                    if k < 3:
                        steps.settle(v, i)
                    else:
                        i.then_inc(s_conv, 1)
            v.wait_ge(s_das, NCH)
            steps.settle(v, nc.vector.tensor_tensor_scan(cp[:, :], da[:, :], zero[:, :], 1.0, ALU.mult, ALU.add))
            v.wait_ge(s_db, NCH)
            steps.settle(v, nc.vector.tensor_tensor(chunks(cp[:, :]), chunks(cp[:, :]), pb[0:ns, :, 0:CH], ALU.mult))
            steps.settle(v, nc.vector.tensor_tensor_scan(yc[:, :], cp[:, :], zero[:, :], 0.0, ALU.add, ALU.add))
            steps.settle(v, nc.vector.tensor_tensor(y[:, 1:TP], yc[:, 0:TP - 1], da[:, 1:TP], ALU.mult))
            steps.settle(v, nc.vector.tensor_tensor(y[:, 1:TP], yc[:, 1:TP], y[:, 1:TP], ALU.subtract))
            nc.vector.tensor_copy(y[:, 0:1], pb[0:ns, 0, 0:1]).then_inc(s_y, 1)
            v.wait_ge(s_ress, NCH)
            for c in range(NCH):
                v.wait_ge(s_y2, c + 1)
                nc.vector.tensor_tensor(chunk(res, c), pa[:, c, 0:CH], chunk(res, c), ALU.mult).then_inc(s_y2s, 1)
            for c in range(NCH):
                v.wait_ge(s_p, c + 1)
                n = LAST if c == NCH - 1 else CH
                a = c * CH
                nc.vector.scalar_tensor_tensor(o[:, a:a + n], pb[:, c, 0:n], chip.w("a2_ob"), xcv[:, a:a + n],
                                               ALU.add, ALU.add, accum_out=acc[:, c:c + 1]).then_inc(s_o, 1)
            v.wait_ge(s_m, 1)
            nc.vector.tensor_reduce(col[:, 0:1], pc[:, 0, 0:NCH], AX.X, ALU.add, negate=True).then_inc(s_negm, 1)
            v.wait_ge(s_rs, 1)
            steps.settle(v, nc.vector.tensor_tensor(col[:, 4:5], col[:, 3:4], chip.w("a2_g"), ALU.mult))
            steps.settle(v, nc.vector.tensor_scalar(col[:, 5:6], col[:, 0:1], col[:, 4:5], chip.w("a2_b"), ALU.mult, ALU.add))
            steps.settle(v, nc.vector.tensor_scalar(o[:, 0:NTOK], o[:, 0:NTOK], col[:, 4:5], col[:, 5:6], ALU.mult, ALU.add))
            nc.vector.tensor_tensor(chip.h[:, 0:NTOK], chip.h[:, 0:NTOK], o[:, 0:NTOK], ALU.add).then_inc(s_h, 1)


def experts3(chip, slab):
    nc = chip.nc
    k_ln = chip.next_norm()
    name, n_e = "f2", 6
    e2, k_rows = 2 * n_e, 3 * 2 * n_e
    nu, pairs, ring = NCH, n_e // 2, 2
    with ExitStack() as ctx:
        def sb(nm, shape, dt=F32):
            return ctx.enter_context(nc.sbuf_tensor(nm, shape, dt))
        slabs = sb("f2slab", [128, n_e * SLAB3])
        ws = sb("f2w", [128, 2, SLAB3 - 64])
        rh = sb("f2rh", [64, TP])
        h1, h2, hg = (sb("f2" + n, [128, ring, CH]) for n in ("h1", "h2", "hg"))
        r = route_tiles(chip, sb, name, n_e, k_rows)
        s = {x: chip.stage_sem(name + "_" + x) for x in
             ("router", "router_sb", "logits", "d", "exp", "gap", "weights", "gates", "rows", "rows_sb", "first",
              "act", "mid", "mid_act", "gated", "third", "done", "step", "slab", "w", "spread")}
        block = ctx.enter_context(nc.Block())
        pa, pb, pc = chip.pa, chip.pb, chip.pc

        @block.sync
        def _(sp):
            sp.dma_start(slabs[:, :], slab).then_inc(s["slab"], 16)

        @block.tensor
        def _(pe):
            norm_tensor(chip, k_ln, chip.h)
            chip.need(pe, 3)
            for c in range(NCH):
                pe.wait_ge(chip.ln_out, NCH * k_ln + c + 1)
                nc.tensor.matmul(pa[0:64, c, 0:CH], chip.w("f2_rw1"), chunk(chip.xl, c), start=True, stop=True).then_inc(s["router"], 1)
            pe.wait_ge(s["router_sb"], NCH)
            for j in range(NT):
                last = nc.tensor.matmul(pc[0:TT, 1, e2 * j:e2 * j + e2], rh[:, TT * j:TT * j + TT],
                                        chip.w("f2_gate", rows=64), start=True, stop=True)
            last.then_inc(s["logits"], 1)
            keep_clock(chip, chip.psum[:, 6], ROUTE_FILL["probs"])
            pe.wait_ge(s["gates"], 1)
            for j in range(NT):
                last = nc.tensor.transpose(pb[0:k_rows, j // 3, TT * (j % 3):TT * (j % 3) + TT], r["tg"][:, j, :],
                                           chip.w("ident", rows=TT, cols=TT))
            last.then_inc(s["rows"], 1)
            keep_clock(chip, chip.psum[:, 6], 4)
            pe.wait_ge(s["rows_sb"], 2)
            for c in range(NCH):
                nc.tensor.matmul(pa[:, c, 0:CH], chip.w("f2_b2", rows=k_rows), chunk(r["rows"], c),
                                 start=True, stop=False, skip_group_check=True)

            def first(i, n):
                i, n = i + n // (2 * nu), n % (2 * nu)
                k, c = divmod(n, nu)
                if c == 0:
                    pe.wait_ge(s["w"], 2 * i + k + 1)
                pe.wait_ge(s["act"], 2 * nu * i + n + 1)
                nc.tensor.matmul(pc[:, n % ring, 0:CH], ws[:, k, 0:128], chunk(chip.xl, c), start=True,
                                 stop=True).then_inc(s["first"], 1)

            def mid(i, n):
                i, n = i + n // (2 * nu), n % (2 * nu)
                k, c = divmod(n, nu)
                pe.wait_ge(s["act"], 2 * nu * i + n + 1 + ring)
                pe.wait_ge(s["mid_act"], 2 * nu * i + n + 1)
                nc.tensor.matmul(pb[:, n % ring, 0:CH], ws[:, k, 128:256], h1[:, n % ring, :], start=True,
                                 stop=True).then_inc(s["mid"], 1)

            def spread(i, n):
                i, n = i + n // (2 * nu), n % (2 * nu)
                k, c = divmod(n, nu)
                sel = slabs[:, :].bitcast(BF16)[0:k_rows, bass.ds(i * (4 * SLAB3) + 2 * (k * SLAB3 + 386), 128)]
                nc.tensor.matmul(pb[:, 2, 0:CH], sel, chunk(r["rows16"][0:k_rows], c), start=True, stop=True
                                 ).then_inc(s["spread"], 1)

            def third(i, n):
                k, c = divmod(n, nu)
                pe.wait_ge(s["gated"], 2 * nu * i + n + 1 + ring)
                nc.tensor.matmul(pa[:, c, 0:CH], ws[:, k, 256:384], hg[:, n % ring, :], start=False, stop=False,
                                 skip_group_check=True).then_inc(s["third"], 1)

            def pair(i, last_pair):
                for n in range(2 * nu):
                    if not (last_pair and n + 2 >= 2 * nu):
                        first(i, n + 2)
                    if not (last_pair and n + 1 >= 2 * nu):
                        mid(i, n + 1)
                    third(i, n)
                    if not (last_pair and n + 1 >= 2 * nu):
                        spread(i, n + 1)

            pe.sem_inc(s["mid"], ring)
            pe.sem_inc(s["third"], 2 * nu)
            first(0, 0)
            first(0, 1)
            mid(0, 0)
            spread(0, 0)
            with pe.Fori(0, pairs - 1) as i:
                pair(i, False)
            pair(pairs - 1, True)

        @block.scalar
        def _(act):
            norm_scalar(chip, k_ln)
            for c in range(NCH):
                act.wait_ge(s["router"], c + 1)
                nc.scalar.activation(rh[:, c * CH:(c + 1) * CH], pa[0:64, c, 0:CH], ACT.Relu,
                                     bias=chip.w("f2_rb1", rows=64)).then_inc(s["router_sb"], 1)
            route_scalar(chip, r, "probs", s)
            act.sem_inc(s["act"], ring)
            act.sem_inc(s["mid_act"], ring)

            def relu1(i, n):
                i, n = i + n // (2 * nu), n % (2 * nu)
                act.wait_ge(s["first"], 2 * nu * i + n + 1)
                act.wait_ge(s["mid"], 2 * nu * i + n + 1)
                nc.scalar.activation(h1[:, n % ring, :], pc[:, n % ring, 0:CH], ACT.Relu,
                                     bias=ws[:, n // nu, 384:385]).then_inc(s["act"], 1)

            def relu2(i, n):
                i, n = i + n // (2 * nu), n % (2 * nu)
                act.wait_ge(s["mid"], 2 * nu * i + n + 1 + ring)
                act.wait_ge(s["gated"], 2 * nu * i + n + 1)
                nc.scalar.activation(h2[:, n % ring, :], pb[:, n % ring, 0:CH], ACT.Relu,
                                     bias=ws[:, n // nu, 385:386]).then_inc(s["mid_act"], 1)

            relu1(0, 0)
            relu1(0, 1)
            relu2(0, 0)
            with act.Fori(0, pairs - 1) as i:
                for n in range(2 * nu):
                    relu1(i, n + 2)
                    relu2(i, n + 1)
            for n in range(2 * nu - 1):
                if n + 2 < 2 * nu:
                    relu1(pairs - 1, n + 2)
                relu2(pairs - 1, n + 1)

        @block.vector
        def _(v):
            steps = Steps(s["step"])
            norm_vector(chip, k_ln, chip.xl)
            chip.need(v, 3)
            route_vector(chip, steps, r, "probs", n_e, False, s)
            v.wait_ge(s["rows"], 1)
            nc.vector.tensor_copy(chunks(r["rows"][:, :]), pb[0:k_rows, :, 0:CH]).then_inc(s["rows_sb"], 1)
            nc.vector.tensor_copy(chunks(r["rows16"][0:k_rows]), pb[0:k_rows, :, 0:CH]).then_inc(s["rows_sb"], 1)
            v.sem_inc(s["gated"], ring)

            def weights(i, k):
                v.wait_ge(s["third"], 2 * nu * i + (k + 1) * nu)
                nc.vector.tensor_copy(ws[:, k, :], slabs[:, bass.ds(i * (2 * SLAB3) + k * SLAB3, SLAB3 - 64)]
                                      ).then_inc(s["w"], 1)

            def gate(i, n):
                v.wait_ge(s["spread"], 2 * nu * i + n + 1)
                v.wait_ge(s["mid_act"], 2 * nu * i + n + 1 + ring)
                v.wait_ge(s["third"], 2 * nu * i + n + 1 + (2 * nu - ring))
                nc.vector.tensor_tensor(hg[:, n % ring, :], h2[:, n % ring, :], pb[:, 2, 0:CH],
                                        ALU.mult).then_inc(s["gated"], 1)

            v.wait_ge(s["slab"], 16)
            weights(0, 0)
            weights(0, 1)
            with v.Fori(0, pairs - 1) as i:
                for n in range(2 * nu):
                    gate(i, n)
                    if (n + 1) % nu == 0:
                        weights(i + 1, n // nu)
            for n in range(2 * nu):
                gate(pairs - 1, n)
            v.wait_ge(s["third"], n_e * nu + 2 * nu)
            nc.vector.tensor_tensor(chunks(chip.h[:, :]), chunks(chip.h[:, :]), pa[:, :, 0:CH], ALU.add).then_inc(s["done"], 1)


def mamba(chip, selbc):
    nc = chip.nc
    k_ln, k_ln1, k_ln2 = chip.next_norm(), chip.next_norm(), chip.next_norm()
    n_s = 16
    with ExitStack() as ctx:
        def sb(name, shape, dt=F32):
            return ctx.enter_context(nc.sbuf_tensor(name, shape, dt))
        sel = sb("a3sel", [128, n_s * 2 * 128], BF16)
        xs = sb("a3xs", [128, NB, 3 + TP])
        xc, z, dt, u = (sb("a3" + n, [128, NB, TP]) for n in ("xc", "z", "dt", "u"))
        t1 = sb("a3t1", [128, NB, TP])
        dbl = sb("a3dbl", [48, NB, TP])
        rem = sb("a3rem", [32, NB, TP])
        low = sb("a3low", [32, NB, TP], BF16)
        bcp = sb("a3bcp", [128, NB, TP], BF16)
        an, ddp = sb("a3an", [128, n_s]), sb("a3ddp", [128, 128])
        da, hst, cs, pr = (sb("a3" + n, [128, 2, TP]) for n in ("da", "hst", "cs", "pr"))
        dbx = sb("a3dbx", [128, 2, TP])
        m1 = sb("a3m1", [P, TP])
        r1, n1 = sb("a3r1", [P, TP]), sb("a3n1", [P, TP])
        names = ("sel_loaded", "xs", "xs_sb", "z", "z_sb", "conv", "xc", "dbl", "dbl_sb", "dt", "abs", "exp", "log",
                 "dt_pos", "dt_done", "dt_done1", "log_done1", "u1", "high", "rem", "rem1", "low", "mid", "parts", "parts1", "aexp", "a", "dp", "u", "b_spread", "c_spread", "da", "dbx", "scan",
                 "c_sb", "prod", "summed", "yo", "wout", "wout_sb", "wlin", "r1", "n1", "up", "up_sb",
                 "down", "r2", "h", "step")
        s = {x: chip.stage_sem("a3_" + x) for x in names}
        block = ctx.enter_context(nc.Block())
        pa, pb, pc = chip.pa, chip.pb, chip.pc
        bank = [pa, pb]
        bc = [(b, c) for b in range(NB) for c in range(NCH)]
        cb = [(c, b) for c in range(NCH) for b in range(NB)]

        @block.sync
        def _(sp):
            sp.dma_start(sel[:, :], selbc.bitcast(BF16)).then_inc(s["sel_loaded"], 16)

        @block.tensor
        def _(pe):
            norm_tensor(chip, k_ln, chip.h)
            chip.need(pe, 4)
            keep_clock(chip, pc[:, 1], 3)
            pe.wait_ge(chip.ln_out, NCH * (k_ln + 1))
            for b, c in bc:
                nc.tensor.matmul(bank[b][:, c, 0:CH], chip.w("a3_win", first=128 * b, cols=128), chunk(chip.xl, c),
                                 start=True, stop=True).then_inc(s["xs"], 1)
            for n, (b, c) in enumerate(bc):
                pe.wait_ge(s["xs_sb"], n + 1)
                nc.tensor.matmul(bank[b][:, c, 0:CH], chip.w("a3_win", first=256 + 128 * b, cols=128),
                                 chunk(chip.xl, c), start=True, stop=True).then_inc(s["z"], 1)
            for b in range(NB):
                for c in range(NCH):
                    pe.wait_ge(s["z_sb"], NCH * b + c + 1)
                    pe.wait_ge(s["xc"], b + 1)
                    nc.tensor.matmul(bank[b][0:48, c, 0:CH], chip.w("a3_wx"), chunk(xc[:, b], c), start=True,
                                     stop=True).then_inc(s["dbl"], 1)
                if b:
                    keep_clock(chip, pc[:, 1], 8)
                for c in range(NCH):
                    pe.wait_ge(s["dbl_sb"], NCH * b + c + 1)
                    nc.tensor.matmul(bank[b][:, c, 0:CH], chip.w("a3_wdt", rows=48), chunk(dbl[:, b], c), start=True,
                                     stop=True).then_inc(s["dt"], 1)
            keep_clock(chip, pc[:, 1], 13)
            pe.wait_ge(s["sel_loaded"], 16)
            pe.wait_ge(s["high"], NB)
            pe.wait_ge(s["mid"], NB)
            pe.wait_ge(s["parts"], 2)
            pe.wait_ge(s["parts1"], 1)
            pe.wait_ge(s["dp"], 1)
            pe.wait_ge(s["abs"], NB)
            pe.wait_ge(s["dt_pos"], NB)

            def spread_b(b, i, k):
                g = n_s * b + k
                pe.wait_ge(s["dbx"], 2 * i + g + 1)
                for c in range(NCH):
                    last = nc.tensor.matmul(pb[:, c, 0:CH], sel[:, bass.ds(i * 512 + 256 * k, 128)],
                                            chunk(bcp[:, b], c), start=True, stop=True)
                last.then_inc(s["b_spread"], 1)

            def spread_c(b, i, k, c):
                g = n_s * b + k
                pe.wait_ge(s["c_sb"], 6 * i + 3 * g + c + 1)
                nc.tensor.matmul(pc[:, (3 * k + c) % 2, 0:CH], sel[:, bass.ds(i * 512 + 256 * k + 128, 128)],
                                 chunk(bcp[:, b], c), start=True, stop=True).then_inc(s["c_spread"], 1)

            def add_up(b, i, k, c):
                if c == 0:
                    pe.wait_ge(s["prod"], 2 * i + n_s * b + k + 1 + 2)
                last = nc.tensor.matmul(pa[:, c, 0:CH], chip.w("ident"), chunk(pr[:, k], c), start=False,
                                        stop=False, skip_group_check=True)
                if c == NCH - 1:
                    last.then_inc(s["summed"], 1)

            def spread(b, i, k):
                spread_b(b, i, k)
                for c in range(NCH):
                    spread_c(b, i, k, c)

            spread(0, 0, 0)
            spread(0, 0, 1)
            for b in range(NB):
                if b:
                    pe.wait_ge(s["yo"], b)
                for c in range(NCH):
                    nc.tensor.matmul(pa[:, c, 0:CH], ddp[:, :], chunk(xc[:, b], c), start=True, stop=False,
                                     skip_group_check=True)
                with pe.Fori(0, n_s // 2 - 1) as i:
                    for k in range(2):
                        spread_b(b, i + 1, k)
                        spread_c(b, i + 1, k, 0)
                        spread_c(b, i + 1, k, 1)
                        add_up(b, i, k, 0)
                        spread_c(b, i + 1, k, 2)
                        add_up(b, i, k, 1)
                        add_up(b, i, k, 2)
                for k in range(2):
                    if b < NB - 1:
                        spread(b + 1, 0, k)
                    for c in range(NCH):
                        add_up(b, n_s // 2 - 1, k, c)

            for b, c in bc:
                pe.wait_ge(s["yo"], b + 1)
                nc.tensor.matmul(pb[64 * b:64 * b + 64, c, 0:CH], chip.w("a3_wout"), chunk(u[:, b], c),
                                 start=True, stop=True).then_inc(s["wout"], 1)
            for c in range(NCH):
                pe.wait_ge(s["wout_sb"], c + 1)
                nc.tensor.matmul(pa[:, c, 0:CH], chip.w("a3_wlin"), chunk(m1, c), start=True, stop=True).then_inc(s["wlin"], 1)
            norm_tensor(chip, k_ln1, r1, s["r1"])
            for c, b in cb:
                pe.wait_ge(s["n1"], c + 1)
                nc.tensor.matmul(bank[b][:, c, 0:CH], chip.w("a3_wexp", first=128 * b, cols=128), chunk(n1, c),
                                 start=True, stop=True).then_inc(s["up"], 1)
            for c, b in cb:
                pe.wait_ge(s["up_sb"], 2 * (c + 1))
                nc.tensor.matmul(pa[64 * b:64 * b + 64, c, 0:CH], chip.w("a3_wsq"), chunk(t1[:, b], c),
                                 start=True, stop=True).then_inc(s["down"], 1)
            norm_tensor(chip, k_ln2, r1, s["r2"])
            keep_clock(chip, pc[:, 1], 7)

        @block.scalar
        def _(act):
            norm_scalar(chip, k_ln)
            chip.need(act, 4)
            nc.scalar.activation(an[:, :], chip.w("a3_alog"), ACT.Exp).then_inc(s["aexp"], 1)
            for n, (b, c) in enumerate(bc):
                act.wait_ge(s["xs"], n + 1)
                nc.scalar.activation(xs[:, b, 3 + c * CH:3 + (c + 1) * CH], bank[b][:, c, 0:CH], ACT.Copy
                                     ).then_inc(s["xs_sb"], 1)
            for b in range(NB):
                for c in range(NCH):
                    act.wait_ge(s["z"], NCH * b + c + 1)
                    nc.scalar.activation(chunk(z[:, b], c), bank[b][:, c, 0:CH], ACT.Silu).then_inc(s["z_sb"], 1)
                if b == 0:
                    act.wait_ge(s["conv"], 1)
                    nc.scalar.activation(xc[:, 0], xc[:, 0], ACT.Silu).then_inc(s["xc"], 1)

            def low_rank(b):
                for c in range(NCH):
                    act.wait_ge(s["dbl"], NCH * b + c + 1)
                    nc.scalar.activation(chunk(dbl[:, b], c), bank[b][0:48, c, 0:CH], ACT.Copy).then_inc(s["dbl_sb"], 1)
                act.wait_ge(s["dbl_sb"], NCH * (b + 1))
                nc.scalar.activation(bcp[0:32, b], dbl[0:32, b], ACT.Copy).then_inc(s["high"], 1)

            def softplus_parts(b):
                act.wait_ge(s["dt"], NCH * (b + 1))
                nc.scalar.activation(chunks(t1[:, b]), bank[b][:, :, 0:CH], ACT.Abs, bias=chip.w("a3_bdt")).then_inc(s["abs"], 1)
                act.wait_ge(s["abs"], b + 1)
                nc.scalar.activation(t1[:, b], t1[:, b], ACT.Exp, scale=-1.0).then_inc(s["exp"], 1)
                act.wait_ge(s["exp"], b + 1)
                nc.scalar.activation(u[:, b], t1[:, b], ACT.Ln, bias=chip.w("eps", first=2, cols=1)).then_inc(s["log"], 1)
                nc.scalar.activation(chunks(dt[:, b]), bank[b][:, :, 0:CH], ACT.Relu, bias=chip.w("a3_bdt")).then_inc(s["dt_pos"], 1)

            def second_part(b):
                act.wait_ge(s["rem"] if b == 0 else s["rem1"], 1)
                nc.scalar.activation(low[:, b], rem[:, b], ACT.Copy).then_inc(s["low"], 1)
                act.wait_ge(s["low"], b + 1)
                nc.scalar.activation(bcp[32:64, b], low[:, b], ACT.Copy).then_inc(s["mid"], 1)

            low_rank(0)
            act.wait_ge(s["conv"], 2)
            nc.scalar.activation(xc[:, 1], xc[:, 1], ACT.Silu).then_inc(s["xc"], 1)
            load_functions(nc, EXP_LN)
            softplus_parts(0)
            second_part(0)
            low_rank(1)
            softplus_parts(1)
            second_part(1)
            act.wait_ge(s["a"], 1)
            act.sem_inc(s["c_sb"], 2)
            for b in range(NB):
                act.wait_ge(s["dt_done"] if b == 0 else s["dt_done1"], 1)
                with act.Fori(0, n_s // 2) as i:
                    for k in range(2):
                        g = n_s * b + k
                        act.wait_ge(s["scan"], 2 * i + g + 1)
                        nc.scalar.activation(da[:, k], dt[:, b], ACT.Exp, scale=an[:, bass.ds(2 * i + k, 1)]
                                             ).then_inc(s["da"], 1)
                        act.wait_ge(s["prod"], 2 * i + g + 1)
                        for c in range(NCH):
                            act.wait_ge(s["c_spread"], 6 * i + 3 * g + c + 1)
                            nc.scalar.activation(chunk(cs[:, k], c), pc[:, (3 * k + c) % 2, 0:CH], ACT.Copy
                                                 ).then_inc(s["c_sb"], 1)
            for c in range(NCH):
                act.wait_ge(s["wout"], NCH + c + 1)
                nc.scalar.activation(chunk(m1, c), pb[:, c, 0:CH], ACT.Copy).then_inc(s["wout_sb"], 1)
            norm_scalar(chip, k_ln1, loaded=True)
            for n, (c, b) in enumerate(cb):
                act.wait_ge(s["up"], n + 1)
                nc.scalar.activation(chunk(t1[:, b], c), bank[b][:, c, 0:CH], ACT.Relu, bias=chip.w("a3_bexp")
                                     ).then_inc(s["up_sb"], 1)
            norm_scalar(chip, k_ln2, loaded=True)

        def remainder(engine, of_engine, b):
            engine.wait_ge(s["high"], b + 1)
            of_engine.tensor_tensor(rem[:, b], dbl[0:32, b], bcp[0:32, b], ALU.subtract
                                    ).then_inc(s["rem"] if b == 0 else s["rem1"], 1)

        def third_part(engine, of_engine, b):
            engine.wait_ge(s["low"], b + 1)
            of_engine.tensor_tensor(bcp[64:96, b], rem[:, b], low[:, b], ALU.subtract
                                    ).then_inc(s["parts"] if b == 0 else s["parts1"], 1)

        def step_size(engine, of_engine, b):
            done = s["dt_done"] if b == 0 else s["dt_done1"]
            engine.wait_ge(s["dt_pos"], b + 1)
            of_engine.tensor_tensor(dt[:, b], dt[:, b], u[:, b], ALU.add).then_inc(done, 1)
            engine.wait_ge(done, 1)
            of_engine.tensor_tensor(u[:, b], dt[:, b], xc[:, b], ALU.mult).then_inc(s["u"] if b == 0 else s["u1"], 1)

        @block.gpsimd
        def _(pool):
            pool.sem_inc(s["prod"], 2)
            remainder(pool, nc.gpsimd, 1)
            third_part(pool, nc.gpsimd, 1)
            pool.wait_ge(s["parts1"], 1)
            pool.wait_ge(s["log_done1"], 1)
            step_size(pool, nc.gpsimd, 1)
            pool.wait_ge(s["u1"], 1)
            for b in range(NB):
                with pool.Fori(0, n_s // 2) as i:
                    for k in range(2):
                        g = n_s * b + k
                        pool.wait_ge(s["scan"], 2 * i + g + 1 + 2)
                        pool.wait_ge(s["c_sb"], 6 * i + 3 * g + 3 + 2)
                        pool.wait_ge(s["summed"], 2 * i + g + 1)
                        nc.gpsimd.tensor_tensor(pr[:, k], hst[:, k], cs[:, k], ALU.mult).then_inc(s["prod"], 1)

        @block.vector
        def _(v):
            steps = Steps(s["step"])
            steps.settle(v, nc.vector.memset(xs[:, :, 0:3], 0.0))
            nc.vector.memset(bcp[96:128], 0.0).then_inc(s["parts"], 1)
            norm_vector(chip, k_ln, chip.xl)
            chip.need(v, 4)
            nc.vector.tensor_scalar(ddp[:, :], chip.w("ident"), chip.w("a3_dp"), None, ALU.mult).then_inc(s["dp"], 1)
            v.wait_ge(s["aexp"], 1)
            nc.vector.tensor_scalar(an[:, :], an[:, :], -1.0, None, ALU.mult).then_inc(s["a"], 1)
            for b in range(NB):
                v.wait_ge(s["xs_sb"], NCH * (b + 1))
                steps.settle(v, nc.vector.tensor_scalar(xc[:, b], xs[:, b, 0:TP], chip.w("a3_convw", cols=1),
                                                        chip.w("a3_convb"), ALU.mult, ALU.add))
                for k in range(1, 4):
                    i = nc.vector.scalar_tensor_tensor(xc[:, b], xs[:, b, k:k + TP], chip.w("a3_convw", first=k, cols=1),
                                                       xc[:, b], ALU.mult, ALU.add)
                    if k < 3:
                        steps.settle(v, i)
                    else:
                        i.then_inc(s["conv"], 1)
            remainder(v, nc.vector, 0)
            for b in range(NB):
                e, ser, small = t1[:, b], hst[:, b], t1[:, b].bitcast(mybir.dt.uint32)
                v.wait_ge(s["exp"], b + 1)
                steps.settle(v, nc.vector.tensor_scalar(ser, e, -0.25, 1.0 / 3.0, ALU.mult, ALU.add))
                steps.settle(v, nc.vector.tensor_tensor(ser, ser, e, ALU.mult))
                for coefficient in (-0.5, 1.0):
                    steps.settle(v, nc.vector.scalar_tensor_tensor(ser, ser, coefficient, e, ALU.add, ALU.mult))
                v.wait_ge(s["log"], b + 1)
                steps.settle(v, nc.vector.tensor_scalar(small, e, SERIES_BELOW, None, ALU.is_lt))
                copied = nc.vector.copy_predicated(u[:, b], small, ser)
                if b == 0:
                    steps.settle(v, copied)
                    step_size(v, nc.vector, 0)
                    third_part(v, nc.vector, 0)
                else:
                    copied.then_inc(s["log_done1"], 1)
            v.wait_ge(s["u"], 1)
            v.wait_ge(s["log_done1"], 1)
            v.sem_inc(s["scan"], 2)
            v.sem_inc(s["summed"], 2)
            v.sem_inc(s["dbx"], 1)

            def states(b, i):
                for k in range(2):
                    g = n_s * b + k
                    v.wait_ge(s["b_spread"], 2 * i + g + 1)
                    v.wait_ge(s["scan"], 2 * i + g + 1)
                    nc.vector.tensor_tensor(chunks(dbx[:, k]), chunks(u[:, b]), pb[:, :, 0:CH], ALU.mult
                                            ).then_inc(s["dbx"], 1)
                    v.wait_ge(s["dbx"], 2 * i + g + 2)
                    v.wait_ge(s["da"], 2 * i + g + 1)
                    v.wait_ge(s["prod"], 2 * i + g + 1)
                    nc.vector.tensor_tensor_scan(hst[:, k], da[:, k], dbx[:, k], 0.0, ALU.mult, ALU.add
                                                 ).then_inc(s["scan"], 1)

            def gated(b):
                v.wait_ge(s["summed"], n_s * (b + 1) + 2)
                nc.vector.tensor_tensor(chunks(u[:, b]), pa[:, :, 0:CH], chunks(z[:, b]), ALU.mult).then_inc(s["yo"], 1)

            with v.Fori(0, n_s // 2) as i:
                states(0, i)
            v.wait_ge(s["u1"], 1)
            states(1, 0)
            gated(0)
            with v.Fori(1, n_s // 2) as i:
                states(1, i)
            gated(1)

            for c in range(NCH):
                v.wait_ge(s["wlin"], c + 1)
                nc.vector.scalar_tensor_tensor(chunk(r1, c), pa[:, c, 0:CH], chip.w("a3_blin"), chunk(chip.xl, c),
                                               ALU.add, ALU.add).then_inc(s["r1"], 1)

            def affine1(c):
                v.wait_ge(chip.ln_out, NCH * k_ln1 + c + 1)
                nc.vector.tensor_scalar(chunk(n1, c), chunk(n1, c), chip.w("a3_g1"), chip.w("a3_b1"), ALU.mult, ALU.add
                                        ).then_inc(s["n1"], 1)

            norm_vector(chip, k_ln1, n1, affine1)
            for c in range(NCH):
                v.wait_ge(s["down"], 2 * (c + 1))
                nc.vector.scalar_tensor_tensor(chunk(r1, c), pa[:, c, 0:CH], chip.w("a3_bsq"), chunk(n1, c),
                                               ALU.add, ALU.add).then_inc(s["r2"], 1)

            def affine2(c):
                v.wait_ge(chip.ln_out, NCH * k_ln2 + c + 1)
                steps.settle(v, nc.vector.tensor_scalar(chunk(n1, c), chunk(n1, c), chip.w("a3_g2"), chip.w("a3_b2"),
                                                        ALU.mult, ALU.add))
                nc.vector.tensor_tensor(chunk(chip.h, c), chunk(chip.h, c), chunk(n1, c), ALU.add).then_inc(s["h"], 1)

            norm_vector(chip, k_ln2, n1, affine2)


def build(nc, t, out):
    with ExitStack() as ctx:
        chip = Chip(nc, ctx)
        work = [
            lambda: tokenise(chip, t["x"], t["xedge"], t["tokw"], t["cls2"], t["small"]),
            lambda: linear_attention(chip),
            lambda: experts2(chip, "f0", t["f0_slab"], 1, 8, 2, ACT.Relu, "switch"),
            lambda: row_attention(chip),
            lambda: experts2(chip, "f1", t["f1_slab"], 1, 8, 1, ACT.Gelu, "mask"),
            lambda: scan_attention(chip),
            lambda: experts3(chip, t["f2_slab"]),
            lambda: mamba(chip, t["selbc"]),
            lambda: experts2(chip, "f3", t["f3_slab"], 4, 8, 1, ACT.Relu, "logits", out),
        ]
        for n, stage in enumerate(work):
            stage()
            if n + 1 < len(work):
                chip.end_stage()



def pack(i):
    import numpy as np
    f = np.float32
    small = np.zeros((128, NSMALL), f)

    def put(name, a, row0=0):
        at, n = COL[name]
        a = np.asarray(a)
        if a.ndim == 1:
            a = a[:, None]
        assert a.shape[1] == n, (name, a.shape)
        small[row0:row0 + a.shape[0], at:at + n] = a

    def bd(w):
        w = np.asarray(w)
        z = np.zeros((2 * w.shape[0], 2 * w.shape[1]), f)
        z[:w.shape[0], :w.shape[1]] = w
        z[w.shape[0]:, w.shape[1]:] = w
        return z

    def two(v):
        return np.concatenate([np.asarray(v), np.asarray(v)])

    def one_seq(w):
        w = np.asarray(w)
        return bd(w)

    def rep(v):
        return np.tile(two(v)[None, :], (128, 1))

    k, p = np.arange(9)[:, None], np.arange(16)[None, :]
    ang = 2 * np.pi * k * p / 16
    dft = np.concatenate([np.cos(ang), -np.sin(ang)], 0) / 4
    dft = dft.reshape(18, 2, 2, 4).transpose(0, 2, 1, 3).reshape(18, 16)
    put("dft", dft.astype(f))
    put("mean", bd(np.full((64, 64), 1 / 64, f)))
    put("centre", bd(np.eye(64, dtype=f) - f(1 / 64)))
    put("eps", np.tile(np.array([[EPS, EPS * EPS, 1.0]], f), (128, 1)))
    put("ident", np.eye(128, dtype=f))
    wqkv = i["L0_attn_Wqkv"]
    put("a0_wq", bd(wqkv[:, 0:64]))
    put("a0_wk", bd(wqkv[:, 64:128]))
    put("a0_wv", bd(wqkv[:, 128:192]))
    put("a0_wproj", bd(i["L0_attn_Wproj"]))
    put("a0_wg1", bd(i["L0_attn_Wg1"]))
    put("a0_wg2", bd(i["L0_attn_Wg2"]))
    put("a0_mask", np.kron(np.eye(16), np.ones((8, 8))).astype(f))
    put("a0_g", two(i["L0_attn_ln_g"]))
    put("a0_b", two(i["L0_attn_ln_b"]))
    put("a0_bproj", two(i["L0_attn_bproj"]))
    put("a0_bg1", two(i["L0_attn_bg1"]))
    put("a0_bg2", two(i["L0_attn_bg2"]))

    def diag(v):
        return two(np.asarray(v).reshape(-1))

    def parts(b2, n):
        return np.concatenate([bd(b2)] * n, 0)

    put("f0_gate", bd(i["L0_ffn_gate_w"]))
    put("f0_gbias", rep(i["L0_ffn_gate_b"]))
    put("f0_b2", parts(i["L0_ffn_b2"], 1))
    sel = np.zeros((2, 128), f)
    sel[0, :64] = 1
    sel[1, 64:] = 1
    put("seqsel", sel, row0=32)
    put("rev8", rep(8 - np.arange(8, dtype=f)))
    put("rev6", rep(6 - np.arange(6, dtype=f)))
    shift = np.zeros((16, 16), f)
    shift[np.arange(8), 8 + np.arange(8)] = 1
    put("shift", shift)

    def dup(w):
        return np.concatenate([np.asarray(w)] * 2, 0)

    put("a1_g", diag(i["L1_attn_gamma"]))
    put("a1_b", diag(i["L1_attn_beta"]))
    put("a1_wq", dup(i["L1_attn_Wq"]))
    put("a1_wk", dup(i["L1_attn_Wk"]))
    put("a1_wv", dup(i["L1_attn_Wv"]))
    put("a1_wg", one_seq(i["L1_attn_Wg"]))
    put("a1_bg", np.asarray(i["L1_attn_bg"]).reshape(2, 128).T)
    put("a1_wo", np.asarray(i["L1_attn_Wo"]).reshape(2, 128, 64).transpose(1, 0, 2).reshape(128, 128))
    put("a1_bo", diag(i["L1_attn_bo"]))
    ones = np.ones((64, 64), f)
    put("tdiff", np.block([[ones, -ones], [-ones, ones]]))
    put("f1_gate", bd(i["L1_ffn_Wg"]))
    put("f1_gbias", rep(i["L1_ffn_bg"]))

    inw = np.asarray(i["L2_attn_in_w"])
    put("a2_wxp", bd(inw[:64].T))
    put("a2_wres", bd(inw[64:].T))
    put("a2_bxp", diag(i["L2_attn_in_b"][:64]))
    put("a2_bres", diag(i["L2_attn_in_b"][64:]))
    put("a2_convw", dup(np.asarray(i["L2_attn_conv_w"]).reshape(64, 4)))
    put("a2_convb", diag(i["L2_attn_conv_b"]))
    put("a2_dt", bd(i["L2_attn_dt"]))
    put("a2_bw", bd(np.asarray(i["L2_attn_B_w"]).T))
    put("a2_cw", bd(np.asarray(i["L2_attn_C_w"]).T))
    put("a2_ow", bd(np.asarray(i["L2_attn_out_w"]).T))
    put("a2_ob", diag(i["L2_attn_out_b"]))
    put("a2_g", diag(i["L2_attn_gamma"]))
    put("a2_b", diag(i["L2_attn_beta"]))
    put("chmean", (np.tile(np.eye(64), (2, 2)) / (NB * NTOK)).astype(f))
    put("f2_rw1", bd(i["L2_ffn_router_w1"]))
    put("f2_rb1", diag(i["L2_ffn_router_b1"]))
    put("f2_gate", bd(i["L2_ffn_router_w2"]))
    put("f2_gbias", rep(i["L2_ffn_router_b2"]))
    put("f2_b2", parts(i["L2_ffn_expert_b3"], 3))

    win = np.asarray(i["L3_attn_W_in"])
    put("a3_win", np.concatenate([one_seq(win[:128].T), one_seq(win[128:].T)], 1))
    put("a3_convw", i["L3_attn_conv_w"])
    put("a3_convb", i["L3_attn_conv_b"])
    wx = np.asarray(i["L3_attn_W_x"])
    put("a3_wx", np.concatenate([wx[16:48], wx[:16]], 0).T)
    put("a3_wdt", np.asarray(i["L3_attn_W_dt"]).T, row0=32)
    put("a3_bdt", i["L3_attn_b_dt"])
    put("a3_alog", i["L3_attn_A_log"])
    put("a3_dp", i["L3_attn_Dp"])
    put("a3_wout", np.asarray(i["L3_attn_W_out"]).T)
    put("a3_wlin", bd(np.asarray(i["L3_attn_W_lin"]).T))
    put("a3_blin", diag(i["L3_attn_b_lin"]))
    put("a3_g1", diag(i["L3_attn_ln1_g"]))
    put("a3_b1", diag(i["L3_attn_ln1_b"]))
    put("a3_wexp", one_seq(np.asarray(i["L3_attn_W_exp"]).T))
    put("a3_bexp", i["L3_attn_b_exp"])
    put("a3_wsq", np.asarray(i["L3_attn_W_sq"]).T)
    put("a3_bsq", diag(i["L3_attn_b_sq"]))
    put("a3_g2", diag(i["L3_attn_ln2_g"]))
    put("a3_b2", diag(i["L3_attn_ln2_b"]))
    put("f3_gate", bd(i["L3_ffn_Wg"]))
    put("f3_gbias", rep(i["L3_ffn_bg"]))
    put("f3_gbias2", rep(i["L3_ffn_bias"]))

    def bf16_bits(ones_at):
        u = np.zeros(ones_at.shape, np.uint16)
        u[ones_at] = 0x3F80
        return u.view(f)

    def slabs2(w1, b1, w2, b2, parts):
        w1, b1, w2 = np.asarray(w1), np.asarray(b1), np.asarray(w2)
        e_n, _, hid = w1.shape
        hc = hid // 128
        out = np.zeros((e_n, 128, SLAB2[hc]), f)
        for e in range(e_n):
            out[e, :, 0:hid] = dup(w1[e])
            out[e, :, hid:hid + 64 * hc] = w2[e].reshape(hc, 128, 64).transpose(1, 0, 2).reshape(128, -1)
            out[e, :, hid + 64 * hc:hid + 65 * hc] = b1[e].reshape(hc, 128).T
            out[e, :, hid + 65 * hc] = diag(b2[e])
            at = np.zeros((128, 128), bool)
            for part in range(parts):
                for b in range(2):
                    at[part * 2 * e_n + b * e_n + e, 64 * b:64 * b + 64] = True
            out[e, :, hid + 65 * hc + 1:] = bf16_bits(at)
        return out.transpose(1, 0, 2).reshape(128, -1)

    def slabs3(w1, b1, w2, b2, w3):
        e_n = w1.shape[0]
        out = np.zeros((e_n, 128, SLAB3), f)
        for e in range(e_n):
            for n, w in enumerate((w1, w2, w3)):
                out[e, :, 128 * n:128 * n + 128] = bd(w[e])
            out[e, :, 384] = diag(b1[e])
            out[e, :, 385] = diag(b2[e])
            at = np.zeros((128, 128), bool)
            for part in range(3):
                for b in range(2):
                    at[part * 2 * e_n + b * e_n + e, 64 * b:64 * b + 64] = True
            out[e, :, 386:450] = bf16_bits(at)
        return out.transpose(1, 0, 2).reshape(128, -1)

    def sel_bc():
        at = np.zeros((128, 16, 2, 128), bool)
        for s in range(16):
            for part in range(3):
                at[32 * part + s, s, 0] = True
                at[32 * part + 16 + s, s, 1] = True
        return bf16_bits(at.reshape(128, -1))

    x = np.asarray(i["x"]).reshape(2, 64, 16, 2, 4, 64).transpose(3, 1, 0, 2, 4, 5)
    edge = x[1, :, :, 15, 3, :]
    return {
        "x": x.reshape(128, 2, 16, 4, 64),
        "xedge": np.concatenate([edge, edge], 0),
        "tokw": np.asarray(i["L0_tok_W"]).reshape(64, 18, 64).transpose(1, 0, 2),
        "cls2": two(np.asarray(i["cls_tok"]).reshape(64))[:, None],
        "small": small,
        "f0_slab": slabs2(i["L0_ffn_w1"], i["L0_ffn_b1"], i["L0_ffn_w2"], i["L0_ffn_b2"], 1),
        "f1_slab": slabs2(i["L1_ffn_W1"], i["L1_ffn_b1"], i["L1_ffn_W2"], i["L1_ffn_b2"], 1),
        "f2_slab": slabs3(i["L2_ffn_expert_w1"], i["L2_ffn_expert_b1"], i["L2_ffn_expert_w2"],
                          i["L2_ffn_expert_b2"], i["L2_ffn_expert_w3"]),
        "f3_slab": slabs2(i["L3_ffn_W1"], i["L3_ffn_b1"], i["L3_ffn_W2"], i["L3_ffn_b2"], 3),
        "selbc": sel_bc(),
    }


def kernel(**inputs):
    import numpy as np
    import concourse.bacc as bacc
    from concourse.bass_utils import run_bass_kernel_spmd

    nc = bacc.Bacc("TRN2", target_bir_lowering=False, num_devices=1)
    arrays, t = {}, {}
    for name, a in pack(inputs).items():
        a = np.ascontiguousarray(a)
        arrays[name + "_dram"] = a
        t[name] = nc.dram_tensor(name + "_dram", a.shape, mybir.dt.from_np(a.dtype), kind="ExternalInput").ap()
    out = nc.dram_tensor("out_dram", (P, NTOK), F32, kind="ExternalOutput").ap()
    build(nc, t, out)
    got = run_bass_kernel_spmd(nc, [arrays], core_ids=[0]).results[0]["out_dram"]
    return np.ascontiguousarray(got.reshape(NB, D, NTOK).transpose(0, 2, 1))
```
